# Optimizing a Trainium2 kernel written in Bass

```python
import numpy as np
import jax
import jax.numpy as jnp

def _softmax(x, axis=-1):
    return jax.nn.softmax(x, axis=axis)

def _gelu(x):
    return jax.nn.gelu(x, approximate=True)

def _silu(x):
    return jax.nn.silu(x)

def _sigmoid(x):
    return jax.nn.sigmoid(x)

def _layernorm(x, axis=-1, eps=1e-05):
    m = jnp.mean(x, axis=axis, keepdims=True)
    v = jnp.var(x, axis=axis, keepdims=True)
    return (x - m) / jnp.sqrt(v + eps)

def _scatter_add(tgt, idx, src, axis=0):
    return tgt.at[idx].add(src)

def _segment_sum(src, seg, n):
    return jax.ops.segment_sum(src, seg, n)
kernel_name = 'mk_xattn_ffn_d4_seqx_r4_22c72f'

def setup_inputs(seed: int=0):
    np.random.seed(seed)
    _w = jnp.asarray

    def _rec_inputs():
        import jax
        import jax.numpy as jnp
        _rk = jax.random.key(seed)
        x = -0.0003929 + 0.9999 * jax.random.normal(jax.random.fold_in(_rk, 1), (8, 256, 256), jnp.float32)
        _lenS = 256 - jax.random.randint(jax.random.fold_in(_rk, 7), (8,), 0, max(1, 256 // 4) + 1, jnp.int32)
        _lenS2 = 256 - jax.random.randint(jax.random.fold_in(_rk, 8), (8,), 0, max(1, 256 // 4) + 1, jnp.int32)
        _ctx_768P = jax.random.normal(jax.random.fold_in(_rk, 11), (8, 16, 192), jnp.float32)
        _ctx_768c = jax.random.dirichlet(jax.random.fold_in(_rk, 511), 0.3 * jnp.ones((16,), jnp.float32), (8, 256))
        _ctx_768t = jnp.einsum('bsk,bkd->bsd', _ctx_768c, _ctx_768P)
        _ctx_768t = _ctx_768t * jax.lax.rsqrt(jnp.mean(jnp.square(_ctx_768t)) + 1e-12) * 0.953939
        ctx_768 = 0.00095986 + 0.999812 * (_ctx_768t + 0.3 * jax.random.normal(jax.random.fold_in(_rk, 611), (8, 256, 192), jnp.float32))
        _validS = jnp.arange(256)[None, :] < _lenS[:, None]
        _validS2 = jnp.arange(256)[None, :] < _lenS2[:, None]
        _causal = jnp.tril(jnp.ones((256, 256), dtype=bool))
        mask_BxS2_bf1 = jnp.ones((8, 256), dtype=bool)
        return (x, ctx_768, mask_BxS2_bf1)
    x, ctx_768, mask_BxS2_bf1 = _rec_inputs()

    def _L0_xattn_setup():
        import jax, jax.numpy as jnp
        import numpy as np
        DIM = 256
        CTX_DIM = 192
        HEADS = 16
        key = jax.random.key(seed)
        ks = jax.random.split(key, 7)
        B, N, M = (4, 1024, 64)
        x = jax.random.normal(ks[0], (B, N, DIM), dtype=jnp.float32)
        context = jax.random.normal(ks[1], (B, M, CTX_DIM), dtype=jnp.float32)
        context_mask = jnp.ones((B, M), dtype=bool)
        s_d = 1.0 / np.sqrt(DIM)
        s_c = 1.0 / np.sqrt(CTX_DIM)
        Wq = jax.random.normal(ks[2], (DIM, DIM), dtype=jnp.float32) * s_d
        Wk = jax.random.normal(ks[3], (CTX_DIM, DIM), dtype=jnp.float32) * s_c
        Wv = jax.random.normal(ks[4], (CTX_DIM, DIM), dtype=jnp.float32) * s_c
        Wo = jax.random.normal(ks[5], (DIM, DIM), dtype=jnp.float32) * s_d
        return {'x': x, 'context': context, 'context_mask': context_mask, 'Wq': Wq, 'Wk': Wk, 'Wv': Wv, 'Wo': Wo}
    _L0_xattn_all = _L0_xattn_setup()
    _L0_xattn_in = {k: v for k, v in _L0_xattn_all.items() if k in ('Wq', 'Wk', 'Wv', 'Wo')}
    del _L0_xattn_all

    def _L0_ffn_setup():
        import jax, jax.numpy as jnp
        import numpy as np
        N_EXPERTS = 8
        CAP_FACTOR = 1.25
        BATCH, SEQ, DMODEL, DFF = (4, 512, 256, 1024)
        key = jax.random.key(seed)
        k0, k1, k2, k3 = jax.random.split(key, 4)
        x = jax.random.normal(k0, (BATCH, SEQ, DMODEL), dtype=jnp.float32)
        Wr = jax.random.normal(k1, (DMODEL, N_EXPERTS), dtype=jnp.float32) * 0.02
        W1 = jax.random.normal(k2, (N_EXPERTS, DMODEL, DFF), dtype=jnp.float32) * 0.02
        W2 = jax.random.normal(k3, (N_EXPERTS, DFF, DMODEL), dtype=jnp.float32) * 0.02
        return {'x': x, 'Wr': Wr, 'W1': W1, 'W2': W2}
    _L0_ffn_all = _L0_ffn_setup()
    _L0_ffn_in = {k: v for k, v in _L0_ffn_all.items() if k in ('Wr', 'W1', 'W2')}
    del _L0_ffn_all

    def _L1_xattn_setup():
        import jax, jax.numpy as jnp
        import numpy as np
        EPS = 1e-08
        key = jax.random.key(seed)
        kv, kt, k1, k2, k3, k4 = jax.random.split(key, 6)
        B, S = (16, 256)
        VD, TD, H = (256, 192, 128)
        visual_features = jax.random.normal(kv, (B, S, VD), dtype=jnp.float32)
        text_features = jax.random.normal(kt, (B, S, TD), dtype=jnp.float32)
        Wv = jax.random.normal(k1, (H, VD), dtype=jnp.float32) * (1.0 / np.sqrt(VD))
        bv = jax.random.normal(k2, (H,), dtype=jnp.float32) * 0.01
        Wt = jax.random.normal(k3, (H, TD), dtype=jnp.float32) * (1.0 / np.sqrt(TD))
        bt = jax.random.normal(k4, (H,), dtype=jnp.float32) * 0.01
        return {'visual_features': visual_features, 'text_features': text_features, 'Wv': Wv, 'bv': bv, 'Wt': Wt, 'bt': bt}
    _L1_xattn_all = _L1_xattn_setup()
    _L1_xattn_in = {k: v for k, v in _L1_xattn_all.items() if k in ('Wv', 'bv', 'Wt', 'bt')}
    del _L1_xattn_all

    def _L1_ffn_setup():
        import jax, jax.numpy as jnp
        import numpy as np
        DIM = 256
        DEPTH = 2
        HEADS = 8
        DIM_HEAD = 64
        WINDOW = 128
        INNER = HEADS * DIM_HEAD
        HID = int(DIM * 4 * 2 / 3)
        B, N = (2, 2048)
        QK_SCALE = 8.0

        def shift_token(t):
            t1, t2 = jnp.split(t, 2, axis=-1)
            t2 = jnp.pad(t2, ((0, 0), (1, 0), (0, 0)))[:, :-1]
            return jnp.concatenate([t1, t2], axis=-1)

        def l2norm(t):
            return t / jnp.clip(jnp.linalg.norm(t, axis=-1, keepdims=True), 1e-12)

        def rotate_half(x):
            x1, x2 = jnp.split(x, 2, axis=-1)
            return jnp.concatenate([-x2, x1], axis=-1)

        def rotary_xpos(q, k):
            n = q.shape[-2]
            half_idx = jnp.arange(0, DIM_HEAD, 2, dtype=jnp.float32)
            inv_freq = 1.0 / 10000.0 ** (half_idx / DIM_HEAD)
            t = jnp.arange(n, dtype=jnp.float32)
            freqs = t[:, None] * inv_freq[None, :]
            freqs = jnp.concatenate([freqs, freqs], axis=-1)
            base = (half_idx + 0.4 * DIM_HEAD) / (1.4 * DIM_HEAD)
            power = (t - n // 2) / float(WINDOW // 2)
            scale = base[None, :] ** power[:, None]
            scale = jnp.concatenate([scale, scale], axis=-1)
            cos, sin = (jnp.cos(freqs), jnp.sin(freqs))
            q = q * cos * scale + rotate_half(q) * sin * scale
            k = k * cos / scale + rotate_half(k) * sin / scale
            return (q, k)

        def local_attention(q, k, v):
            b, h, n, d = q.shape
            w = n // WINDOW
            bq = q.reshape(b, h, w, WINDOW, d) * QK_SCALE
            bk = k.reshape(b, h, w, WINDOW, d)
            bv = v.reshape(b, h, w, WINDOW, d)

            def look_around(t):
                p = jnp.pad(t, ((0, 0), (0, 0), (1, 0), (0, 0), (0, 0)))
                return jnp.concatenate([p[:, :, :w], p[:, :, 1:]], axis=3)
            bk, bv = (look_around(bk), look_around(bv))
            bt = jnp.arange(n).reshape(w, WINDOW)
            btp = jnp.pad(bt, ((1, 0), (0, 0)), constant_values=-1)
            btk = jnp.concatenate([btp[:w], btp[1:]], axis=1)
            sim = jnp.einsum('bhwid,bhwjd->bhwij', bq, bk)
            i = bt[:, :, None]
            j = btk[:, None, :]
            mask = (i < j) | (i > j + WINDOW) | (j == -1)
            sim = jnp.where(mask, -jnp.finfo(sim.dtype).max, sim)
            attn = jax.nn.softmax(sim, axis=-1)
            out = jnp.einsum('bhwij,bhwjd->bhwid', attn, bv)
            return out.reshape(b, h, n, d)

        def _layer(x, wqkv, qs, ksc, wo, lg, lb, w1, b1, w2, b2):
            b, n, _ = x.shape
            h = shift_token(x)
            qkv = h @ wqkv
            q, k, v = jnp.split(qkv, 3, axis=-1)
            to_heads = lambda t: t.reshape(b, n, HEADS, DIM_HEAD).transpose(0, 2, 1, 3)
            q, k, v = (to_heads(q), to_heads(k), to_heads(v))
            q = l2norm(q) * qs
            k = l2norm(k) * ksc
            q, k = rotary_xpos(q, k)
            o = local_attention(q, k, v)
            o = o.transpose(0, 2, 1, 3).reshape(b, n, INNER)
            x = x + o @ wo
            h = shift_token(x)
            mu = h.mean(-1, keepdims=True)
            var = h.var(-1, keepdims=True)
            h = (h - mu) / jnp.sqrt(var + 1e-05) * lg + lb
            h = h @ w1 + b1
            a, g = jnp.split(h, 2, axis=-1)
            h = a * jax.nn.gelu(g, approximate=False)
            x = x + h @ w2 + b2
            return x
        key = jax.random.key(seed)
        ks = jax.random.split(key, 6)
        return {'x': jax.random.normal(ks[0], (B, N, DIM), jnp.float32), 'wqkv': jax.random.normal(ks[1], (DEPTH, DIM, 3 * INNER), jnp.float32) * 0.02, 'q_scale': jnp.ones((DEPTH, DIM_HEAD), jnp.float32), 'k_scale': jnp.ones((DEPTH, DIM_HEAD), jnp.float32), 'wo': jax.random.normal(ks[2], (DEPTH, INNER, DIM), jnp.float32) * 0.02, 'ln_g': jnp.ones((DEPTH, DIM), jnp.float32), 'ln_b': jnp.zeros((DEPTH, DIM), jnp.float32), 'w1': jax.random.normal(ks[3], (DEPTH, DIM, 2 * HID), jnp.float32) * 0.02, 'b1': jnp.zeros((DEPTH, 2 * HID), jnp.float32), 'w2': jax.random.normal(ks[4], (DEPTH, HID, DIM), jnp.float32) * 0.02, 'b2': jnp.zeros((DEPTH, DIM), jnp.float32)}
    _L1_ffn_all = _L1_ffn_setup()
    _L1_ffn_in = {k: v for k, v in _L1_ffn_all.items() if k in ('wqkv', 'q_scale', 'k_scale', 'wo', 'ln_g', 'ln_b', 'w1', 'b1', 'w2', 'b2')}
    del _L1_ffn_all

    def _L2_xattn_setup():
        import jax, jax.numpy as jnp
        import numpy as np
        B, LQ, LKV = (4, 128, 512)
        DQ, DKV, H = (256, 192, 16)
        HD = DQ // H
        key = jax.random.key(seed)
        ks = jax.random.split(key, 12)
        s_q = 1.0 / np.sqrt(DQ)
        s_kv = 1.0 / np.sqrt(DKV)
        return {'q': jax.random.normal(ks[0], (B, LQ, DQ), jnp.float32), 'kv': jax.random.normal(ks[1], (B, LKV, DKV), jnp.float32), 'Wq': jax.random.normal(ks[2], (DQ, DQ), jnp.float32) * s_q, 'bq': jnp.zeros((DQ,), jnp.float32), 'Wk': jax.random.normal(ks[3], (DKV, DQ), jnp.float32) * s_kv, 'bk': jnp.zeros((DQ,), jnp.float32), 'Wv': jax.random.normal(ks[4], (DKV, DQ), jnp.float32) * s_kv, 'bv': jnp.zeros((DQ,), jnp.float32), 'Wo': jax.random.normal(ks[5], (DQ, DQ), jnp.float32) * s_q, 'bo': jnp.zeros((DQ,), jnp.float32), 'scale': jnp.ones((1,), jnp.float32) * DQ ** (-0.5)}
    _L2_xattn_all = _L2_xattn_setup()
    _L2_xattn_in = {k: v for k, v in _L2_xattn_all.items() if k in ('Wq', 'bq', 'Wk', 'bk', 'Wv', 'bv', 'Wo', 'bo', 'scale')}
    del _L2_xattn_all

    def _L2_ffn_setup():
        import jax, jax.numpy as jnp
        import numpy as np
        B, S, H = (2, 512, 256)
        F = 1024
        E = 8
        TOP_K = 2
        SHARED_SCALE = 0.1
        EPS = 1e-09

        def _moe_forward(x3, Wg, W1, b1, W2, b2, Ws1, bs1, Ws2, bs2):
            b, s, h = x3.shape
            x = x3.reshape(-1, h)
            T = x.shape[0]
            logits = x @ Wg
            probs = jax.nn.softmax(logits, axis=-1)
            vals, idx = jax.lax.top_k(probs, TOP_K)
            weights = vals / (jnp.sum(vals, axis=-1, keepdims=True) + EPS)
            cw = jnp.zeros((T, E), dtype=x.dtype).at[jnp.arange(T)[:, None], idx].set(weights)
            hpre = jnp.einsum('th,ehf->tef', x, W1) + b1
            act = jax.nn.silu(hpre)
            y = jnp.einsum('tef,efh->teh', act, W2) + b2
            out = jnp.einsum('te,teh->th', cw, y)
            shared = jax.nn.silu(x @ Ws1 + bs1) @ Ws2 + bs2
            out = out + SHARED_SCALE * shared
            return out.reshape(b, s, h)
        key = jax.random.key(seed)
        ks = jax.random.split(key, 10)
        sc = 0.02
        return {'hidden_states': jax.random.normal(ks[0], (B, S, H), dtype=jnp.float32), 'Wg': jax.random.normal(ks[1], (H, E), dtype=jnp.float32) * sc, 'W1': jax.random.normal(ks[2], (E, H, F), dtype=jnp.float32) * sc, 'b1': jnp.zeros((E, F), dtype=jnp.float32), 'W2': jax.random.normal(ks[3], (E, F, H), dtype=jnp.float32) * sc, 'b2': jnp.zeros((E, H), dtype=jnp.float32), 'Ws1': jax.random.normal(ks[4], (H, F), dtype=jnp.float32) * sc, 'bs1': jnp.zeros((F,), dtype=jnp.float32), 'Ws2': jax.random.normal(ks[5], (F, H), dtype=jnp.float32) * sc, 'bs2': jnp.zeros((H,), dtype=jnp.float32)}
    _L2_ffn_all = _L2_ffn_setup()
    _L2_ffn_in = {k: v for k, v in _L2_ffn_all.items() if k in ('Wg', 'W1', 'b1', 'W2', 'b2', 'Ws1', 'bs1', 'Ws2', 'bs2')}
    del _L2_ffn_all

    def _L3_xattn_setup():
        import jax, jax.numpy as jnp
        import numpy as np
        EMBED_DIM = 256
        HIDDEN_DIM = 256
        NUM_HEADS = 16
        CONTEXT_DIM = 192
        HEAD_DIM = EMBED_DIM // NUM_HEADS
        SCALE = HEAD_DIM ** (-0.5)

        def _split_heads(x):
            b, n, _ = x.shape
            return x.reshape(b, n, NUM_HEADS, -1).transpose(0, 2, 1, 3)
        key = jax.random.key(seed)
        ks = jax.random.split(key, 7)
        B, N, M = (4, 1024, 256)
        tokens = jax.random.normal(ks[0], (B, N, HIDDEN_DIM), dtype=jnp.float32)
        context = jax.random.normal(ks[1], (B, M, CONTEXT_DIM), dtype=jnp.float32)
        Wq = jax.random.normal(ks[2], (HIDDEN_DIM, EMBED_DIM), dtype=jnp.float32) * HIDDEN_DIM ** (-0.5)
        Wk = jax.random.normal(ks[3], (CONTEXT_DIM, EMBED_DIM), dtype=jnp.float32) * CONTEXT_DIM ** (-0.5)
        Wv = jax.random.normal(ks[4], (CONTEXT_DIM, HIDDEN_DIM), dtype=jnp.float32) * CONTEXT_DIM ** (-0.5)
        Wo = jax.random.normal(ks[5], (HIDDEN_DIM, HIDDEN_DIM), dtype=jnp.float32) * HIDDEN_DIM ** (-0.5)
        bo = jax.random.normal(ks[6], (HIDDEN_DIM,), dtype=jnp.float32) * 0.01
        return {'tokens': tokens, 'context': context, 'Wq': Wq, 'Wk': Wk, 'Wv': Wv, 'Wo': Wo, 'bo': bo}
    _L3_xattn_all = _L3_xattn_setup()
    _L3_xattn_in = {k: v for k, v in _L3_xattn_all.items() if k in ('Wq', 'Wk', 'Wv', 'Wo', 'bo')}
    del _L3_xattn_all

    def _L3_ffn_setup():
        import jax, jax.numpy as jnp
        import numpy as np
        from jax import lax
        TOP_K = 4
        N_GROUP = 4
        TOPK_GROUP = 2
        ROUTED_SCALE = 2.5
        NEG_INF = -1000000000.0

        def _route(xf, router_weight, router_bias):
            T = xf.shape[0]
            E = router_weight.shape[0]
            logits = xf @ router_weight.T
            scores = jax.nn.sigmoid(logits)
            s_choice = scores + router_bias
            per_group = E // N_GROUP
            sg = s_choice.reshape(T, N_GROUP, per_group)
            group_scores = lax.top_k(sg, 2)[0].sum(-1)
            _, gidx = lax.top_k(group_scores, TOPK_GROUP)
            gmask = jnp.zeros((T, N_GROUP), dtype=bool).at[jnp.arange(T)[:, None], gidx].set(True)
            masked = jnp.where(gmask[:, :, None], sg, NEG_INF).reshape(T, E)
            _, topk_idx = lax.top_k(masked, TOP_K)
            w = jnp.take_along_axis(scores, topk_idx, axis=1)
            w = w / (w.sum(-1, keepdims=True) + 1e-20) * ROUTED_SCALE
            combine = jnp.zeros((T, E), dtype=xf.dtype).at[jnp.arange(T)[:, None], topk_idx].add(w)
            return combine
        key = jax.random.key(seed)
        ks = jax.random.split(key, 6)
        B, S, H, I, E = (2, 512, 256, 128, 16)
        x = jax.random.normal(ks[0], (B, S, H), dtype=jnp.float32)
        router_weight = jax.random.normal(ks[1], (E, H), dtype=jnp.float32) * 0.02
        router_bias = jnp.zeros((E,), dtype=jnp.float32)
        w_gate = jax.random.normal(ks[2], (E, I, H), dtype=jnp.float32) * 0.02
        w_up = jax.random.normal(ks[3], (E, I, H), dtype=jnp.float32) * 0.02
        w_down = jax.random.normal(ks[4], (E, H, I), dtype=jnp.float32) * 0.02
        return {'x': x, 'router_weight': router_weight, 'router_bias': router_bias, 'w_gate': w_gate, 'w_up': w_up, 'w_down': w_down}
    _L3_ffn_all = _L3_ffn_setup()
    _L3_ffn_in = {k: v for k, v in _L3_ffn_all.items() if k in ('router_weight', 'router_bias', 'w_gate', 'w_up', 'w_down')}
    del _L3_ffn_all
    return {'x': x, 'ctx_768': ctx_768, 'mask_BxS2_bf1': mask_BxS2_bf1, 'L0_xattn_Wq': _L0_xattn_in['Wq'], 'L0_xattn_Wk': _L0_xattn_in['Wk'], 'L0_xattn_Wv': _L0_xattn_in['Wv'], 'L0_xattn_Wo': _L0_xattn_in['Wo'], 'L0_ffn_Wr': _L0_ffn_in['Wr'], 'L0_ffn_W1': _L0_ffn_in['W1'], 'L0_ffn_W2': _L0_ffn_in['W2'], 'L1_xattn_Wv': _L1_xattn_in['Wv'], 'L1_xattn_bv': _L1_xattn_in['bv'], 'L1_xattn_Wt': _L1_xattn_in['Wt'], 'L1_xattn_bt': _L1_xattn_in['bt'], 'L1_ffn_wqkv': _L1_ffn_in['wqkv'], 'L1_ffn_q_scale': _L1_ffn_in['q_scale'], 'L1_ffn_k_scale': _L1_ffn_in['k_scale'], 'L1_ffn_wo': _L1_ffn_in['wo'], 'L1_ffn_ln_g': _L1_ffn_in['ln_g'], 'L1_ffn_ln_b': _L1_ffn_in['ln_b'], 'L1_ffn_w1': _L1_ffn_in['w1'], 'L1_ffn_b1': _L1_ffn_in['b1'], 'L1_ffn_w2': _L1_ffn_in['w2'], 'L1_ffn_b2': _L1_ffn_in['b2'], 'L2_xattn_Wq': _L2_xattn_in['Wq'], 'L2_xattn_bq': _L2_xattn_in['bq'], 'L2_xattn_Wk': _L2_xattn_in['Wk'], 'L2_xattn_bk': _L2_xattn_in['bk'], 'L2_xattn_Wv': _L2_xattn_in['Wv'], 'L2_xattn_bv': _L2_xattn_in['bv'], 'L2_xattn_Wo': _L2_xattn_in['Wo'], 'L2_xattn_bo': _L2_xattn_in['bo'], 'L2_xattn_scale': _L2_xattn_in['scale'], 'L2_ffn_Wg': _L2_ffn_in['Wg'], 'L2_ffn_W1': _L2_ffn_in['W1'], 'L2_ffn_b1': _L2_ffn_in['b1'], 'L2_ffn_W2': _L2_ffn_in['W2'], 'L2_ffn_b2': _L2_ffn_in['b2'], 'L2_ffn_Ws1': _L2_ffn_in['Ws1'], 'L2_ffn_bs1': _L2_ffn_in['bs1'], 'L2_ffn_Ws2': _L2_ffn_in['Ws2'], 'L2_ffn_bs2': _L2_ffn_in['bs2'], 'L3_xattn_Wq': _L3_xattn_in['Wq'], 'L3_xattn_Wk': _L3_xattn_in['Wk'], 'L3_xattn_Wv': _L3_xattn_in['Wv'], 'L3_xattn_Wo': _L3_xattn_in['Wo'], 'L3_xattn_bo': _L3_xattn_in['bo'], 'L3_ffn_router_weight': _L3_ffn_in['router_weight'], 'L3_ffn_router_bias': _L3_ffn_in['router_bias'], 'L3_ffn_w_gate': _L3_ffn_in['w_gate'], 'L3_ffn_w_up': _L3_ffn_in['w_up'], 'L3_ffn_w_down': _L3_ffn_in['w_down']}

def reference(x, ctx_768, mask_BxS2_bf1, L0_xattn_Wq, L0_xattn_Wk, L0_xattn_Wv, L0_xattn_Wo, L0_ffn_Wr, L0_ffn_W1, L0_ffn_W2, L1_xattn_Wv, L1_xattn_bv, L1_xattn_Wt, L1_xattn_bt, L1_ffn_wqkv, L1_ffn_q_scale, L1_ffn_k_scale, L1_ffn_wo, L1_ffn_ln_g, L1_ffn_ln_b, L1_ffn_w1, L1_ffn_b1, L1_ffn_w2, L1_ffn_b2, L2_xattn_Wq, L2_xattn_bq, L2_xattn_Wk, L2_xattn_bk, L2_xattn_Wv, L2_xattn_bv, L2_xattn_Wo, L2_xattn_bo, L2_xattn_scale, L2_ffn_Wg, L2_ffn_W1, L2_ffn_b1, L2_ffn_W2, L2_ffn_b2, L2_ffn_Ws1, L2_ffn_bs1, L2_ffn_Ws2, L2_ffn_bs2, L3_xattn_Wq, L3_xattn_Wk, L3_xattn_Wv, L3_xattn_Wo, L3_xattn_bo, L3_ffn_router_weight, L3_ffn_router_bias, L3_ffn_w_gate, L3_ffn_w_up, L3_ffn_w_down):
    import jax
    import jax.numpy as jnp

    def _L0_xattn_ref(x, context, context_mask, Wq, Wk, Wv, Wo):
        import jax, jax.numpy as jnp
        import numpy as np
        DIM = 256
        CTX_DIM = 192
        HEADS = 16
        B, N, _ = x.shape
        M = context.shape[1]
        hd = DIM // HEADS
        scale = hd ** (-0.5)
        q = (x @ Wq).reshape(B, N, HEADS, hd).transpose(0, 2, 1, 3)
        k = (context @ Wk).reshape(B, M, HEADS, hd).transpose(0, 2, 1, 3)
        v = (context @ Wv).reshape(B, M, HEADS, hd).transpose(0, 2, 1, 3)
        scores = jnp.einsum('bhid,bhjd->bhij', q, k) * scale
        max_neg = -jnp.finfo(scores.dtype).max
        scores = jnp.where(context_mask[:, None, None, :], scores, max_neg)
        attn = jax.nn.softmax(scores, axis=-1)
        out = jnp.einsum('bhij,bhjd->bhid', attn, v)
        out = out.transpose(0, 2, 1, 3).reshape(B, N, DIM)
        return out @ Wo

    def _L0_ffn_ref(x, Wr, W1, W2):
        import jax, jax.numpy as jnp
        import numpy as np
        N_EXPERTS = 8
        CAP_FACTOR = 1.25
        BATCH, SEQ, DMODEL, DFF = (4, 512, 256, 1024)
        B, S, D = x.shape
        E = W1.shape[0]
        cap = int(CAP_FACTOR * B * S / E)
        t = x.reshape(-1, D)
        probs = jax.nn.softmax(t @ Wr, axis=-1)
        idx = jnp.argmax(probs, axis=-1)
        pmax = jnp.max(probs, axis=-1)
        onehot = jax.nn.one_hot(idx, E, dtype=jnp.int32)
        pos = jnp.sum(jnp.cumsum(onehot, axis=0) * onehot, axis=-1) - 1
        kept = pos < cap
        flat = idx * cap + jnp.minimum(pos, cap - 1)
        disp = jnp.zeros((E * cap, D), t.dtype).at[flat].add(t * kept[:, None].astype(t.dtype))
        ein = disp.reshape(E, cap, D)
        h = jax.nn.relu(jnp.einsum('ecd,edf->ecf', ein, W1))
        eout = jnp.einsum('ecf,efd->ecd', h, W2).reshape(E * cap, D)
        comb = jnp.where(kept[:, None], eout[flat], t)
        factor = jnp.where(kept, pmax, jnp.ones_like(pmax))
        out = (comb * factor[:, None]).reshape(B, S, D)
        return out

    def _L1_xattn_ref(visual_features, text_features, Wv, bv, Wt, bt):
        import jax, jax.numpy as jnp
        import numpy as np
        EPS = 1e-08
        v = jnp.einsum('bsd,hd->bsh', visual_features, Wv) + bv
        t = jnp.einsum('bsd,hd->bsh', text_features, Wt) + bt
        dots = jnp.einsum('bih,bjh->bij', v, t)
        vn = jnp.linalg.norm(v, axis=-1)
        tn = jnp.linalg.norm(t, axis=-1)
        denom = jnp.maximum(vn[:, :, None] * tn[:, None, :], EPS)
        return dots / denom

    def _L1_ffn_ref(x, wqkv, q_scale, k_scale, wo, ln_g, ln_b, w1, b1, w2, b2):
        import jax, jax.numpy as jnp
        import numpy as np
        DIM = 256
        DEPTH = 2
        HEADS = 8
        DIM_HEAD = 64
        WINDOW = 128
        INNER = HEADS * DIM_HEAD
        HID = int(DIM * 4 * 2 / 3)
        B, N = (2, 2048)
        QK_SCALE = 8.0

        def shift_token(t):
            t1, t2 = jnp.split(t, 2, axis=-1)
            t2 = jnp.pad(t2, ((0, 0), (1, 0), (0, 0)))[:, :-1]
            return jnp.concatenate([t1, t2], axis=-1)

        def l2norm(t):
            return t / jnp.clip(jnp.linalg.norm(t, axis=-1, keepdims=True), 1e-12)

        def rotate_half(x):
            x1, x2 = jnp.split(x, 2, axis=-1)
            return jnp.concatenate([-x2, x1], axis=-1)

        def rotary_xpos(q, k):
            n = q.shape[-2]
            half_idx = jnp.arange(0, DIM_HEAD, 2, dtype=jnp.float32)
            inv_freq = 1.0 / 10000.0 ** (half_idx / DIM_HEAD)
            t = jnp.arange(n, dtype=jnp.float32)
            freqs = t[:, None] * inv_freq[None, :]
            freqs = jnp.concatenate([freqs, freqs], axis=-1)
            base = (half_idx + 0.4 * DIM_HEAD) / (1.4 * DIM_HEAD)
            power = (t - n // 2) / float(WINDOW // 2)
            scale = base[None, :] ** power[:, None]
            scale = jnp.concatenate([scale, scale], axis=-1)
            cos, sin = (jnp.cos(freqs), jnp.sin(freqs))
            q = q * cos * scale + rotate_half(q) * sin * scale
            k = k * cos / scale + rotate_half(k) * sin / scale
            return (q, k)

        def local_attention(q, k, v):
            b, h, n, d = q.shape
            w = n // WINDOW
            bq = q.reshape(b, h, w, WINDOW, d) * QK_SCALE
            bk = k.reshape(b, h, w, WINDOW, d)
            bv = v.reshape(b, h, w, WINDOW, d)

            def look_around(t):
                p = jnp.pad(t, ((0, 0), (0, 0), (1, 0), (0, 0), (0, 0)))
                return jnp.concatenate([p[:, :, :w], p[:, :, 1:]], axis=3)
            bk, bv = (look_around(bk), look_around(bv))
            bt = jnp.arange(n).reshape(w, WINDOW)
            btp = jnp.pad(bt, ((1, 0), (0, 0)), constant_values=-1)
            btk = jnp.concatenate([btp[:w], btp[1:]], axis=1)
            sim = jnp.einsum('bhwid,bhwjd->bhwij', bq, bk)
            i = bt[:, :, None]
            j = btk[:, None, :]
            mask = (i < j) | (i > j + WINDOW) | (j == -1)
            sim = jnp.where(mask, -jnp.finfo(sim.dtype).max, sim)
            attn = jax.nn.softmax(sim, axis=-1)
            out = jnp.einsum('bhwij,bhwjd->bhwid', attn, bv)
            return out.reshape(b, h, n, d)

        def _layer(x, wqkv, qs, ksc, wo, lg, lb, w1, b1, w2, b2):
            b, n, _ = x.shape
            h = shift_token(x)
            qkv = h @ wqkv
            q, k, v = jnp.split(qkv, 3, axis=-1)
            to_heads = lambda t: t.reshape(b, n, HEADS, DIM_HEAD).transpose(0, 2, 1, 3)
            q, k, v = (to_heads(q), to_heads(k), to_heads(v))
            q = l2norm(q) * qs
            k = l2norm(k) * ksc
            q, k = rotary_xpos(q, k)
            o = local_attention(q, k, v)
            o = o.transpose(0, 2, 1, 3).reshape(b, n, INNER)
            x = x + o @ wo
            h = shift_token(x)
            mu = h.mean(-1, keepdims=True)
            var = h.var(-1, keepdims=True)
            h = (h - mu) / jnp.sqrt(var + 1e-05) * lg + lb
            h = h @ w1 + b1
            a, g = jnp.split(h, 2, axis=-1)
            h = a * jax.nn.gelu(g, approximate=False)
            x = x + h @ w2 + b2
            return x
        for l in range(DEPTH):
            x = _layer(x, wqkv[l], q_scale[l], k_scale[l], wo[l], ln_g[l], ln_b[l], w1[l], b1[l], w2[l], b2[l])
        return x

    def _L2_xattn_ref(q, kv, Wq, bq, Wk, bk, Wv, bv, Wo, bo, scale):
        import jax, jax.numpy as jnp
        import numpy as np
        B, LQ, LKV = (4, 128, 512)
        DQ, DKV, H = (256, 192, 16)
        HD = DQ // H
        b, lq, _ = q.shape
        lkv = kv.shape[1]
        qh = (q @ Wq + bq).reshape(b, lq, H, HD).transpose(0, 2, 1, 3)
        kh = (kv @ Wk + bk).reshape(b, lkv, H, HD).transpose(0, 2, 1, 3)
        vh = (kv @ Wv + bv).reshape(b, lkv, H, HD).transpose(0, 2, 1, 3)
        scores = jnp.einsum('bhqd,bhkd->bhqk', qh, kh) * scale[0]
        attn = jax.nn.softmax(scores, axis=-1)
        out = jnp.einsum('bhqk,bhkd->bhqd', attn, vh)
        out = out.transpose(0, 2, 1, 3).reshape(b, lq, DQ)
        return out @ Wo + bo

    def _L2_ffn_ref(hidden_states, Wg, W1, b1, W2, b2, Ws1, bs1, Ws2, bs2):
        import jax, jax.numpy as jnp
        import numpy as np
        B, S, H = (2, 512, 256)
        F = 1024
        E = 8
        TOP_K = 2
        SHARED_SCALE = 0.1
        EPS = 1e-09

        def _moe_forward(x3, Wg, W1, b1, W2, b2, Ws1, bs1, Ws2, bs2):
            b, s, h = x3.shape
            x = x3.reshape(-1, h)
            T = x.shape[0]
            logits = x @ Wg
            probs = jax.nn.softmax(logits, axis=-1)
            vals, idx = jax.lax.top_k(probs, TOP_K)
            weights = vals / (jnp.sum(vals, axis=-1, keepdims=True) + EPS)
            cw = jnp.zeros((T, E), dtype=x.dtype).at[jnp.arange(T)[:, None], idx].set(weights)
            hpre = jnp.einsum('th,ehf->tef', x, W1) + b1
            act = jax.nn.silu(hpre)
            y = jnp.einsum('tef,efh->teh', act, W2) + b2
            out = jnp.einsum('te,teh->th', cw, y)
            shared = jax.nn.silu(x @ Ws1 + bs1) @ Ws2 + bs2
            out = out + SHARED_SCALE * shared
            return out.reshape(b, s, h)
        return _moe_forward(hidden_states, Wg, W1, b1, W2, b2, Ws1, bs1, Ws2, bs2)

    def _L3_xattn_ref(tokens, context, Wq, Wk, Wv, Wo, bo):
        import jax, jax.numpy as jnp
        import numpy as np
        EMBED_DIM = 256
        HIDDEN_DIM = 256
        NUM_HEADS = 16
        CONTEXT_DIM = 192
        HEAD_DIM = EMBED_DIM // NUM_HEADS
        SCALE = HEAD_DIM ** (-0.5)

        def _split_heads(x):
            b, n, _ = x.shape
            return x.reshape(b, n, NUM_HEADS, -1).transpose(0, 2, 1, 3)
        Q = _split_heads(tokens @ Wq)
        K = _split_heads(context @ Wk)
        V = _split_heads(context @ Wv)
        scores = jnp.einsum('bhnd,bhmd->bhnm', Q, K) * SCALE
        attn = jax.nn.softmax(scores, axis=-1)
        out = jnp.einsum('bhnm,bhmd->bhnd', attn, V)
        b, h, n, d = out.shape
        out = out.transpose(0, 2, 1, 3).reshape(b, n, h * d)
        return out @ Wo + bo

    def _L3_ffn_ref(x, router_weight, router_bias, w_gate, w_up, w_down):
        import jax, jax.numpy as jnp
        import numpy as np
        from jax import lax
        TOP_K = 4
        N_GROUP = 4
        TOPK_GROUP = 2
        ROUTED_SCALE = 2.5
        NEG_INF = -1000000000.0

        def _route(xf, router_weight, router_bias):
            T = xf.shape[0]
            E = router_weight.shape[0]
            logits = xf @ router_weight.T
            scores = jax.nn.sigmoid(logits)
            s_choice = scores + router_bias
            per_group = E // N_GROUP
            sg = s_choice.reshape(T, N_GROUP, per_group)
            group_scores = lax.top_k(sg, 2)[0].sum(-1)
            _, gidx = lax.top_k(group_scores, TOPK_GROUP)
            gmask = jnp.zeros((T, N_GROUP), dtype=bool).at[jnp.arange(T)[:, None], gidx].set(True)
            masked = jnp.where(gmask[:, :, None], sg, NEG_INF).reshape(T, E)
            _, topk_idx = lax.top_k(masked, TOP_K)
            w = jnp.take_along_axis(scores, topk_idx, axis=1)
            w = w / (w.sum(-1, keepdims=True) + 1e-20) * ROUTED_SCALE
            combine = jnp.zeros((T, E), dtype=xf.dtype).at[jnp.arange(T)[:, None], topk_idx].add(w)
            return combine
        B, S, H = x.shape
        E = w_gate.shape[0]
        xf = x.reshape(-1, H)
        combine = _route(xf, router_weight, router_bias)
        out = jnp.zeros_like(xf)
        for e in range(E):
            g = xf @ w_gate[e].T
            u = xf @ w_up[e].T
            y_e = jax.nn.silu(g) * u @ w_down[e].T
            out = out + combine[:, e:e + 1] * y_e
        return out.reshape(B, S, H)
    x = x + _L0_xattn_ref(_layernorm(x, axis=-1), ctx_768, mask_BxS2_bf1, L0_xattn_Wq, L0_xattn_Wk, L0_xattn_Wv, L0_xattn_Wo)
    x = x + _L0_ffn_ref(_layernorm(x, axis=-1), L0_ffn_Wr, L0_ffn_W1, L0_ffn_W2)
    x = x + _L1_xattn_ref(_layernorm(x, axis=-1), ctx_768, L1_xattn_Wv, L1_xattn_bv, L1_xattn_Wt, L1_xattn_bt)
    x = x + _L1_ffn_ref(_layernorm(x, axis=-1), L1_ffn_wqkv, L1_ffn_q_scale, L1_ffn_k_scale, L1_ffn_wo, L1_ffn_ln_g, L1_ffn_ln_b, L1_ffn_w1, L1_ffn_b1, L1_ffn_w2, L1_ffn_b2)
    x = x + _L2_xattn_ref(_layernorm(x, axis=-1), ctx_768, L2_xattn_Wq, L2_xattn_bq, L2_xattn_Wk, L2_xattn_bk, L2_xattn_Wv, L2_xattn_bv, L2_xattn_Wo, L2_xattn_bo, L2_xattn_scale)
    x = x + _L2_ffn_ref(_layernorm(x, axis=-1), L2_ffn_Wg, L2_ffn_W1, L2_ffn_b1, L2_ffn_W2, L2_ffn_b2, L2_ffn_Ws1, L2_ffn_bs1, L2_ffn_Ws2, L2_ffn_bs2)
    x = x + _L3_xattn_ref(_layernorm(x, axis=-1), ctx_768, L3_xattn_Wq, L3_xattn_Wk, L3_xattn_Wv, L3_xattn_Wo, L3_xattn_bo)
    x = x + _L3_ffn_ref(_layernorm(x, axis=-1), L3_ffn_router_weight, L3_ffn_router_bias, L3_ffn_w_gate, L3_ffn_w_up, L3_ffn_w_down)
    return x

_drawn_inputs = setup_inputs


def setup_inputs(seed=0):
    import zlib

    import numpy as np

    out = dict(_drawn_inputs(seed))
    spreads = {'L1_ffn_q_scale': (1.0, 0.6),
     'L1_ffn_k_scale': (1.0, 0.6),
     'L1_ffn_ln_g': (1.0, 0.6),
     'L1_ffn_ln_b': (0.0, 0.8),
     'L1_ffn_b1': (0.0, 0.8),
     'L1_ffn_b2': (0.0, 0.1),
     'L2_xattn_bq': (0.0, 0.8),
     'L2_xattn_bk': (0.0, 2.0),
     'L2_xattn_bv': (0.0, 0.1),
     'L2_xattn_bo': (0.0, 0.1),
     'L2_ffn_b1': (0.0, 0.8),
     'L2_ffn_b2': (0.0, 0.298),
     'L2_ffn_bs1': (0.0, 0.8),
     'L2_ffn_bs2': (0.0, 0.8),
     'L3_ffn_router_bias': (0.0, 0.8)}
    factors = {'L0_ffn_W1': 3.435,
     'L0_ffn_W2': 2.879,
     'L1_xattn_bv': 8.0,
     'L1_xattn_bt': 41.565,
     'L1_ffn_w1': 3.081,
     'L1_ffn_w2': 3.057,
     'L2_xattn_Wq': 3.166,
     'L2_xattn_Wk': 3.171,
     'L2_ffn_Ws1': 8.0,
     'L2_ffn_Ws2': 8.0,
     'L3_xattn_bo': 8.0,
     'L3_ffn_router_weight': 8.0,
     'L3_ffn_w_gate': 8.0,
     'L3_ffn_w_up': 8.0,
     'L3_ffn_w_down': 8.0}
    for name, (base, spread) in spreads.items():
        noise = np.random.default_rng([zlib.crc32(name.encode()), seed]).standard_normal(out[name].shape)
        drawn = base * np.exp(spread * noise) if base else spread * noise
        out[name] = jnp.asarray(drawn.astype(out[name].dtype))
    for name, factor in factors.items():
        out[name] = (out[name] * factor).astype(out[name].dtype)
    return out
```

```python
from contextlib import ExitStack

import numpy as np

import concourse.bass as bass
from concourse import mybir

F32 = mybir.dt.float32
BF16 = mybir.dt.bfloat16
F32R = mybir.dt.float32r
U8 = mybir.dt.uint8
ALU = mybir.AluOpType
ACT = mybir.ActivationFunctionType
AX_X = mybir.AxisListType.X
ds = bass.ds

P = 128
B, S, D = 8, 256, 256
T = B * S
NT = T // P
KD = D // P
DC = 192
KC = [P, DC - P]
GROUP = 512
NG = T // GROUP
TPG = GROUP // P
EPS = 1e-5
HUGE = 1e30

HEADS, HD, SLOT = 16, 16, 32
CHUNKS = HEADS * SLOT // P
HPC = P // SLOT
MASK_ROW, MAX_ROW = HD, HD + 1

E, FF = 8, 1024
FC = FF // P
CAP = int(1.25 * T / E)
E3, I3, NGRP3, TOPG3, TOPK3, SCALED3 = 16, 128, 4, 2, 4, 2.5

HSIM = 128
DEPTH, LH, LD, WIN = 2, 8, 64, 128
INNER = LH * LD
HID = int(D * 4 * 2 / 3)
HC_FF = -(-HID // P)
HPAD = HC_FF * P
QK_SCALE = 8.0


SIGNALS = """dve_step dve_pair pool_step variance powered normed turned xT_put kept mask_step ctx_staged qk_proj
qk_put v_proj v_put scored max_put max_turned q_topped scored_T exped weighed summed o_normed o_turned o_put y_done
y_added logits logitsT_put shifted chosen counted h_done h_put gated expert_used squared sq_summed rooted z_staged
h_turned qkv_done lengthed q_rotated k_rotated qk_turned max_negated p_turned p_put inverted set_up
q_rest_put k_rest_put spread""".split()
DMA_SIGNALS = "loaded weights_in even_expert_in odd_expert_in shifted_in stored".split()


class Signal:

    def __init__(self, sem, base):
        self.sem, self.base = sem, base

    def __call__(self, n):
        return self.sem, self.base + n

    def spent(self, n):
        self.base += n


class Steps:

    def __init__(self, count, i=0, per=0):
        self.count, self.at, self.n = count, i * per, 0

    def mark(self, ins):
        self.n += 1
        return ins.then_inc(self.count.sem, 1)

    def settle(self, eng):
        eng.wait_ge(*self.count(self.at + self.n))

    def link(self, eng, ins):
        self.mark(ins)
        self.settle(eng)


class Core:

    def __init__(self, nc, ctx, dram):
        self.nc, self.ctx, self.dram, self.counts, self.tensors = nc, ctx, dram, {}, 0
        for names, base in ((SIGNALS, 1), (DMA_SIGNALS, 0)):
            for name in names:
                self.counts[name] = Signal(ctx.enter_context(nc.semaphore(name)), base)
        self.x = self.sb("x_res", [P, NT, D])
        self.xT = self.sb("xn_T", [P, KD, T])
        self.xn = self.sb("xn_tok", [P, NT, D])
        self.ctxT = self.sb("ctx_T", [P, 2, T])
        self.ident = self.sb("ident", [P, P])
        self.ones = self.sb("ones", [P, P])
        self.half = self.sb("pow_half", [P, 2, P])
        self.ps = ctx.enter_context(nc.psum_tensor("ps", [P, 8, 512], F32))

    def sb(self, name, shape, dt=F32, ctx=None):
        self.tensors += 1
        return (ctx or self.ctx).enter_context(self.nc.sbuf_tensor(f"{name}_{self.tensors}", shape, dt))

    def sig(self, name):
        return self.counts[name]


def load_phase(c):
    nc, loaded, set_up = c.nc, c.sig("loaded"), c.sig("set_up")
    with nc.Block() as block:
        @block.vector
        def _(dve):
            for name in SIGNALS:
                if name != "set_up":
                    dve.sem_inc(c.sig(name).sem, 1)

        @block.sync
        def _(sp):
            for name, dst in (("x", c.x), ("ctxT", c.ctxT), ("ident", c.ident)):
                sp.dma_start(dst[:], c.dram[name]).then_inc(loaded.sem, 16)
            sp.wait_ge(*loaded(48))

        @block.gpsimd
        def _(pool):
            nc.gpsimd.memset(c.ones[:], 1.0).then_inc(set_up.sem, 1)
            nc.gpsimd.memset(c.half[:, 0], 0.5).then_inc(set_up.sem, 1)
            nc.gpsimd.memset(c.half[:, 1], -0.5).then_inc(set_up.sem, 1)
            pool.sem_inc(set_up.sem, 1)
            pool.wait_ge(*set_up(3))
    loaded.spent(48)
    set_up.spent(3)


def store_phase(c):
    nc, stored = c.nc, c.sig("stored")
    with nc.Block() as block:
        @block.sync
        def _(sp):
            sp.dma_start(c.dram["out"], c.x[:]).then_inc(stored.sem, 16)
            sp.wait_ge(*stored(16))
    stored.spent(16)


def norm_phase(c, pieces, keep=False, transposed=True, affine=None):
    nc, ctx = c.nc, ExitStack()
    stepped, variance, powered = c.sig("dve_step"), c.sig("variance"), c.sig("powered")
    normed, turned, put, kept = c.sig("normed"), c.sig("turned"), c.sig("xT_put"), c.sig("kept")
    npc, count = len(pieces), [0]
    ns = 2 * npc
    with ctx:
        xs = c.sb("ln_row", [P, 2, D], ctx=ctx)
        stats = c.sb("ln_stats", [P, NT, ns, 3], ctx=ctx)
        mean, rstd, var = (c.sb("ln_" + n, [P, NT], ctx=ctx) for n in ("mean", "rstd", "var"))
        total, sq_in, sq_dev = (c.sb("ln_" + n, [P, NT], ctx=ctx) for n in ("total", "sq_in", "sq_dev"))
        dev = c.sb("ln_dev", [P, 2, NT, ns], ctx=ctx)
        block = ctx.enter_context(nc.Block(no_gpsimd_drain=True))

        @block.vector
        def _(dve):
            step = Steps(stepped)
            for t in range(NT):
                for n, (src, _) in enumerate(pieces):
                    ins = nc.vector.bn_stats(stats[:, t, 2 * n:2 * n + 2].rearrange("p a b -> p (a b)"), src[:, t])
            step.link(dve, ins)
            step.mark(nc.vector.tensor_reduce(sq_in[:], stats[:, :, :, 2], AX_X, ALU.add))
            step.link(dve, nc.vector.tensor_reduce(total[:], stats[:, :, :, 1], AX_X, ALU.add))
            step.link(dve, nc.vector.tensor_scalar(mean[:], total[:], 1.0 / ns, None, ALU.mult))
            step.link(dve, nc.vector.tensor_tensor(dev[:, 0], stats[:, :, :, 1],
                                                   mean[:].unsqueeze(2).to_broadcast([P, NT, ns]), ALU.subtract))
            step.link(dve, nc.vector.tensor_tensor(dev[:, 1], dev[:, 0], dev[:, 0], ALU.mult))
            step.link(dve, nc.vector.tensor_reduce(sq_dev[:], dev[:, 1], AX_X, ALU.add))
            step.link(dve, nc.vector.scalar_tensor_tensor(total[:], sq_dev[:], float(D // ns), sq_in[:], ALU.mult,
                                                          ALU.add))
            nc.vector.tensor_scalar(var[:], total[:], 1.0 / D, EPS, ALU.mult, ALU.add).then_inc(variance.sem, 1)
            count[0] = step.n
            dve.wait_ge(*powered(1))
            with dve.Fori(0, NT // 2) as i:
                for s in range(2):
                    t = 2 * i + s
                    if transposed:
                        dve.wait_ge(*turned(2 * i))
                    if keep:
                        dve.wait_ge(*kept(2 * i))
                    for src, at in pieces:
                        ins = nc.vector.tensor_scalar(xs[:, s, at:at + D // npc], src[:, ds(t, 1)].squeeze(1),
                                                      mean[:, ds(t, 1)], rstd[:, ds(t, 1)], ALU.subtract, ALU.mult)
                    ins.then_inc(normed.sem, 1)

        @block.gpsimd
        def _(pool):
            pool.wait_ge(*variance(1))
            nc.gpsimd.tensor_tensor(rstd[:], var[:], c.half[:, 1, 0:NT], ALU.pow).then_inc(powered.sem, 1)
            if keep:
                with pool.Fori(0, NT // 2) as i:
                    for s in range(2):
                        pool.wait_ge(*normed(2 * i + s + 1))
                        nc.gpsimd.tensor_copy(c.xn[:, ds(2 * i + s, 1)], xs[:, s]).then_inc(kept.sem, 1)
                pool.wait_ge(*kept(NT))

        if transposed:
            @block.tensor
            def _(pe):
                with pe.Fori(0, NT // 2) as i:
                    for s in range(2):
                        pe.wait_ge(*put(2 * i))
                        pe.wait_ge(*normed(2 * i + s + 1))
                        for k in range(KD):
                            ins = nc.tensor.transpose(c.ps[:, s, k * P:(k + 1) * P], xs[:, s, k * P:(k + 1) * P],
                                                      c.ident[:])
                        ins.then_inc(turned.sem, 1)

            @block.scalar
            def _(act):
                with act.Fori(0, NT // 2) as i:
                    for s in range(2):
                        cols = ds((2 * i + s) * P, P)
                        act.wait_ge(*turned(2 * i + s + 1))
                        if affine is None:
                            ins = nc.scalar.copy(c.xT[:, :, cols], c.ps[:, s, 0:D].rearrange("p (k t) -> p k t", k=KD))
                        else:
                            for k in range(KD):
                                ins = nc.scalar.activation(c.xT[:, k, cols], c.ps[:, s, k * P:(k + 1) * P],
                                                           ACT.Identity, scale=affine[:, 0, k:k + 1],
                                                           bias=affine[:, 1, k:k + 1])
                        ins.then_inc(put.sem, 1)
    stepped.spent(count[0])
    for sgn, n in ((variance, 1), (powered, 1), (normed, NT)):
        sgn.spent(n)
    if transposed:
        turned.spent(NT)
        put.spent(NT)
    if keep:
        kept.spent(NT)


def xattn_phase(c, tag, masked=False, scale=0.25, biased=False, scale_in=False):
    nc, ctx, dram = c.nc, ExitStack(), c.dram
    names = ("weights_in", "mask_step", "ctx_staged", "qk_proj", "qk_put", "v_proj", "v_put", "q_rest_put",
             "k_rest_put", "scored", "max_put", "max_turned", "q_topped", "scored_T", "exped", "weighed", "o_put",
             "summed", "inverted", "spread", "o_normed", "y_done", "y_added")
    (loaded, mstep, staged, qk_proj, qk_put, v_proj, v_put, q_rest, k_rest, scored, max_put, max_turned,
     topped, scored_T, exped, weighed, o_put, summed, inverted, spread, o_normed, y_done, y_added) = (
        c.sig(n) for n in names)
    PAIRS = HEADS // 2
    with ctx:
        def sb(name, shape, dt=F32):
            return c.sb("xa_" + name, shape, dt, ctx)

        wq, wk = sb("wq", [P, KD, HEADS * SLOT]), sb("wk", [P, 2, HEADS * SLOT])
        wv, wo = sb("wv", [P, 2, D]), sb("wo", [P, CHUNKS, D])
        cols = sb("cols", [P, 2, CHUNKS])
        pick, give = sb("pick", [P, CHUNKS, HEADS]), sb("give", [P, CHUNKS, P])
        rows = sb("rows", [1, 2, D]) if biased else None
        qk = sb("qk", [P, 2, 2, S])
        qh, ql = sb("qh", [P, CHUNKS, S], F32R), sb("ql", [P, CHUNKS, S], F32R)
        kh, kl = sb("kh", [P, HEADS, S], F32R), sb("kl", [P, HEADS, S], F32R)
        cst = sb("ctx", [P, 2, S])
        va = sb("v", [P, 2, HEADS, SLOT])
        mx = sb("mx", [P, 2, CHUNKS, HPC, SLOT], F32R)
        pt = sb("pT", [P, 2, HPC, 2, S])
        ot, rec = sb("ot", [P, CHUNKS, S]), sb("rec", [P, S])
        qscale = sb("qscale", [P, 1]) if scale_in else None
        qcols = sb("qcols", [P, CHUNKS]) if scale_in else None
        ctxk = c.ctxT
        if masked:
            mask8, mask = sb("mask8", [P, T], U8), sb("mask", [P, T])
            anyk, mbias, ctxk = sb("anyk", [P, B]), sb("mbias", [1, T]), sb("ctxk", [P, 2, T])
            rowsel = sb("rowsel", [1, P])
        n_loads = 7 + biased + scale_in + 2 * masked
        block = ctx.enter_context(nc.Block(no_gpsimd_drain=True))
        MSTEPS = 7 if masked else 2 if scale_in else 1

        @block.sync
        def _(sp):
            loads = [(wq, tag + "wq"), (wk, tag + "wk"), (wv, tag + "wv"), (wo, tag + "wo"), (cols, tag + "cols"),
                     (pick, "pick"), (give, "give")]
            loads += [(rows, tag + "rows")] if biased else []
            loads += [(rowsel, "rowsel")] if masked else []
            for dst, name in loads:
                sp.dma_start(dst[:], dram[name]).then_inc(loaded.sem, 16)
            if scale_in:
                sp.dma_start(qscale[:], dram[tag + "scale"].partition_broadcast(P)).then_inc(loaded.sem, 16)
            if masked:
                sp.dma_start(mask8[:], dram["mask"].partition_broadcast(P)).then_inc(loaded.sem, 16)

        @block.gpsimd
        def _(pool):
            nc.gpsimd.memset(kh[:].bitcast(F32), 0.0)
            nc.gpsimd.memset(kl[:].bitcast(F32), 0.0)
            nc.gpsimd.memset(rec[:], 0.0)
            nc.gpsimd.memset(mx[:].bitcast(F32), 0.0)
            nc.gpsimd.memset(va[:], 1.0).then_inc(mstep.sem, 1)
            pool.wait_ge(*mstep(1))
            with pool.Fori(0, B) as i:
                pool.wait_ge(*v_proj(2 * i))
                nc.gpsimd.tensor_copy(cst[:], c.ctxT[:, :, ds(i * S, S)]).then_inc(staged.sem, 1)
                for ch in range(CHUNKS):
                    pool.wait_ge(*qk_put(CHUNKS * i + ch + 1))
                    nc.gpsimd.tensor_tensor(ql[:, ch], qk[:, ch % 2, 0], qh[:, ch].bitcast(F32), ALU.subtract
                                            ).then_inc(q_rest.sem, 1)
            pool.wait_ge(*q_rest(CHUNKS * B))

        @block.tensor
        def _(pe):
            pe.wait_ge(*loaded(16 * n_loads))
            pe.wait_ge(*mstep(MSTEPS))
            with pe.Fori(0, B) as i:
                cols_of = ds(i * S, S)
                for ch in range(CHUNKS):
                    if ch < 2:
                        pe.wait_ge(*o_normed(2 * i))
                    else:
                        pe.wait_ge(*qk_put(CHUNKS * i + ch - 1))
                    bank = c.ps[:, 4 + ch % 2]
                    w = slice(ch * P, (ch + 1) * P)
                    for kk in range(KD):
                        nc.tensor.matmul(bank[:, 0:S], wq[:, kk, w], c.xT[:, kk, cols_of],
                                         start=(kk == 0), stop=(kk == KD - 1))
                    for kk, rows_k in enumerate(KC):
                        ins = nc.tensor.matmul(bank[:, S:2 * S], wk[0:rows_k, kk, w], ctxk[0:rows_k, kk, cols_of],
                                               start=(kk == 0), stop=(kk == 1 and not masked))
                    if masked:
                        ins = nc.tensor.matmul(bank[:, S:2 * S], rowsel[:], mbias[:, cols_of], start=False, stop=True)
                    ins.then_inc(qk_proj.sem, 1)
                pe.wait_ge(*staged(i + 1))
                for kt in range(2):
                    bank = c.ps[:, 6 + kt]
                    if biased:
                        nc.tensor.matmul(bank[:, 0:D], c.ones[0:1, :], rows[:, 0], start=True, stop=False)
                    for kk, rows_k in enumerate(KC):
                        ins = nc.tensor.matmul(bank[:, 0:D], cst[0:rows_k, kk, kt * P:(kt + 1) * P], wv[0:rows_k, kk],
                                               start=(kk == 0 and not biased), stop=(kk == 1))
                    ins.then_inc(v_proj.sem, 1)
                pe.wait_ge(*y_added(2 * i))
                for p in range(PAIRS):
                    ch = p // 2
                    if p % 2 == 0:
                        pe.wait_ge(*qk_put(CHUNKS * i + ch + 1))
                    if p < 2:
                        pe.wait_ge(*exped(PAIRS * i))
                    else:
                        pe.wait_ge(*max_put(PAIRS * i + p - 1))
                    for j in range(2):
                        for qt in range(2):
                            ins = nc.tensor.matmul(c.ps[:, 2 * (p % 2) + j, qt * S:(qt + 1) * S],
                                                   qh[:, ch, qt * P:(qt + 1) * P], kh[:, 2 * p + j, :],
                                                   start=True, stop=True)
                    ins.then_inc(scored.sem, 1)
                for ch in range(CHUNKS):
                    pe.wait_ge(*max_put(PAIRS * i + 2 * ch + 2))
                    if ch < 2:
                        pe.wait_ge(*qk_put(CHUNKS * i + CHUNKS))
                    else:
                        pe.wait_ge(*topped(CHUNKS * i + ch - 1))
                    for qt in range(2):
                        ins = nc.tensor.transpose(c.ps[:, 4 + ch % 2, qt * P:(qt + 1) * P],
                                                  mx[:, qt, ch].rearrange("p h s -> p (h s)").bitcast(F32),
                                                  c.ident[:])
                    ins.then_inc(max_turned.sem, 1)

                def score_T(p):
                    ch = p // 2
                    pe.wait_ge(*topped(CHUNKS * i + ch + 1))
                    pe.wait_ge(*k_rest(CHUNKS * i + ch + 1))
                    pe.wait_ge(*q_rest(CHUNKS * i + ch + 1))
                    if p < 2:
                        pe.wait_ge(*max_put(PAIRS * i + PAIRS))
                    else:
                        pe.wait_ge(*exped(PAIRS * i + p - 1))
                    for j in range(2):
                        for kt in range(2):
                            out = c.ps[:, 2 * (p % 2) + j, kt * S:(kt + 1) * S]
                            keys = slice(kt * P, (kt + 1) * P)
                            nc.tensor.matmul(out, kh[:, 2 * p + j, keys], qh[:, ch, :], start=True, stop=False)
                            nc.tensor.matmul(out, kh[:, 2 * p + j, keys], ql[:, ch, :], start=False, stop=False)
                            ins = nc.tensor.matmul(out, kl[:, 2 * p + j, keys], qh[:, ch, :], start=False, stop=True)
                    ins.then_inc(scored_T.sem, 1)

                def weigh(ch):
                    pe.wait_ge(*exped(PAIRS * i + 2 * ch + 2))
                    if ch == 0:
                        pe.wait_ge(*v_put(2 * i + 2))
                    for kt in range(2):
                        for j in range(HPC):
                            ins = nc.tensor.matmul(
                                c.ps[j * SLOT:(j + 1) * SLOT, 6 + ch // 2, (ch % 2) * S:(ch % 2 + 1) * S],
                                va[:, kt, ch * HPC + j], pt[:, ch % 2, j, kt], start=(kt == 0), stop=(kt == 1),
                                tile_position=(0, j * SLOT))
                    ins.then_inc(weighed.sem, 1)

                for ch in range(CHUNKS):
                    score_T(2 * ch)
                    score_T(2 * ch + 1)
                    if ch >= 1:
                        weigh(ch - 1)
                weigh(CHUNKS - 1)
                pe.wait_ge(*o_put(2 * i + 2))
                for ch in range(CHUNKS):
                    ins = nc.tensor.matmul(c.ps[0:HEADS, 4, 0:S], pick[:, ch], ot[:, ch], start=(ch == 0),
                                           stop=(ch == CHUNKS - 1))
                ins.then_inc(summed.sem, 1)
                pe.wait_ge(*inverted(i + 1))
                for ch in range(CHUNKS):
                    ins = nc.tensor.matmul(c.ps[:, 5 - ch // 2, (ch % 2) * S:(ch % 2 + 1) * S], give[:, ch], rec[:],
                                           start=True, stop=True)
                    if ch % 2:
                        ins.then_inc(spread.sem, 1)
                pe.wait_ge(*o_normed(2 * i + 2))
                for qt in range(2):
                    if biased:
                        nc.tensor.matmul(c.ps[:, qt, 0:D], c.ones[0:1, :], rows[:, 1], start=True, stop=False)
                    for ch in range(CHUNKS):
                        ins = nc.tensor.matmul(c.ps[:, qt, 0:D], ot[:, ch, qt * P:(qt + 1) * P], wo[:, ch],
                                               start=(ch == 0 and not biased), stop=(ch == CHUNKS - 1))
                    ins.then_inc(y_done.sem, 1)

        @block.scalar
        def _(act):
            act.wait_ge(*loaded(16 * n_loads))
            act.wait_ge(*mstep(MSTEPS))
            with act.Fori(0, B) as i:
                for ch in range(CHUNKS):
                    act.wait_ge(*qk_proj(CHUNKS * i + ch + 1))
                    before = CHUNKS * i + ch - 1 if ch >= 2 else CHUNKS * i
                    act.wait_ge(*q_rest(before))
                    act.wait_ge(*k_rest(before))
                    bank = c.ps[:, 4 + ch % 2]
                    for q in (qk[:, ch % 2, 0], qh[:, ch]):
                        nc.scalar.activation(q, bank[:, 0:S], ACT.Identity,
                                             bias=qcols[:, ch:ch + 1] if scale_in else cols[:, 0, ch:ch + 1],
                                             scale=qscale[:, 0:1] if scale_in else scale)
                    nc.scalar.activation(qk[:, ch % 2, 1], bank[:, S:2 * S], ACT.Identity, bias=cols[:, 1, ch:ch + 1])
                    for j in range(HPC):
                        r = slice(j * SLOT, (j + 1) * SLOT)
                        ins = nc.scalar.activation(kh[r, ch * HPC + j], bank[r, S:2 * S], ACT.Identity,
                                                   bias=cols[r, 1, ch:ch + 1])
                    ins.then_inc(qk_put.sem, 1)
                for p in range(PAIRS):
                    act.wait_ge(*scored_T(PAIRS * i + p + 1))
                    if p >= 4:
                        act.wait_ge(*weighed(CHUNKS * i + p // 2 - 1))
                    b0 = 2 * (p % 2)
                    nc.scalar.activation(pt[:, p // 2 % 2, b0:b0 + 2].rearrange("p j k s -> p (j k s)"),
                                         c.ps[:, b0:b0 + 2].rearrange("p j n -> p (j n)"),
                                         ACT.Exp).then_inc(exped.sem, 1)
                for n in range(2):
                    act.wait_ge(*weighed(CHUNKS * i + 2 * n + 2))
                    nc.scalar.copy(ot[:, 2 * n:2 * n + 2].rearrange("p c s -> p (c s)"), c.ps[:, 6 + n]
                                   ).then_inc(o_put.sem, 1)

        @block.vector
        def _(dve):
            step = Steps(mstep)
            step.n = 1
            dve.wait_ge(*mstep(1))
            dve.wait_ge(*loaded(16 * n_loads))
            if masked:
                step.link(dve, nc.vector.tensor_copy(mask[:], mask8[:]))
                step.mark(nc.vector.tensor_tensor(ctxk[:, 0], c.ctxT[:, 0], mask[:], ALU.mult))
                step.mark(nc.vector.tensor_tensor(ctxk[0:KC[1], 1], c.ctxT[0:KC[1], 1], mask[0:KC[1]], ALU.mult))
                step.link(dve, nc.vector.tensor_reduce(anyk[:], mask[:].rearrange("p (b s) -> p b s", b=B), AX_X,
                                                       ALU.max))
                step.link(dve, nc.vector.tensor_scalar(mbias[:], mask[0:1], -1.0, HUGE, ALU.add, ALU.mult))
                step.link(dve, nc.vector.tensor_tensor(
                    mbias[:].rearrange("p (b s) -> p b s", b=B), mbias[:].rearrange("p (b s) -> p b s", b=B),
                    anyk[0:1].unsqueeze(2).to_broadcast([1, B, S]), ALU.mult))
            elif scale_in:
                step.link(dve, nc.vector.tensor_scalar(qcols[:], cols[:, 0], qscale[:, 0:1], None, ALU.mult))
            assert step.n == MSTEPS
            with dve.Fori(0, B) as i:
                def rest(ch):
                    dve.wait_ge(*qk_put(CHUNKS * i + ch + 1))
                    for j in range(HPC):
                        r = slice(j * SLOT, (j + 1) * SLOT)
                        ins = nc.vector.tensor_tensor(kl[r, ch * HPC + j], qk[r, ch % 2, 1],
                                                      kh[r, ch * HPC + j].bitcast(F32), ALU.subtract)
                    ins.then_inc(k_rest.sem, 1)

                for ch in range(CHUNKS):
                    rest(ch)
                for kt in range(2):
                    dve.wait_ge(*v_proj(2 * i + kt + 1))
                    nc.vector.tensor_copy(va[:, kt, :, 0:HD],
                                          c.ps[:, 6 + kt, 0:D].rearrange("p (h d) -> p h d", h=HEADS)
                                          ).then_inc(v_put.sem, 1)
                for p in range(PAIRS):
                    dve.wait_ge(*scored(PAIRS * i + p + 1))
                    b0 = 2 * (p % 2)
                    nc.vector.tensor_reduce(mx[:, :, p // 2, b0:b0 + 2, MAX_ROW].rearrange("p t h -> p h t"),
                                            c.ps[:, b0:b0 + 2].rearrange("p j (t n) -> p j t n", t=2), AX_X,
                                            ALU.max).then_inc(max_put.sem, 1)
                for ch in range(CHUNKS):
                    dve.wait_ge(*q_rest(CHUNKS * i + ch + 1))
                    dve.wait_ge(*max_turned(CHUNKS * i + ch + 1))
                    nc.vector.tensor_tensor(qh[:, ch], qh[:, ch].bitcast(F32), c.ps[:, 4 + ch % 2, 0:S], ALU.add
                                            ).then_inc(topped.sem, 1)
                dve.wait_ge(*summed(i + 1))
                nc.vector.reciprocal(rec[0:HEADS], c.ps[0:HEADS, 4, 0:S]).then_inc(inverted.sem, 1)
                for n in range(2):
                    dve.wait_ge(*spread(2 * i + n + 1))
                    o = ot[:, 2 * n:2 * n + 2].rearrange("p c s -> p (c s)")
                    nc.vector.tensor_tensor(o, o, c.ps[:, 5 - n], ALU.mult).then_inc(o_normed.sem, 1)
                for qt in range(2):
                    dve.wait_ge(*y_done(2 * i + qt + 1))
                    xt = c.x[:, ds(2 * i + qt, 1)].squeeze(1)
                    nc.vector.tensor_tensor(xt, xt, c.ps[:, qt, 0:D], ALU.add).then_inc(y_added.sem, 1)
    loaded.spent(16 * n_loads)
    mstep.spent(MSTEPS)
    for sgn, n in ((staged, 1), (qk_proj, CHUNKS), (qk_put, CHUNKS), (v_proj, 2), (v_put, 2),
                   (q_rest, CHUNKS), (k_rest, CHUNKS), (scored, PAIRS), (max_put, PAIRS),
                   (max_turned, CHUNKS), (topped, CHUNKS), (scored_T, PAIRS), (exped, PAIRS), (weighed, CHUNKS),
                   (o_put, 2), (summed, 1), (inverted, 1), (spread, 2), (o_normed, 2), (y_done, 2), (y_added, 2)):
        sgn.spent(B * n)


def rank_rule(nc, dve, step, v, gt, eq, tri, rank):
    shape = [P, v.shape[1], v.shape[2], v.shape[2]]
    other, own = v.unsqueeze(2).to_broadcast(shape), v.unsqueeze(3).to_broadcast(shape)
    step.mark(nc.vector.tensor_tensor(gt, other, own, ALU.is_gt))
    step.link(dve, nc.vector.tensor_tensor(eq, other, own, ALU.is_equal))
    step.link(dve, nc.vector.tensor_tensor(eq, eq, tri.unsqueeze(1).to_broadcast(shape), ALU.mult))
    step.link(dve, nc.vector.tensor_tensor(gt, gt, eq, ALU.add))
    step.link(dve, nc.vector.tensor_reduce(rank, gt, AX_X, ALU.add))


def logits_on_pe(c, pe, wr, lgT, n, made, copied, lg_bank=2):
    nc = c.nc
    for g in range(NG):
        if g >= 2:
            pe.wait_ge(*copied(g - 1))
        for k in range(KD):
            ins = nc.tensor.matmul(c.ps[0:n, g % 2, :], wr[:, k], c.xT[:, k, g * GROUP:(g + 1) * GROUP],
                                   start=(k == 0), stop=(k == KD - 1))
        ins.then_inc(made.sem, 1)
    pe.wait_ge(*copied(NG))
    for t in range(NT):
        ins = nc.tensor.transpose(c.ps[:, lg_bank, t * n:(t + 1) * n], lgT[0:n, t * P:(t + 1) * P],
                                  c.ident[0:n, 0:n])
    ins.then_inc(made.sem, 1)


def softmax_router(c, tag, cw, top, passed=None):
    nc, ctx = c.nc, ExitStack()
    loaded, made, copied, step_s = c.sig("weights_in"), c.sig("logits"), c.sig("logitsT_put"), c.sig("dve_step")
    shifted, exped, chosen, counted = c.sig("shifted"), c.sig("exped"), c.sig("chosen"), c.sig("counted")
    with ctx:
        def sb(name, shape):
            return c.sb("ro_" + name, shape, F32, ctx)

        wr, lgT, tri = sb("wr", [P, KD, E]), sb("lgT", [P, T]), sb("tri", [P, E, E])
        upto = sb("upto", [P, P])
        v, pr, hot = sb("v", [P, NT, E]), sb("pr", [P, NT, E]), sb("hot", [P, NT, E])
        gt, eq, rank = sb("gt", [P, NT, E, E]), sb("eq", [P, NT, E, E]), sb("rank", [P, NT, E])
        m, s = sb("m", [P, NT]), sb("s", [P, NT])
        before, run = sb("before", [P, 2, NT, E]), sb("run", [P, NT, E])
        kept = sb("kept", [P, NT])
        block = ctx.enter_context(nc.Block(no_gpsimd_drain=True))
        count = [0]

        @block.sync
        def _(sp):
            sp.dma_start(wr[:], c.dram[tag + "wr"]).then_inc(loaded.sem, 16)
            sp.dma_start(tri[:], c.dram["tri8"].partition_broadcast(P)).then_inc(loaded.sem, 16)
            sp.dma_start(upto[:], c.dram["upto"]).then_inc(loaded.sem, 16)

        @block.tensor
        def _(pe):
            pe.wait_ge(*loaded(48))
            logits_on_pe(c, pe, wr, lgT, E, made, copied)
            if top == 1:
                pe.wait_ge(*chosen(1))
                flat = hot[:].rearrange("p t e -> p (t e)")
                nc.tensor.matmul(c.ps[:, 3, 0:NT * E], upto[:], flat, start=True, stop=True)
                nc.tensor.matmul(c.ps[:, 4, 0:NT * E], c.ones[:], flat, start=True, stop=True
                                 ).then_inc(counted.sem, 1)

        @block.scalar
        def _(act):
            for g in range(NG):
                act.wait_ge(*made(g + 1))
                nc.scalar.copy(lgT[0:E, g * GROUP:(g + 1) * GROUP], c.ps[0:E, g % 2, :]).then_inc(copied.sem, 1)
            act.wait_ge(*shifted(1))
            nc.scalar.activation(pr[:].rearrange("p t e -> p (t e)"), v[:].rearrange("p t e -> p (t e)"),
                                 ACT.Exp).then_inc(exped.sem, 1)

        @block.vector
        def _(dve):
            step = Steps(step_s)
            dve.wait_ge(*made(NG + 1))
            dve.wait_ge(*loaded(48))
            lg = c.ps[:, 2, 0:NT * E].rearrange("p (t e) -> p t e", e=E)
            step.link(dve, nc.vector.tensor_reduce(m[:], lg, AX_X, ALU.max))
            nc.vector.tensor_tensor(v[:], lg, m[:].unsqueeze(2).to_broadcast([P, NT, E]), ALU.subtract
                                    ).then_inc(shifted.sem, 1)
            dve.wait_ge(*exped(1))
            step.link(dve, nc.vector.tensor_reduce(s[:], pr[:], AX_X, ALU.add))
            step.link(dve, nc.vector.reciprocal(s[:], s[:]))
            step.link(dve, nc.vector.tensor_tensor(pr[:], pr[:], s[:].unsqueeze(2).to_broadcast([P, NT, E]),
                                                   ALU.mult))
            rank_rule(nc, dve, step, pr[:], gt[:], eq[:], tri[:], rank[:])
            if top == 2:
                step.link(dve, nc.vector.tensor_scalar(hot[:], rank[:], float(top), None, ALU.is_lt))
                step.link(dve, nc.vector.tensor_tensor(hot[:], hot[:], pr[:], ALU.mult))
                step.link(dve, nc.vector.tensor_reduce(s[:], hot[:], AX_X, ALU.add))
                step.link(dve, nc.vector.tensor_scalar(s[:], s[:], 1e-9, None, ALU.add))
                step.link(dve, nc.vector.reciprocal(s[:], s[:]))
                step.mark(nc.vector.memset(cw[:, :, E], 0.1))
                step.link(dve, nc.vector.tensor_tensor(cw[:, :, 0:E], hot[:],
                                                       s[:].unsqueeze(2).to_broadcast([P, NT, E]), ALU.mult))
            else:
                nc.vector.tensor_scalar(hot[:], rank[:], 1.0, None, ALU.is_lt).then_inc(chosen.sem, 1)
                dve.wait_ge(*counted(1))
                within = c.ps[:, 3, 0:NT * E].rearrange("p (t e) -> p t e", e=E)
                whole = c.ps[:, 4, 0:NT * E].rearrange("p (t e) -> p t e", e=E)
                step.mark(nc.vector.memset(before[:, 0, 0:1], 0.0))
                step.link(dve, nc.vector.tensor_copy(before[:, 0, 1:NT], whole[:, 0:NT - 1]))
                side, d = 0, 1
                while d < NT:
                    a, b = before[:, side], before[:, 1 - side]
                    step.mark(nc.vector.tensor_copy(b[:, 0:d], a[:, 0:d]))
                    step.link(dve, nc.vector.tensor_tensor(b[:, d:NT], a[:, d:NT], a[:, 0:NT - d], ALU.add))
                    side, d = 1 - side, 2 * d
                step.link(dve, nc.vector.tensor_tensor(run[:], within, before[:, side], ALU.add))
                step.link(dve, nc.vector.tensor_tensor(run[:], run[:], hot[:], ALU.mult))
                step.link(dve, nc.vector.tensor_reduce(s[:], run[:], AX_X, ALU.add))
                step.link(dve, nc.vector.tensor_scalar(kept[:], s[:], float(CAP), None, ALU.is_le))
                step.mark(nc.vector.tensor_scalar(passed[:], kept[:], -1.0, 1.0, ALU.mult, ALU.add))
                step.link(dve, nc.vector.tensor_tensor(pr[:], pr[:], hot[:], ALU.mult))
                step.link(dve, nc.vector.tensor_tensor(cw[:, :, 0:E], pr[:],
                                                       kept[:].unsqueeze(2).to_broadcast([P, NT, E]), ALU.mult))
            count[0] = step.n
    step_s.spent(count[0])
    loaded.spent(48)
    made.spent(NG + 1)
    copied.spent(NG)
    shifted.spent(1)
    exped.spent(1)
    if top == 1:
        chosen.spent(1)
        counted.spent(1)


def expert_phases(c, tag):
    nc, ctx, first = c.nc, ExitStack(), tag == "L0f_"
    n_exp = E if first else E + 1
    loads = 2 if first else 4
    w_in, h_done, h_put = [c.sig("even_expert_in"), c.sig("odd_expert_in")], c.sig("h_done"), c.sig("h_put")
    y_done, y_added, used, passing = c.sig("y_done"), c.sig("y_added"), c.sig("expert_used"), c.sig("dve_step")
    with ctx:
        cw = c.sb("cw", [P, NT, n_exp], ctx=ctx)
        passed = c.sb("passed", [P, NT], ctx=ctx) if first else None
        softmax_router(c, tag, cw, 1 if first else 2, passed)
        w1 = c.sb("ex_w1", [P, 2, KD, FF], ctx=ctx)
        w2 = c.sb("ex_w2", [P, 2, FC, D], ctx=ctx)
        b1 = c.sb("ex_b1", [P, 2, FC], ctx=ctx)
        b2 = c.sb("ex_b2", [1, 2, D], ctx=ctx)
        h = c.sb("ex_h", [P, FC, GROUP], ctx=ctx)
        block = ctx.enter_context(nc.Block(no_gpsimd_drain=True))

        def experts(eng, body):
            with eng.Fori(0, n_exp // 2) as i:
                for par in range(2):
                    body(2 * i + par, par, i)
            if n_exp % 2:
                body(n_exp - 1, 0, n_exp // 2)

        @block.sync
        def _(sp):
            def load(e, par):
                parts = [(w1[:, par], "w1"), (w2[:, par], "w2")]
                parts += [] if first else [(b1[:, par], "b1"), (b2[:, par], "b2")]
                for dst, name in parts:
                    sp.dma_start(dst, c.dram[tag + name][ds(e, 1)].squeeze(0)).then_inc(w_in[par].sem, 16)

            load(0, 0)
            load(1, 1)

            with sp.Fori(0, (n_exp - 2) // 2) as i:
                for par in range(2):
                    sp.wait_ge(*used(2 * i + par + 1))
                    load(2 * i + par + 2, par)
            if n_exp % 2:
                sp.wait_ge(*used(n_exp - 2))
                load(n_exp - 1, 0)

        @block.tensor
        def _(pe):
            def expert(e, par, pair):
                with pe.Fori(0, NG) as g:
                    n = e * NG + g
                    pe.wait_ge(*w_in[par](pair * 16 * loads + 16 * loads))
                    for f in range(FC):
                        if f < 2:
                            pe.wait_ge(*h_put(FC * n))
                        else:
                            pe.wait_ge(*h_put(FC * n + f - 1))
                        for k in range(KD):
                            ins = nc.tensor.matmul(c.ps[:, f % 2, :], w1[:, par, k, f * P:(f + 1) * P],
                                                   c.xT[:, k, ds(g * GROUP, GROUP)], start=(k == 0),
                                                   stop=(k == KD - 1))
                        ins.then_inc(h_done.sem, 1)
                    pe.wait_ge(*h_put(FC * n + FC))
                    pe.wait_ge(*y_added(TPG * n))
                    for tt in range(TPG):
                        out = c.ps[:, 2 + tt, 0:D]
                        if not first:
                            nc.tensor.matmul(out, c.ones[0:1, :], b2[:, par], start=True, stop=False)
                        for f in range(FC):
                            ins = nc.tensor.matmul(out, h[:, f, tt * P:(tt + 1) * P], w2[:, par, f],
                                                   start=(first and f == 0), stop=(f == FC - 1))
                        ins.then_inc(y_done.sem, 1)
                pe.wait_ge(*y_added(TPG * NG * (e + 1)))
                pe.sem_inc(used.sem, 1)

            experts(pe, expert)

        @block.scalar
        def _(act):
            def expert(e, par, pair):
                with act.Fori(0, NG) as g:
                    n = e * NG + g
                    for f in range(FC):
                        if not first and f == 0:
                            act.wait_ge(*w_in[par](pair * 16 * loads + 16 * loads))
                        act.wait_ge(*h_done(FC * n + f + 1))
                        nc.scalar.activation(h[:, f], c.ps[:, f % 2, :], ACT.Relu if first else ACT.Silu,
                                             bias=0.0 if first else b1[:, par, f:f + 1]).then_inc(h_put.sem, 1)

            experts(act, expert)

        @block.vector
        def _(dve):
            if first:
                with dve.Fori(0, NT) as t:
                    xt = c.x[:, ds(t, 1)].squeeze(1)
                    nc.vector.scalar_tensor_tensor(xt, c.xn[:, ds(t, 1)].squeeze(1), passed[:, ds(t, 1)], xt, ALU.mult,
                                                   ALU.add).then_inc(passing.sem, 1)
                dve.wait_ge(*passing(NT))

            def expert(e, par, pair):
                with dve.Fori(0, NG) as g:
                    n = e * NG + g
                    dve.wait_ge(*y_added(TPG * n))
                    for tt in range(TPG):
                        dve.wait_ge(*y_done(TPG * n + tt + 1))
                        xt = c.x[:, ds(g * TPG + tt, 1)].squeeze(1)
                        weight = cw[:].rearrange("p t e -> p (t e)")[:, ds((g * TPG + tt) * n_exp + e, 1)]
                        nc.vector.scalar_tensor_tensor(xt, c.ps[:, 2 + tt, 0:D], weight, xt, ALU.mult, ALU.add
                                                       ).then_inc(y_added.sem, 1)

            experts(dve, expert)
    w_in[0].spent(16 * loads * (n_exp - n_exp // 2))
    w_in[1].spent(16 * loads * (n_exp // 2))
    used.spent(n_exp)
    h_done.spent(FC * NG * n_exp)
    h_put.spent(FC * NG * n_exp)
    y_done.spent(TPG * NG * n_exp)
    y_added.spent(TPG * NG * n_exp)
    if first:
        passing.spent(NT)


def grouped_router(c, cw):
    nc, ctx = c.nc, ExitStack()
    loaded, made, copied, step_s = c.sig("weights_in"), c.sig("logits"), c.sig("logitsT_put"), c.sig("dve_step")
    scored = c.sig("exped")
    n, per = E3, E3 // NGRP3
    with ctx:
        def sb(name, shape):
            return c.sb("gr_" + name, shape, F32, ctx)

        wr, lgT = sb("wr", [P, KD, n]), sb("lgT", [P, T])
        tri4, tri16, bias = sb("tri4", [P, per, per]), sb("tri16", [P, n, n]), sb("bias", [P, 1, n])
        score, choice, hot = sb("score", [P, NT, n]), sb("choice", [P, NT, n]), sb("hot", [P, NT, n])
        gt, eq, rank = sb("gt", [P, NT, n, n]), sb("eq", [P, NT, n, n]), sb("rank", [P, NT, n])
        gs, grank, s = sb("gs", [P, NT, NGRP3]), sb("grank", [P, NT, NGRP3]), sb("s", [P, NT])
        block = ctx.enter_context(nc.Block(no_gpsimd_drain=True))
        count = [0]

        @block.sync
        def _(sp):
            sp.dma_start(wr[:], c.dram["L3f_wr"]).then_inc(loaded.sem, 16)
            sp.dma_start(tri4[:], c.dram["tri4"].partition_broadcast(P)).then_inc(loaded.sem, 16)
            sp.dma_start(tri16[:], c.dram["tri16"].partition_broadcast(P)).then_inc(loaded.sem, 16)
            sp.dma_start(bias[:], c.dram["L3f_bias"].partition_broadcast(P)).then_inc(loaded.sem, 16)

        @block.tensor
        def _(pe):
            pe.wait_ge(*loaded(64))
            logits_on_pe(c, pe, wr, lgT, n, made, copied)

        @block.scalar
        def _(act):
            for g in range(NG):
                act.wait_ge(*made(g + 1))
                nc.scalar.copy(lgT[0:n, g * GROUP:(g + 1) * GROUP], c.ps[0:n, g % 2, :]).then_inc(copied.sem, 1)
            act.wait_ge(*made(NG + 1))
            nc.scalar.activation(score[:].rearrange("p t e -> p (t e)"), c.ps[:, 2, 0:NT * n], ACT.Sigmoid
                                 ).then_inc(scored.sem, 1)

        @block.vector
        def _(dve):
            step = Steps(step_s)
            dve.wait_ge(*scored(1))
            dve.wait_ge(*loaded(64))
            step.link(dve, nc.vector.tensor_tensor(choice[:], score[:], bias[:].to_broadcast([P, NT, n]), ALU.add))
            by_group = choice[:].rearrange("p t (g e) -> p (t g) e", g=NGRP3)
            small = [P, NT * NGRP3, per, per]
            gt4 = gt[:].rearrange("p t a b -> p (t a b)")[:, 0:NT * n * per].rearrange(
                "p (g a b) -> p g a b", a=per, b=per)
            eq4 = eq[:].rearrange("p t a b -> p (t a b)")[:, 0:NT * n * per].rearrange(
                "p (g a b) -> p g a b", a=per, b=per)
            rank_rule(nc, dve, step, by_group, gt4, eq4, tri4[:], rank[:].rearrange("p t (g e) -> p (t g) e", g=NGRP3))
            step.link(dve, nc.vector.tensor_scalar(hot[:], rank[:], 2.0, None, ALU.is_lt))
            step.link(dve, nc.vector.tensor_tensor(hot[:], hot[:], choice[:], ALU.mult))
            step.link(dve, nc.vector.tensor_reduce(gs[:].rearrange("p t g -> p (t g)"),
                                                   hot[:].rearrange("p t (g e) -> p (t g) e", g=NGRP3), AX_X, ALU.add))
            gtg = gt[:].rearrange("p t a b -> p (t a b)")[:, 0:NT * per * per].rearrange(
                "p (t a b) -> p t a b", a=per, b=per)
            eqg = eq[:].rearrange("p t a b -> p (t a b)")[:, 0:NT * per * per].rearrange(
                "p (t a b) -> p t a b", a=per, b=per)
            rank_rule(nc, dve, step, gs[:], gtg, eqg, tri4[:], grank[:])
            step.link(dve, nc.vector.tensor_scalar(gs[:], grank[:], float(TOPG3), None, ALU.is_lt))
            step.link(dve, nc.vector.tensor_scalar(grank[:], gs[:], -1.0, 1e9, ALU.add, ALU.mult))
            step.link(dve, nc.vector.tensor_tensor(
                by_group, by_group,
                gs[:].rearrange("p t g -> p (t g)").unsqueeze(2).to_broadcast([P, NT * NGRP3, per]), ALU.mult))
            step.link(dve, nc.vector.tensor_tensor(
                by_group, by_group,
                grank[:].rearrange("p t g -> p (t g)").unsqueeze(2).to_broadcast([P, NT * NGRP3, per]), ALU.add))
            rank_rule(nc, dve, step, choice[:], gt[:], eq[:], tri16[:], rank[:])
            step.link(dve, nc.vector.tensor_scalar(hot[:], rank[:], float(TOPK3), None, ALU.is_lt))
            step.link(dve, nc.vector.tensor_tensor(hot[:], hot[:], score[:], ALU.mult))
            step.link(dve, nc.vector.tensor_reduce(s[:], hot[:], AX_X, ALU.add))
            step.link(dve, nc.vector.tensor_scalar(s[:], s[:], 1e-20, None, ALU.add))
            step.link(dve, nc.vector.reciprocal(s[:], s[:]))
            step.link(dve, nc.vector.tensor_scalar(s[:], s[:], SCALED3, None, ALU.mult))
            step.link(dve, nc.vector.tensor_tensor(cw[:], hot[:], s[:].unsqueeze(2).to_broadcast([P, NT, n]),
                                                   ALU.mult))
            count[0] = step.n
    step_s.spent(count[0])
    loaded.spent(64)
    made.spent(NG + 1)
    copied.spent(NG)
    scored.spent(1)


def grouped_experts(c):
    nc, ctx = c.nc, ExitStack()
    w_in = [c.sig("even_expert_in"), c.sig("odd_expert_in")]
    h_done, gated, h_put = c.sig("h_done"), c.sig("gated"), c.sig("h_put")
    y_done, y_added = c.sig("y_done"), c.sig("y_added")
    WE = 2 * KD * I3 + D
    with ctx:
        cw = c.sb("cw", [P, NT, E3], ctx=ctx)
        grouped_router(c, cw)
        w = c.sb("ge_w", [P, 2, WE], ctx=ctx)
        sg = c.sb("ge_gate", [P, 2, GROUP], ctx=ctx)
        h = c.sb("ge_h", [P, 2, GROUP], ctx=ctx)
        block = ctx.enter_context(nc.Block(no_gpsimd_drain=True))

        @block.sync
        def _(sp):
            for e in range(2):
                sp.dma_start(w[:, e], c.dram["L3f_w"][e]).then_inc(w_in[e].sem, 16)
            with sp.Fori(0, E3 // 2 - 1) as i:
                for par in range(2):
                    sp.wait_ge(*y_done((2 * i + par + 1) * NG * TPG))
                    sp.dma_start(w[:, par], c.dram["L3f_w"][ds(2 * i + par + 2, 1)].squeeze(0)
                                 ).then_inc(w_in[par].sem, 16)

        @block.tensor
        def _(pe):
            with pe.Fori(0, E3 // 2) as i:
                for par in range(2):
                    n0 = (2 * i + par) * NG
                    pe.wait_ge(*w_in[par](16 * i + 16))
                    gate = w[:, par, 0:KD * I3].rearrange("p (k m) -> p k m", k=KD)
                    up = w[:, par, KD * I3:2 * KD * I3].rearrange("p (k m) -> p k m", k=KD)

                    def rise(g):
                        pe.wait_ge(*h_put(n0 + max(g - 1, 0)))
                        for n, m in enumerate((gate, up)):
                            for k in range(KD):
                                ins = nc.tensor.matmul(c.ps[:, 2 * (g % 2) + n, :], m[:, k],
                                                       c.xT[:, k, g * GROUP:(g + 1) * GROUP],
                                                       start=(k == 0), stop=(k == KD - 1))
                        ins.then_inc(h_done.sem, 1)

                    def fall(g):
                        pe.wait_ge(*h_put(n0 + g + 1))
                        pe.wait_ge(*y_added((n0 + g) * TPG))
                        for tt in range(TPG):
                            nc.tensor.matmul(c.ps[:, 4 + tt, 0:D], h[:, g % 2, tt * P:(tt + 1) * P],
                                             w[:, par, 2 * KD * I3:WE], start=True, stop=True
                                             ).then_inc(y_done.sem, 1)

                    rise(0)
                    for g in range(NG):
                        if g + 1 < NG:
                            rise(g + 1)
                        fall(g)

        @block.scalar
        def _(act):
            with act.Fori(0, E3 // 2) as i:
                for par in range(2):
                    for g in range(NG):
                        act.wait_ge(*h_done((2 * i + par) * NG + g + 1))
                        nc.scalar.activation(sg[:, g % 2], c.ps[:, 2 * (g % 2), :], ACT.Silu).then_inc(gated.sem, 1)

        @block.vector
        def _(dve):
            with dve.Fori(0, E3 // 2) as i:
                for par in range(2):
                    e = 2 * i + par

                    def multiply(g):
                        n = e * NG + g
                        dve.wait_ge(*gated(n + 1))
                        nc.vector.tensor_tensor(h[:, g % 2], sg[:, g % 2], c.ps[:, 2 * (g % 2) + 1, :], ALU.mult
                                                ).then_inc(h_put.sem, 1)

                    def add(g):
                        n = e * NG + g
                        dve.wait_ge(*y_added(n * TPG))
                        for tt in range(TPG):
                            dve.wait_ge(*y_done(TPG * n + tt + 1))
                            t = g * TPG + tt
                            weight = cw[:, t, ds(e, 1)]
                            nc.vector.scalar_tensor_tensor(c.x[:, t], c.ps[:, 4 + tt, 0:D], weight, c.x[:, t],
                                                           ALU.mult, ALU.add).then_inc(y_added.sem, 1)

                    multiply(0)
                    for g in range(NG):
                        if g + 1 < NG:
                            multiply(g + 1)
                        add(g)
    for sgn in w_in:
        sgn.spent(16 * E3 // 2)
    h_done.spent(NG * E3)
    gated.spent(NG * E3)
    h_put.spent(NG * E3)
    y_done.spent(TPG * NG * E3)
    y_added.spent(TPG * NG * E3)


def similarity_phase(c):
    nc, ctx = c.nc, ExitStack()
    loaded, staged, projected, put = c.sig("weights_in"), c.sig("ctx_staged"), c.sig("qk_proj"), c.sig("qk_put")
    squared, summed, rooted = c.sig("squared"), c.sig("sq_summed"), c.sig("rooted")
    dotted, added, step_s = c.sig("y_done"), c.sig("y_added"), c.sig("dve_step")
    with ctx:
        def sb(name, shape):
            return c.sb("si_" + name, shape, F32, ctx)

        w, b = sb("w", [P, 2, KD, HSIM]), sb("b", [P, 2])
        vt, sq = sb("vt", [P, 2, 2, S]), sb("sq", [P, 2, 2 * S])
        nrm = sb("nrm", [1, 2, 2 * S])
        r = sb("r", [P, 2, 2 * S])
        block = ctx.enter_context(nc.Block(no_gpsimd_drain=True))
        H = B // 2

        @block.sync
        def _(sp):
            sp.dma_start(w[:], c.dram["L1x_w"]).then_inc(loaded.sem, 16)
            sp.dma_start(b[:], c.dram["L1x_b"]).then_inc(loaded.sem, 16)

        @block.tensor
        def _(pe):
            pe.wait_ge(*loaded(32))
            with pe.Fori(0, H) as i:
                for s in range(2):
                    bank = c.ps[:, s, :]
                    pe.wait_ge(*squared(2 * i))
                    cols = ds((2 * i + s) * S, S)
                    for k in range(KD):
                        nc.tensor.matmul(bank[:, 0:S], w[:, 0, k], c.xT[:, k, cols], start=(k == 0),
                                         stop=(k == KD - 1))
                    for k, rows in enumerate(KC):
                        ins = nc.tensor.matmul(bank[:, S:2 * S], w[0:rows, 1, k], c.ctxT[0:rows, k, cols],
                                               start=(k == 0), stop=(k == 1))
                    ins.then_inc(projected.sem, 1)
                for s in range(2):
                    pe.wait_ge(*squared(2 * i + s + 1))
                    pe.wait_ge(*rooted(2 * i))
                    nc.tensor.matmul(c.ps[0:1, 2 + s, :], c.ones[:, 0:1], sq[:, s], start=True, stop=True
                                     ).then_inc(summed.sem, 1)
                for s in range(2):
                    pe.wait_ge(*added(2 * i))
                    for qt in range(2):
                        nc.tensor.matmul(c.ps[:, 6 + s, qt * S:(qt + 1) * S], vt[:, s, 0, qt * P:(qt + 1) * P],
                                         vt[:, s, 1], start=True, stop=True)
                    pe.wait_ge(*rooted(2 * i + s + 1))
                    for qt in range(2):
                        ins = nc.tensor.matmul(c.ps[:, 4 + s, qt * S:(qt + 1) * S], nrm[:, s, qt * P:(qt + 1) * P],
                                               nrm[:, s, S:2 * S], start=True, stop=True)
                    ins.then_inc(dotted.sem, 1)

        @block.scalar
        def _(act):
            act.wait_ge(*loaded(32))
            with act.Fori(0, H) as i:
                for s in range(2):
                    act.wait_ge(*projected(2 * i + s + 1))
                    for side in range(2):
                        part = c.ps[:, s, side * S:(side + 1) * S]
                        nc.scalar.activation(vt[:, s, side], part, ACT.Identity, bias=b[:, side:side + 1])
                        ins = nc.scalar.activation(sq[:, s, side * S:(side + 1) * S], part, ACT.Square,
                                                   bias=b[:, side:side + 1])
                    ins.then_inc(squared.sem, 1)
                for s in range(2):
                    act.wait_ge(*summed(2 * i + s + 1))
                    nc.scalar.activation(nrm[:, s], c.ps[0:1, 2 + s, :], ACT.Sqrt).then_inc(rooted.sem, 1)

        @block.vector
        def _(dve):
            with dve.Fori(0, H) as i:
                for s in range(2):
                    step = Steps(step_s, 2 * i + s, 3)
                    dve.wait_ge(*dotted(2 * i + s + 1))
                    dve.wait_ge(*added(2 * i))
                    step.link(dve, nc.vector.tensor_scalar(r[:, s], c.ps[:, 4 + s, :], 1e-8, None, ALU.max))
                    step.link(dve, nc.vector.reciprocal(r[:, s], r[:, s]))
                    step.link(dve, nc.vector.tensor_tensor(r[:, s], r[:, s], c.ps[:, 6 + s, :], ALU.mult))
                    xt = c.x[:, ds(2 * (2 * i + s), 2)].rearrange("p t d -> p (t d)")
                    nc.vector.tensor_tensor(xt, xt, r[:, s], ALU.add).then_inc(added.sem, 1)
    loaded.spent(32)
    step_s.spent(3 * B)
    for sgn in (projected, squared, summed, rooted, dotted, added):
        sgn.spent(B)



def local_attention(c, d, z):
    nc, ctx, dram = c.nc, ExitStack(), c.dram
    names = ("weights_in", "dve_step", "z_staged", "h_turned", "h_put", "qkv_done", "squared", "v_put", "sq_summed",
             "rooted", "lengthed", "q_rotated", "k_rotated", "qk_turned", "qk_put", "scored", "max_put", "max_negated",
             "exped", "p_turned", "p_put", "weighed", "inverted", "o_normed", "o_turned", "o_put", "y_done",
             "y_added", "pool_step", "dve_pair")
    (loaded, step_s, z_staged, h_turned, h_put, qkv_done, squared, v_put, summed, rooted, lengthed, q_rot, k_rot,
     qk_turned, qk_put, scored, topped, negated, exped, p_turned, p_put, weighed, inverted, o_normed, o_turned,
     o_put, y_done, added, pool_s, pair_s) = (c.sig(n) for n in names)
    HC = INNER // P
    HALF = LD // 2
    with ctx:
        def sb(name, shape):
            return c.sb("la_" + name, shape, F32, ctx)

        wqkv, wo = sb("wqkv", [P, KD, 3 * INNER]), sb("wo", [P, HC, D])
        rope, gain = sb("rope", [P, 2, 2, 2, LD]), sb("gain", [P, 2, LD])
        tab = sb("tab", [P, 2, 2, 2, LD])
        mask = sb("mask", [P, 3 * WIN])
        maskb, identb = (c.sb("la_" + n, [P, m], BF16, ctx) for n, m in (("maskb", 3 * WIN), ("identb", P)))
        zst, hs = sb("zst", [P, 2, D]), sb("hs", [P, KD, S])
        sq, ss = sb("sq", [P, 2, 2 * INNER]), sb("ss", [P, 2, 2 * LH])
        root, rn = sb("root", [P, 2, 2 * LH]), sb("rn", [P, 2, 2 * LH])
        t1, t2 = sb("t1", [P, 2, 2, INNER]), sb("t2", [P, 2, 2, INNER])
        qT, kT, v = sb("qT", [P, HC, S]), sb("kT", [P, HC, S]), sb("v", [P, 2, INNER])
        pr, pT = sb("p", [P, 2, 3 * WIN]), sb("pT", [P, 2, 3 * WIN])
        mx, nm, rs = sb("mx", [P, LH, 2]), sb("nm", [P, LH, 2]), sb("rs", [P, LH, 2])
        rec, on, ot = sb("rec", [P, LH, 2]), sb("on", [P, 2, INNER]), sb("ot", [P, 2, HC, P])
        block = ctx.enter_context(nc.Block(no_gpsimd_drain=True))
        SPLIT = [(0, WIN), (WIN, 3 * WIN)]
        SETUP = 9

        @block.sync
        def _(sp):
            for dst, name in ((wqkv, "wqkv"), (wo, "wo")):
                sp.dma_start(dst[:], dram["L1f_" + name][d]).then_inc(loaded.sem, 16)
            sp.dma_start(gain[:], dram["L1f_gain"][d].partition_broadcast(P)).then_inc(loaded.sem, 16)
            sp.dma_start(rope[:], dram["rope"]).then_inc(loaded.sem, 16)
            sp.dma_start(mask[:], dram["window"]).then_inc(loaded.sem, 16)

        def rotate(engine, eng, step, tt, side):
            a = t1[:, tt, side].rearrange("p (h d) -> p h d", h=LH)
            b = t2[:, tt, side].rearrange("p (h d) -> p h d", h=LH)
            for lo, hi in ((0, HALF), (HALF, LD)):
                src = a[:, :, HALF - lo:HALF - lo + HALF]
                step.mark(engine.tensor_tensor(
                    b[:, :, lo:hi], src, tab[:, side, 1, tt, lo:hi].unsqueeze(1).to_broadcast([P, LH, HALF]), ALU.mult))
            step.settle(eng)
            step.link(eng, engine.tensor_tensor(
                a, a, tab[:, side, 0, tt].unsqueeze(1).to_broadcast([P, LH, LD]), ALU.mult))
            return engine.tensor_tensor(a, a, b, ALU.add)

        @block.gpsimd
        def _(pool):
            nc.gpsimd.memset(hs[:, 1, 0:1], 0.0).then_inc(pool_s.sem, 1)
            with pool.Fori(0, B) as i:
                pool.wait_ge(*h_turned(i))
                nc.gpsimd.tensor_copy(zst[:], z[:, ds(2 * i, 2)]).then_inc(z_staged.sem, 1)
                for tt in range(2):
                    pool.wait_ge(*summed(2 * i + tt + 1))
                    nc.gpsimd.tensor_tensor(root[:, tt], ss[:, tt], c.half[:, 0, 0:2 * LH], ALU.pow
                                            ).then_inc(rooted.sem, 1)
                for tt in range(2):
                    step = Steps(pool_s, i, 6)
                    step.n = 1 + 3 * tt
                    pool.wait_ge(*lengthed(2 * i + tt + 1))
                    rotate(nc.gpsimd, pool, step, tt, 1).then_inc(k_rot.sem, 1)
            pool.wait_ge(*k_rot(2 * B))

        @block.tensor
        def _(pe):
            pe.wait_ge(*loaded(80))
            pe.wait_ge(*pair_s(SETUP - 1))
            with pe.Fori(0, B) as i:
                pe.wait_ge(*p_put(LH * i))
                pe.wait_ge(*z_staged(i + 1))
                for k in range(KD):
                    for tt in range(2):
                        ins = nc.tensor.transpose(c.ps[:, 0, k * S + tt * P:k * S + (tt + 1) * P],
                                                  zst[:, tt, k * P:(k + 1) * P], c.ident[:])
                ins.then_inc(h_turned.sem, 1)
                pe.wait_ge(*h_put(i + 1))
                pe.wait_ge(*added(2 * i))
                pe.wait_ge(*o_put(2 * i))
                pe.wait_ge(*o_normed(2 * i))
                for tt in range(2):
                    for n in range(3):
                        for k in range(KD):
                            ins = nc.tensor.matmul(c.ps[:, 1 + 3 * tt + n, :], hs[:, k, tt * P:(tt + 1) * P],
                                                   wqkv[:, k, n * INNER:(n + 1) * INNER],
                                                   start=(k == 0), stop=(k == KD - 1))
                    ins.then_inc(qkv_done.sem, 1)
                for tt in range(2):
                    pe.wait_ge(*q_rot(2 * i + tt + 1))
                    pe.wait_ge(*k_rot(2 * i + tt + 1))
                    for side in range(2):
                        bank = c.ps[:, ((7, 0), (1, 2))[tt][side], :]
                        for hc in range(HC):
                            ins = nc.tensor.transpose(bank[:, hc * P:(hc + 1) * P],
                                                      t1[:, tt, side, hc * P:(hc + 1) * P], c.ident[:])
                        ins.then_inc(qk_turned.sem, 1)

                def score(h):
                    r, hc = LD * (h % 2), h // 2
                    if h >= 2:
                        pe.wait_ge(*exped(LH * i + h - 1))
                    bank = c.ps[:, 3 + h % 2, :]
                    nc.tensor.matmul(bank[:, 0:3 * WIN], identb[:], maskb[:], start=True, stop=False)
                    nc.tensor.matmul(bank[:, 0:WIN], qT[r:r + LD, hc, 0:WIN], kT[r:r + LD, hc, 0:WIN],
                                     start=False, stop=False)
                    nc.tensor.matmul(bank[:, WIN:3 * WIN], qT[r:r + LD, hc, WIN:S], kT[r:r + LD, hc, :],
                                     start=False, stop=True).then_inc(scored.sem, 1)

                def turn(h):
                    pe.wait_ge(*exped(LH * i + h + 1))
                    if h >= 2:
                        pe.wait_ge(*p_put(LH * i + h - 1))
                    for n in range(3):
                        ins = nc.tensor.transpose(c.ps[:, 7 * (1 - h % 2), n * P:(n + 1) * P],
                                                  pr[:, h % 2, n * P:(n + 1) * P], c.ident[:])
                    ins.then_inc(p_turned.sem, 1)

                def weigh(h):
                    pe.wait_ge(*p_put(LH * i + h + 1))
                    cols = slice(h * LD, (h + 1) * LD)
                    nc.tensor.matmul(c.ps[:, 5, cols], pT[:, h % 2, 0:P], v[:, 0, cols], start=True, stop=True)
                    for kt in range(2):
                        ins = nc.tensor.matmul(c.ps[:, 6, cols], pT[:, h % 2, (1 + kt) * P:(2 + kt) * P],
                                               v[:, kt, cols], start=(kt == 0), stop=(kt == 1))
                    ins.then_inc(weighed.sem, 1)

                pe.wait_ge(*qk_put(4 * i + 4))
                pe.wait_ge(*v_put(2 * i + 2))
                score(0)
                score(1)
                for h in range(LH):
                    turn(h)
                    if h + 2 < LH:
                        score(h + 2)
                    if h >= 1:
                        weigh(h - 1)
                weigh(LH - 1)
                for qt in range(2):
                    pe.wait_ge(*o_normed(2 * i + qt + 1))
                    for hc in range(HC):
                        ins = nc.tensor.transpose(c.ps[:, 3 + qt, hc * P:(hc + 1) * P],
                                                  on[:, qt, hc * P:(hc + 1) * P], c.ident[:])
                    ins.then_inc(o_turned.sem, 1)
                for qt in range(2):
                    pe.wait_ge(*o_put(2 * i + qt + 1))
                    for hc in range(HC):
                        ins = nc.tensor.matmul(c.ps[:, 1 + qt, 0:D], ot[:, qt, hc], wo[:, hc],
                                               start=(hc == 0), stop=(hc == HC - 1))
                    ins.then_inc(y_done.sem, 1)

        @block.scalar
        def _(act):
            with act.Fori(0, B) as i:
                act.wait_ge(*h_turned(i + 1))
                nc.scalar.copy(hs[:, 0, :], c.ps[:, 0, 0:S])
                nc.scalar.copy(hs[:, 1, 1:S], c.ps[:, 0, S:2 * S - 1]).then_inc(h_put.sem, 1)
                for tt in range(2):
                    act.wait_ge(*qkv_done(2 * i + tt + 1))
                    nc.scalar.activation(sq[:, tt], c.ps[:, 1 + 3 * tt:3 + 3 * tt, :].rearrange("p a b -> p (a b)"),
                                         ACT.Square).then_inc(squared.sem, 1)
                    nc.scalar.copy(v[:, tt], c.ps[:, 3 + 3 * tt, :]).then_inc(v_put.sem, 1)
                for tt in range(2):
                    for side, dst in ((0, qT), (1, kT)):
                        act.wait_ge(*qk_turned(4 * i + 2 * tt + side + 1))
                        nc.scalar.copy(dst[:, :, tt * P:(tt + 1) * P],
                                       c.ps[:, ((7, 0), (1, 2))[tt][side], :].rearrange("p (h t) -> p h t", h=HC)
                                       ).then_inc(qk_put.sem, 1)
                for h in range(LH + 1):
                    if h < LH:
                        act.wait_ge(*negated(LH * i + h + 1))
                        if h >= 2:
                            act.wait_ge(*p_turned(LH * i + h - 1))
                        for n, (lo, hi) in enumerate(SPLIT):
                            ins = nc.scalar.activation(pr[:, h % 2, lo:hi], c.ps[:, 3 + h % 2, lo:hi], ACT.Exp,
                                                       bias=nm[:, h, n:n + 1], accum_out=rs[:, h, n:n + 1])
                        ins.then_inc(exped.sem, 1)
                    if h >= 1:
                        g = h - 1
                        act.wait_ge(*p_turned(LH * i + g + 1))
                        if g >= 2:
                            act.wait_ge(*weighed(LH * i + g - 1))
                        nc.scalar.copy(pT[:, g % 2], c.ps[:, 7 * (1 - g % 2), 0:3 * WIN]).then_inc(p_put.sem, 1)
                for qt in range(2):
                    act.wait_ge(*o_turned(2 * i + qt + 1))
                    nc.scalar.copy(ot[:, qt].rearrange("p k t -> p (k t)"), c.ps[:, 3 + qt, :]).then_inc(o_put.sem, 1)

        @block.vector
        def _(dve):
            dve.wait_ge(*loaded(80))
            step = Steps(pair_s)
            for side in range(2):
                g = gain[:, side]
                step.mark(nc.vector.tensor_tensor(tab[:, side, 0], rope[:, side, 0],
                                                  g.unsqueeze(1).to_broadcast([P, 2, LD]), ALU.mult))
                for lo, hi in ((0, HALF), (HALF, LD)):
                    step.mark(nc.vector.tensor_tensor(
                        tab[:, side, 1, :, lo:hi], rope[:, side, 1, :, lo:hi],
                        g[:, HALF - lo:HALF - lo + HALF].unsqueeze(1).to_broadcast([P, 2, HALF]), ALU.mult))
            step.mark(nc.vector.tensor_copy(maskb[:], mask[:]))
            step.mark(nc.vector.tensor_copy(identb[:], c.ident[:]))
            step.settle(dve)
            assert step.n == SETUP - 1
            with dve.Fori(0, B) as i:
                step = Steps(step_s, i, 5)
                for tt in range(2):
                    dve.wait_ge(*squared(2 * i + tt + 1))
                    nc.vector.tensor_reduce(ss[:, tt], sq[:, tt].rearrange("p (h d) -> p h d", d=LD), AX_X, ALU.add
                                            ).then_inc(summed.sem, 1)
                for tt in range(2):
                    dve.wait_ge(*rooted(2 * i + tt + 1))
                    step.link(dve, nc.vector.tensor_scalar(rn[:, tt], root[:, tt], 1e-12, None, ALU.max))
                    step.link(dve, nc.vector.reciprocal(rn[:, tt], rn[:, tt]))
                    nc.vector.tensor_tensor(
                        t1[:, tt].rearrange("p a (h d) -> p (a h) d", d=LD),
                        c.ps[:, 1 + 3 * tt:3 + 3 * tt, :].rearrange("p a (h d) -> p (a h) d", d=LD),
                        rn[:, tt].unsqueeze(2).to_broadcast([P, 2 * LH, LD]), ALU.mult).then_inc(lengthed.sem, 1)
                for tt in range(2):
                    dve.wait_ge(*lengthed(2 * i + tt + 1))
                    rot = Steps(pair_s, i, 6)
                    rot.n = SETUP - 1 + 3 * tt
                    rotate(nc.vector, dve, rot, tt, 0).then_inc(q_rot.sem, 1)
                for h in range(LH):
                    dve.wait_ge(*scored(LH * i + h + 1))
                    for n, (lo, hi) in enumerate(SPLIT):
                        ins = nc.vector.tensor_reduce(mx[:, h, n:n + 1], c.ps[:, 3 + h % 2, lo:hi], AX_X, ALU.max)
                    ins.then_inc(topped.sem, 1)
                    dve.wait_ge(*topped(LH * i + h + 1))
                    nc.vector.tensor_scalar(nm[:, h], mx[:, h], -1.0, None, ALU.mult).then_inc(negated.sem, 1)
                dve.wait_ge(*exped(LH * i + LH))
                step.link(dve, nc.vector.reciprocal(rec[:], rs[:]))
                dve.wait_ge(*weighed(LH * i + LH))
                for qt in range(2):
                    nc.vector.tensor_tensor(on[:, qt].rearrange("p (h d) -> p h d", h=LH),
                                            c.ps[:, 5 + qt, :].rearrange("p (h d) -> p h d", h=LH),
                                            rec[:, :, qt].unsqueeze(2).to_broadcast([P, LH, LD]), ALU.mult
                                            ).then_inc(o_normed.sem, 1)
                for qt in range(2):
                    dve.wait_ge(*y_done(2 * i + qt + 1))
                    zt = z[:, ds(2 * i + qt, 1)].squeeze(1)
                    nc.vector.tensor_tensor(zt, zt, c.ps[:, 1 + qt, 0:D], ALU.add).then_inc(added.sem, 1)
    loaded.spent(80)
    pool_s.spent(1 + 6 * B)
    pair_s.spent(SETUP - 1 + 6 * B)
    step_s.spent(5 * B)
    for sgn, n in ((z_staged, 1), (h_turned, 1), (h_put, 1), (qkv_done, 2), (squared, 2), (v_put, 2), (summed, 2),
                   (rooted, 2), (lengthed, 2), (q_rot, 2), (k_rot, 2), (qk_turned, 4), (qk_put, 4), (scored, LH),
                   (topped, LH), (negated, LH), (exped, LH), (p_turned, LH), (p_put, LH), (weighed, LH),
                   (o_normed, 2), (o_turned, 2), (o_put, 2), (y_done, 2), (added, 2)):
        sgn.spent(B * n)


def local_ff(c, d, z, last):
    nc, ctx, dram = c.nc, ExitStack(), c.dram
    loaded, moved, zeroed = c.sig("weights_in"), c.sig("shifted_in"), c.sig("pool_step")
    h_done, gated, h_put = c.sig("h_done"), c.sig("gated"), c.sig("h_put")
    y_done, added, ended = c.sig("y_done"), c.sig("y_added"), c.sig("dve_step")
    with ctx:
        def sb(name, shape):
            return c.sb("lf_" + name, shape, F32, ctx)

        w1, w2 = sb("w1", [P, KD, 2 * HPAD]), sb("w2", [P, HC_FF, D])
        b1, b2, affine = sb("b1", [P, 2, HC_FF]), sb("b2", [1, D]), sb("affine", [P, 2, KD])
        late = sb("late", [P, NT, D // 2])
        with nc.Block(no_gpsimd_drain=True) as block:
            @block.gpsimd
            def _(pool):
                nc.gpsimd.memset(late[0:1, :, :], 0.0).then_inc(zeroed.sem, 1)
                pool.wait_ge(*zeroed(1))

            @block.sync
            def _(sp):
                sp.dma_start(late[1:P], z[0:P - 1, :, D // 2:D]).then_inc(moved.sem, 16)
                sp.wait_ge(*zeroed(1))
                sp.dma_start(late[0:1].rearrange("p (b t) d -> p b t d", t=2)[:, :, 1],
                             z[P - 1:P].rearrange("p (b t) d -> p b t d", t=2)[:, :, 0, D // 2:D]
                             ).then_inc(moved.sem, 16)
                for dst, name in ((w1, "w1"), (w2, "w2"), (b1, "b1"), (b2, "b2"), (affine, "affine")):
                    sp.dma_start(dst[:], dram["L1f_" + name][d]).then_inc(loaded.sem, 16)
                sp.wait_ge(*moved(32))
                sp.wait_ge(*loaded(80))
        zeroed.spent(1)
        moved.spent(32)
        loaded.spent(80)
        norm_phase(c, [(z[:, :, 0:D // 2], 0), (late, D // 2)], affine=affine)
        gs = sb("gs", [P, 2, GROUP])
        h = sb("h", [P, HC_FF, GROUP])
        block = ctx.enter_context(nc.Block(no_gpsimd_drain=True))
        NH = HC_FF

        @block.tensor
        def _(pe):
            with pe.Fori(0, NG) as g:
                for f in range(NH):
                    pe.wait_ge(*h_put(NH * g + max(f - 1, 0)))
                    for side in range(2):
                        for k in range(KD):
                            ins = nc.tensor.matmul(c.ps[:, 2 * (f % 2) + side, :],
                                                   w1[:, k, side * HPAD + f * P:side * HPAD + (f + 1) * P],
                                                   c.xT[:, k, ds(g * GROUP, GROUP)], start=(k == 0),
                                                   stop=(k == KD - 1))
                    ins.then_inc(h_done.sem, 1)
                pe.wait_ge(*h_put(NH * g + NH))
                pe.wait_ge(*added(TPG * g))
                for tt in range(TPG):
                    nc.tensor.matmul(c.ps[:, 4 + tt, 0:D], c.ones[0:1, :], b2[:], start=True, stop=False)
                    for f in range(NH):
                        ins = nc.tensor.matmul(c.ps[:, 4 + tt, 0:D], h[:, f, tt * P:(tt + 1) * P], w2[:, f],
                                               start=False, stop=(f == NH - 1))
                    ins.then_inc(y_done.sem, 1)

        @block.scalar
        def _(act):
            with act.Fori(0, NG) as g:
                for f in range(NH):
                    act.wait_ge(*h_done(NH * g + f + 1))
                    nc.scalar.activation(gs[:, f % 2], c.ps[:, 2 * (f % 2) + 1, :], ACT.Gelu,
                                         bias=b1[:, 1, f:f + 1]).then_inc(gated.sem, 1)

        @block.vector
        def _(dve):
            with dve.Fori(0, NG) as g:
                for f in range(NH):
                    dve.wait_ge(*gated(NH * g + f + 1))
                    nc.vector.scalar_tensor_tensor(h[:, f], c.ps[:, 2 * (f % 2), :], b1[:, 0, f:f + 1],
                                                   gs[:, f % 2], ALU.add, ALU.mult).then_inc(h_put.sem, 1)
                for tt in range(TPG):
                    dve.wait_ge(*y_done(TPG * g + tt + 1))
                    zt = z[:, ds(g * TPG + tt, 1)].squeeze(1)
                    nc.vector.tensor_tensor(zt, zt, c.ps[:, 4 + tt, 0:D], ALU.add).then_inc(added.sem, 1)
            if last:
                dve.wait_ge(*added(NT))
                nc.vector.tensor_tensor(c.x[:], c.x[:], z[:], ALU.add).then_inc(ended.sem, 1)
    h_done.spent(NH * NG)
    gated.spent(NH * NG)
    h_put.spent(NH * NG)
    y_done.spent(NT)
    added.spent(NT)
    if last:
        ended.spent(1)


def local_transformer(c):
    norm_phase(c, [(c.x, 0)], keep=True, transposed=False)
    for d in range(DEPTH):
        local_attention(c, d, c.xn)
        local_ff(c, d, c.xn, last=(d == DEPTH - 1))


def _more_layouts(a, o):
    f4 = np.float32
    for n, name in ((E, "tri8"), (4, "tri4"), (16, "tri16")):
        o[name] = np.tril(np.ones((n, n), f4), -1)[None]
    o["upto"] = np.triu(np.ones((P, P), f4))
    o["L0f_wr"] = _chunked(a["L0_ffn_Wr"])
    o["L2f_wr"] = _chunked(a["L2_ffn_Wg"])
    for tag, w1, w2 in (("L0f_", a["L0_ffn_W1"], a["L0_ffn_W2"]),
                        ("L2f_", np.concatenate([a["L2_ffn_W1"], a["L2_ffn_Ws1"][None]]),
                         np.concatenate([a["L2_ffn_W2"], a["L2_ffn_Ws2"][None]]))):
        o[tag + "w1"] = w1.reshape(-1, KD, P, FF).swapaxes(1, 2)
        o[tag + "w2"] = w2.reshape(-1, FC, P, D).swapaxes(1, 2)
    b1 = np.concatenate([a["L2_ffn_b1"], a["L2_ffn_bs1"][None]])
    b2 = np.concatenate([a["L2_ffn_b2"], a["L2_ffn_bs2"][None]])
    o["L2f_b1"] = b1.reshape(-1, FC, P).swapaxes(1, 2)
    o["L2f_b2"] = b2[:, None]
    o["L3f_wr"] = _chunked(a["L3_ffn_router_weight"].T)
    o["L3f_bias"] = a["L3_ffn_router_bias"].reshape(1, 1, E3)
    gu = [a["L3_ffn_w_" + n].swapaxes(1, 2).reshape(E3, KD, P, I3).swapaxes(1, 2).reshape(E3, P, KD * I3)
          for n in ("gate", "up")]
    o["L3f_w"] = np.concatenate(gu + [a["L3_ffn_w_down"].swapaxes(1, 2)], 2)
    o["L1x_w"] = np.stack([_chunked(a["L1_xattn_Wv"].T), _chunked(a["L1_xattn_Wt"].T)], 1)
    o["L1x_b"] = np.stack([a["L1_xattn_bv"], a["L1_xattn_bt"]], 1)
    w1 = np.zeros((DEPTH, D, 2, HPAD), f4)
    w1[..., 0:HID] = a["L1_ffn_w1"].reshape(DEPTH, D, 2, HID)
    for name, w in (("wqkv", a["L1_ffn_wqkv"]), ("wo", a["L1_ffn_wo"]), ("w1", w1.reshape(DEPTH, D, 2 * HPAD)),
                    ("w2", a["L1_ffn_w2"])):
        o["L1f_" + name] = np.stack([_chunked(m) for m in w])
    o["L1f_gain"] = np.stack([a["L1_ffn_q_scale"], a["L1_ffn_k_scale"]], 1)[:, None]
    b1 = a["L1_ffn_b1"].reshape(DEPTH, 2, HID)
    o["L1f_b1"] = np.stack([np.stack([_chunked(b[s]) for s in range(2)], 1) for b in b1])
    o["L1f_b2"] = a["L1_ffn_b2"][:, None]
    o["L1f_affine"] = np.stack([a["L1_ffn_ln_g"], a["L1_ffn_ln_b"]], 1).reshape(DEPTH, 2, KD, P).transpose(0, 3, 1, 2)
    o["rope"] = _rope()
    q, k = np.arange(P)[:, None], np.arange(P)[None]
    off = lambda seen: np.where(seen, 0.0, -HUGE).astype(f4)
    o["window"] = np.concatenate([off(k <= q), off(k >= q), off(k <= q)], 1)


def _rope():
    f4 = np.float32
    half = np.arange(0, LD, 2, dtype=f4)
    t = np.arange(S, dtype=f4)
    freqs = t[:, None] * (f4(1.0) / f4(10000.0) ** (half / f4(LD)))[None]
    base = (half + f4(0.4 * LD)) / f4(1.4 * LD)
    scale = base[None] ** ((t - S // 2) / f4(WIN // 2))[:, None]
    cos, sin = np.cos(freqs), np.sin(freqs)
    out = np.empty((2, 2, S, LD), f4)
    for side, s in ((0, scale * f4(QK_SCALE)), (1, f4(1.0) / scale)):
        out[side, 0] = np.concatenate([cos * s, cos * s], 1)
        out[side, 1] = np.concatenate([-sin * s, sin * s], 1)
    return out.reshape(2, 2, 2, P, LD).transpose(3, 0, 1, 2, 4)


STAGES = (0, 8)


def _program(nc, dram, stages):
    with ExitStack() as ctx:
        c = Core(nc, ctx, dram)
        load_phase(c)
        layers = [
            lambda: (norm_phase(c, [(c.x, 0)]), xattn_phase(c, "L0x_", masked=True)),
            lambda: (norm_phase(c, [(c.x, 0)], keep=True), expert_phases(c, "L0f_")),
            lambda: (norm_phase(c, [(c.x, 0)]), similarity_phase(c)),
            lambda: local_transformer(c),
            lambda: (norm_phase(c, [(c.x, 0)]), xattn_phase(c, "L2x_", biased=True, scale_in=True)),
            lambda: (norm_phase(c, [(c.x, 0)]), expert_phases(c, "L2f_")),
            lambda: (norm_phase(c, [(c.x, 0)]), xattn_phase(c, "L3x_", biased=True)),
            lambda: (norm_phase(c, [(c.x, 0)]), grouped_experts(c)),
        ]
        for n in range(*stages):
            layers[n]()
        store_phase(c)


def _chunked(a, rows=P):
    n = -(-a.shape[0] // rows)
    out = np.zeros((n * rows,) + a.shape[1:], a.dtype)
    out[:a.shape[0]] = a
    return out.reshape((n, rows) + a.shape[1:]).swapaxes(0, 1)


def _padded_heads(w):
    out = np.zeros(w.shape[:-1] + (HEADS, SLOT), w.dtype)
    out[..., 0:HD] = w.reshape(w.shape[:-1] + (HEADS, HD))
    return out.reshape(w.shape[:-1] + (HEADS * SLOT,))


def _layouts(inp):
    f4 = np.float32
    a = {k: np.asarray(v) for k, v in inp.items()}
    o = {}
    o["x"] = a["x"].reshape(NT, P, D).swapaxes(0, 1)
    o["ctxT"] = _chunked(a["ctx_768"].reshape(T, DC).T)
    o["mask"] = a["mask_BxS2_bf1"].reshape(1, T).view(np.uint8)
    o["ident"] = np.eye(P, dtype=f4)
    z = np.zeros(D, f4)
    for tag, src, bq, bk, bv, bo in (("L0x_", "L0_xattn_", z, z, z, z),
                                     ("L2x_", "L2_xattn_", a["L2_xattn_bq"], a["L2_xattn_bk"], a["L2_xattn_bv"],
                                      a["L2_xattn_bo"]),
                                     ("L3x_", "L3_xattn_", z, z, z, a["L3_xattn_bo"])):
        o[tag + "wq"] = _chunked(_padded_heads(a[src + "Wq"]))
        o[tag + "wk"] = _chunked(_padded_heads(a[src + "Wk"]))
        o[tag + "wv"] = _chunked(a[src + "Wv"])
        o[tag + "wo"] = _chunked(np.ascontiguousarray(_padded_heads(a[src + "Wo"].T).T))
        qb = _padded_heads(bq).reshape(HEADS, SLOT).copy()
        kb = _padded_heads(bk).reshape(HEADS, SLOT).copy()
        qb[:, MASK_ROW] = 1.0 if tag == "L0x_" else 0.0
        kb[:, MAX_ROW] = -1.0
        o[tag + "cols"] = np.stack([qb.reshape(CHUNKS, P).T, kb.reshape(CHUNKS, P).T], 1)
        if tag != "L0x_":
            o[tag + "rows"] = np.stack([bv, bo])[None]
    sel = np.zeros((1, HPC, SLOT), f4)
    sel[:, :, MASK_ROW] = 1.0
    o["rowsel"] = sel.reshape(1, P)
    pick, give = np.zeros((HPC, SLOT, CHUNKS, HEADS), f4), np.zeros((P, CHUNKS, HPC, SLOT), f4)
    for h in range(HEADS):
        pick[h % HPC, HD, h // HPC, h] = 1.0
        give[h, h // HPC, h % HPC] = 1.0
    o["pick"], o["give"] = pick.reshape(P, CHUNKS, HEADS), give.reshape(P, CHUNKS, P)
    o["L2x_scale"] = a["L2_xattn_scale"].reshape(1, 1)
    _more_layouts(a, o)
    return {k: np.ascontiguousarray(v) for k, v in o.items()}


def kernel(**inputs):
    import concourse.bacc as _bacc
    from concourse import mybir as _mybir
    from concourse.bass_utils import run_bass_kernel_spmd as _run

    nc = _bacc.Bacc("TRN2", target_bir_lowering=False, num_devices=1)
    arrays, dram = {}, {}
    for name, a in _layouts(inputs).items():
        arrays[f"in_{name}_dram"] = a
        dram[name] = nc.dram_tensor(f"in_{name}_dram", a.shape, _mybir.dt.from_np(a.dtype), kind="ExternalInput").ap()
    out = nc.dram_tensor("out_0_dram", (B, S, D), _mybir.dt.float32, kind="ExternalOutput").ap()
    dram["out"] = out.rearrange("b (t p) d -> p (b t) d", p=P)
    _program(nc, dram, STAGES)
    r = _run(nc, [arrays], core_ids=[0])
    return r.results[0]["out_0_dram"]
```

```python
from contextlib import ExitStack

import numpy as np

import concourse.bass as bass
from concourse import mybir

F32 = mybir.dt.float32
BF16 = mybir.dt.bfloat16
F32R = mybir.dt.float32r
U8, U32, I32 = mybir.dt.uint8, mybir.dt.uint32, mybir.dt.int32
ALU = mybir.AluOpType
ACT = mybir.ActivationFunctionType
AX_X = mybir.AxisListType.X
ds = bass.ds

P = 128
B, S, D = 8, 256, 256
T = B * S
NT = T // P
KD = D // P
DC = 192
KC = [P, DC - P]
GROUP = 512
NG = T // GROUP
TPG = GROUP // P
EPS = 1e-5
HUGE = 1e30

HEADS, HD, SLOT = 16, 16, 32
CHUNKS = HEADS * SLOT // P
HPC = P // SLOT
MASK_ROW, MAX_ROW = HD, HD + 1

E, FF = 8, 1024
FC = FF // P
CAP = int(1.25 * T / E)
SLOT_ROWS = -(-(2 * T // P + E - 1) // 8) * 8 * P
E3, I3, NGRP3, TOPG3, TOPK3, SCALED3 = 16, 128, 4, 2, 4, 2.5

HSIM = 128
DEPTH, LH, LD, WIN = 2, 8, 64, 128
INNER = LH * LD
HID = int(D * 4 * 2 / 3)
HC_FF = -(-HID // P)
HPAD = HC_FF * P
QK_SCALE = 8.0


SIGNALS = """dve_step dve_pair pool_step variance powered normed turned xT_put kept mask_step ctx_staged qk_proj
qk_put v_proj v_put scored max_put max_turned q_topped scored_T exped weighed summed o_normed o_turned o_put y_done
y_added logits logitsT_put shifted chosen counted h_done h_put gated expert_used squared sq_summed rooted z_staged
h_turned qkv_done lengthed q_rotated k_rotated qk_turned max_negated p_turned p_put inverted set_up
q_rest_put k_rest_put spread y_put""".split()
DMA_SIGNALS = """loaded weights_in even_expert_in odd_expert_in shifted_in stored
rows_sent scratch_zeroed even_part_in odd_part_in tile_stored quarter0_back quarter1_back quarter2_back
quarter3_back""".split()


class Signal:

    def __init__(self, sem, base):
        self.sem, self.base = sem, base

    def __call__(self, n):
        return self.sem, self.base + n

    def spent(self, n):
        self.base += n


class Steps:

    def __init__(self, count, i=0, per=0):
        self.count, self.at, self.n = count, i * per, 0

    def mark(self, ins):
        self.n += 1
        return ins.then_inc(self.count.sem, 1)

    def settle(self, eng):
        eng.wait_ge(*self.count(self.at + self.n))

    def link(self, eng, ins):
        self.mark(ins)
        self.settle(eng)


class Core:

    def __init__(self, nc, ctx, dram):
        self.nc, self.ctx, self.dram, self.counts, self.tensors = nc, ctx, dram, {}, 0
        for names, base in ((SIGNALS, 1), (DMA_SIGNALS, 0)):
            for name in names:
                self.counts[name] = Signal(ctx.enter_context(nc.semaphore(name)), base)
        self.x = self.sb("x_res", [P, NT, D])
        self.xT = self.sb("xn_T", [P, KD, T])
        self.xn = self.sb("xn_tok", [P, NT, D])
        self.ctxT = self.sb("ctx_T", [P, 2, T])
        self.ident = self.sb("ident", [P, P])
        self.ones = self.sb("ones", [P, P])
        self.half = self.sb("pow_half", [P, 2, P])
        self.zero = self.sb("zero", [P, 1, D])
        self.ps = ctx.enter_context(nc.psum_tensor("ps", [P, 8, 512], F32))

    def sb(self, name, shape, dt=F32, ctx=None):
        self.tensors += 1
        return (ctx or self.ctx).enter_context(self.nc.sbuf_tensor(f"{name}_{self.tensors}", shape, dt))

    def sig(self, name):
        return self.counts[name]


def load_phase(c):
    nc, loaded, set_up = c.nc, c.sig("loaded"), c.sig("set_up")
    with nc.Block() as block:
        @block.vector
        def _(dve):
            for name in SIGNALS:
                if name != "set_up":
                    dve.sem_inc(c.sig(name).sem, 1)

        @block.sync
        def _(sp):
            for name, dst in (("x", c.x), ("ctxT", c.ctxT), ("ident", c.ident)):
                sp.dma_start(dst[:], c.dram[name]).then_inc(loaded.sem, 16)
            sp.wait_ge(*set_up(4))
            rows = c.dram["rows_in"][0:SLOT_ROWS].rearrange("(a p) d -> p a d", p=P)
            sp.dma_start(rows, c.zero[:].to_broadcast([P, SLOT_ROWS // P, D])).then_inc(c.sig("scratch_zeroed").sem, 16)
            sp.wait_ge(*loaded(48))

        @block.gpsimd
        def _(pool):
            nc.gpsimd.memset(c.ones[:], 1.0).then_inc(set_up.sem, 1)
            nc.gpsimd.memset(c.half[:, 0], 0.5).then_inc(set_up.sem, 1)
            nc.gpsimd.memset(c.half[:, 1], -0.5).then_inc(set_up.sem, 1)
            nc.gpsimd.memset(c.zero[:], 0.0).then_inc(set_up.sem, 1)
            pool.sem_inc(set_up.sem, 1)
            pool.wait_ge(*set_up(4))
    loaded.spent(48)
    set_up.spent(4)


def store_phase(c):
    nc, stored = c.nc, c.sig("stored")
    with nc.Block() as block:
        @block.sync
        def _(sp):
            sp.dma_start(c.dram["out"], c.x[:]).then_inc(stored.sem, 16)
            sp.wait_ge(*stored(16))
    stored.spent(16)


def norm_phase(c, pieces, keep=False, transposed=True, affine=None):
    nc, ctx = c.nc, ExitStack()
    stepped, variance, powered = c.sig("dve_step"), c.sig("variance"), c.sig("powered")
    normed, turned, put, kept = c.sig("normed"), c.sig("turned"), c.sig("xT_put"), c.sig("kept")
    npc, count = len(pieces), [0]
    ns = 2 * npc
    with ctx:
        xs = c.sb("ln_row", [P, 2, D], ctx=ctx)
        stats = c.sb("ln_stats", [P, NT, ns, 3], ctx=ctx)
        mean, rstd, var = (c.sb("ln_" + n, [P, NT], ctx=ctx) for n in ("mean", "rstd", "var"))
        total, sq_in, sq_dev = (c.sb("ln_" + n, [P, NT], ctx=ctx) for n in ("total", "sq_in", "sq_dev"))
        dev = c.sb("ln_dev", [P, 2, NT, ns], ctx=ctx)
        block = ctx.enter_context(nc.Block(no_gpsimd_drain=True))

        @block.vector
        def _(dve):
            step = Steps(stepped)
            for t in range(NT):
                for n, (src, _) in enumerate(pieces):
                    ins = nc.vector.bn_stats(stats[:, t, 2 * n:2 * n + 2].rearrange("p a b -> p (a b)"), src[:, t])
            step.link(dve, ins)
            step.mark(nc.vector.tensor_reduce(sq_in[:], stats[:, :, :, 2], AX_X, ALU.add))
            step.link(dve, nc.vector.tensor_reduce(total[:], stats[:, :, :, 1], AX_X, ALU.add))
            step.link(dve, nc.vector.tensor_scalar(mean[:], total[:], 1.0 / ns, None, ALU.mult))
            step.link(dve, nc.vector.tensor_tensor(dev[:, 0], stats[:, :, :, 1],
                                                   mean[:].unsqueeze(2).to_broadcast([P, NT, ns]), ALU.subtract))
            step.link(dve, nc.vector.tensor_tensor(dev[:, 1], dev[:, 0], dev[:, 0], ALU.mult))
            step.link(dve, nc.vector.tensor_reduce(sq_dev[:], dev[:, 1], AX_X, ALU.add))
            step.link(dve, nc.vector.scalar_tensor_tensor(total[:], sq_dev[:], float(D // ns), sq_in[:], ALU.mult,
                                                          ALU.add))
            nc.vector.tensor_scalar(var[:], total[:], 1.0 / D, EPS, ALU.mult, ALU.add).then_inc(variance.sem, 1)
            count[0] = step.n
            dve.wait_ge(*powered(1))
            with dve.Fori(0, NT // 2) as i:
                for s in range(2):
                    t = 2 * i + s
                    if transposed:
                        dve.wait_ge(*turned(2 * i))
                    if keep:
                        dve.wait_ge(*kept(2 * i))
                    for src, at in pieces:
                        ins = nc.vector.tensor_scalar(xs[:, s, at:at + D // npc], src[:, ds(t, 1)].squeeze(1),
                                                      mean[:, ds(t, 1)], rstd[:, ds(t, 1)], ALU.subtract, ALU.mult)
                    ins.then_inc(normed.sem, 1)

        @block.gpsimd
        def _(pool):
            pool.wait_ge(*variance(1))
            nc.gpsimd.tensor_tensor(rstd[:], var[:], c.half[:, 1, 0:NT], ALU.pow).then_inc(powered.sem, 1)
            if keep:
                with pool.Fori(0, NT // 2) as i:
                    for s in range(2):
                        pool.wait_ge(*normed(2 * i + s + 1))
                        nc.gpsimd.tensor_copy(c.xn[:, ds(2 * i + s, 1)], xs[:, s]).then_inc(kept.sem, 1)
                pool.wait_ge(*kept(NT))

        if transposed:
            @block.tensor
            def _(pe):
                with pe.Fori(0, NT // 2) as i:
                    for s in range(2):
                        pe.wait_ge(*put(2 * i))
                        pe.wait_ge(*normed(2 * i + s + 1))
                        for k in range(KD):
                            ins = nc.tensor.transpose(c.ps[:, s, k * P:(k + 1) * P], xs[:, s, k * P:(k + 1) * P],
                                                      c.ident[:])
                        ins.then_inc(turned.sem, 1)

            @block.scalar
            def _(act):
                with act.Fori(0, NT // 2) as i:
                    for s in range(2):
                        cols = ds((2 * i + s) * P, P)
                        act.wait_ge(*turned(2 * i + s + 1))
                        if affine is None:
                            ins = nc.scalar.copy(c.xT[:, :, cols], c.ps[:, s, 0:D].rearrange("p (k t) -> p k t", k=KD))
                        else:
                            for k in range(KD):
                                ins = nc.scalar.activation(c.xT[:, k, cols], c.ps[:, s, k * P:(k + 1) * P],
                                                           ACT.Identity, scale=affine[:, 0, k:k + 1],
                                                           bias=affine[:, 1, k:k + 1])
                        ins.then_inc(put.sem, 1)
    stepped.spent(count[0])
    for sgn, n in ((variance, 1), (powered, 1), (normed, NT)):
        sgn.spent(n)
    if transposed:
        turned.spent(NT)
        put.spent(NT)
    if keep:
        kept.spent(NT)


def xattn_phase(c, tag, masked=False, scale=0.25, biased=False, scale_in=False):
    nc, ctx, dram = c.nc, ExitStack(), c.dram
    names = ("weights_in", "mask_step", "ctx_staged", "qk_proj", "qk_put", "v_proj", "v_put", "q_rest_put",
             "k_rest_put", "scored", "max_put", "max_turned", "q_topped", "scored_T", "exped", "weighed", "o_put",
             "summed", "inverted", "spread", "o_normed", "y_done", "y_added")
    (loaded, mstep, staged, qk_proj, qk_put, v_proj, v_put, q_rest, k_rest, scored, max_put, max_turned,
     topped, scored_T, exped, weighed, o_put, summed, inverted, spread, o_normed, y_done, y_added) = (
        c.sig(n) for n in names)
    PAIRS = HEADS // 2
    with ctx:
        def sb(name, shape, dt=F32):
            return c.sb("xa_" + name, shape, dt, ctx)

        wq, wk = sb("wq", [P, KD, HEADS * SLOT]), sb("wk", [P, 2, HEADS * SLOT])
        wv, wo = sb("wv", [P, 2, D]), sb("wo", [P, CHUNKS, D])
        cols = sb("cols", [P, 2, CHUNKS])
        pick, give = sb("pick", [P, CHUNKS, HEADS]), sb("give", [P, CHUNKS, P])
        rows = sb("rows", [1, 2, D]) if biased else None
        qk = sb("qk", [P, 2, 2, S])
        qh, ql = sb("qh", [P, CHUNKS, S], F32R), sb("ql", [P, CHUNKS, S], F32R)
        kh, kl = sb("kh", [P, HEADS, S], F32R), sb("kl", [P, HEADS, S], F32R)
        cst = sb("ctx", [P, 2, S])
        va = sb("v", [P, 2, HEADS, SLOT])
        mx = sb("mx", [P, 2, CHUNKS, HPC, SLOT], F32R)
        pt = sb("pT", [P, 2, HPC, 2, S])
        ot, rec = sb("ot", [P, CHUNKS, S]), sb("rec", [P, S])
        qscale = sb("qscale", [P, 1]) if scale_in else None
        qcols = sb("qcols", [P, CHUNKS]) if scale_in else None
        ctxk = c.ctxT
        if masked:
            mask8, mask = sb("mask8", [P, T], U8), sb("mask", [P, T])
            anyk, mbias, ctxk = sb("anyk", [P, B]), sb("mbias", [1, T]), sb("ctxk", [P, 2, T])
            rowsel = sb("rowsel", [1, P])
        n_loads = 7 + biased + scale_in + 2 * masked
        block = ctx.enter_context(nc.Block(no_gpsimd_drain=True))
        MSTEPS = 7 if masked else 2 if scale_in else 1

        @block.sync
        def _(sp):
            loads = [(wq, tag + "wq"), (wk, tag + "wk"), (wv, tag + "wv"), (wo, tag + "wo"), (cols, tag + "cols"),
                     (pick, "pick"), (give, "give")]
            loads += [(rows, tag + "rows")] if biased else []
            loads += [(rowsel, "rowsel")] if masked else []
            for dst, name in loads:
                sp.dma_start(dst[:], dram[name]).then_inc(loaded.sem, 16)
            if scale_in:
                sp.dma_start(qscale[:], dram[tag + "scale"].partition_broadcast(P)).then_inc(loaded.sem, 16)
            if masked:
                sp.dma_start(mask8[:], dram["mask"].partition_broadcast(P)).then_inc(loaded.sem, 16)

        @block.gpsimd
        def _(pool):
            nc.gpsimd.memset(kh[:].bitcast(F32), 0.0)
            nc.gpsimd.memset(kl[:].bitcast(F32), 0.0)
            nc.gpsimd.memset(rec[:], 0.0)
            nc.gpsimd.memset(mx[:].bitcast(F32), 0.0)
            nc.gpsimd.memset(va[:], 1.0).then_inc(mstep.sem, 1)
            pool.wait_ge(*mstep(1))
            with pool.Fori(0, B) as i:
                pool.wait_ge(*v_proj(2 * i))
                nc.gpsimd.tensor_copy(cst[:], c.ctxT[:, :, ds(i * S, S)]).then_inc(staged.sem, 1)
                for ch in range(CHUNKS):
                    pool.wait_ge(*qk_put(CHUNKS * i + ch + 1))
                    nc.gpsimd.tensor_tensor(ql[:, ch], qk[:, ch % 2, 0], qh[:, ch].bitcast(F32), ALU.subtract
                                            ).then_inc(q_rest.sem, 1)
            pool.wait_ge(*q_rest(CHUNKS * B))

        @block.tensor
        def _(pe):
            pe.wait_ge(*loaded(16 * n_loads))
            pe.wait_ge(*mstep(MSTEPS))
            with pe.Fori(0, B) as i:
                cols_of = ds(i * S, S)
                for ch in range(CHUNKS):
                    if ch < 2:
                        pe.wait_ge(*o_normed(2 * i))
                    else:
                        pe.wait_ge(*qk_put(CHUNKS * i + ch - 1))
                    bank = c.ps[:, 4 + ch % 2]
                    w = slice(ch * P, (ch + 1) * P)
                    for kk in range(KD):
                        nc.tensor.matmul(bank[:, 0:S], wq[:, kk, w], c.xT[:, kk, cols_of],
                                         start=(kk == 0), stop=(kk == KD - 1))
                    for kk, rows_k in enumerate(KC):
                        ins = nc.tensor.matmul(bank[:, S:2 * S], wk[0:rows_k, kk, w], ctxk[0:rows_k, kk, cols_of],
                                               start=(kk == 0), stop=(kk == 1 and not masked))
                    if masked:
                        ins = nc.tensor.matmul(bank[:, S:2 * S], rowsel[:], mbias[:, cols_of], start=False, stop=True)
                    ins.then_inc(qk_proj.sem, 1)
                pe.wait_ge(*staged(i + 1))
                for kt in range(2):
                    bank = c.ps[:, 6 + kt]
                    if biased:
                        nc.tensor.matmul(bank[:, 0:D], c.ones[0:1, :], rows[:, 0], start=True, stop=False)
                    for kk, rows_k in enumerate(KC):
                        ins = nc.tensor.matmul(bank[:, 0:D], cst[0:rows_k, kk, kt * P:(kt + 1) * P], wv[0:rows_k, kk],
                                               start=(kk == 0 and not biased), stop=(kk == 1))
                    ins.then_inc(v_proj.sem, 1)
                pe.wait_ge(*y_added(2 * i))
                for p in range(PAIRS):
                    ch = p // 2
                    if p % 2 == 0:
                        pe.wait_ge(*qk_put(CHUNKS * i + ch + 1))
                    if p < 2:
                        pe.wait_ge(*exped(PAIRS * i))
                    else:
                        pe.wait_ge(*max_put(PAIRS * i + p - 1))
                    for j in range(2):
                        for qt in range(2):
                            ins = nc.tensor.matmul(c.ps[:, 2 * (p % 2) + j, qt * S:(qt + 1) * S],
                                                   qh[:, ch, qt * P:(qt + 1) * P], kh[:, 2 * p + j, :],
                                                   start=True, stop=True)
                    ins.then_inc(scored.sem, 1)
                for ch in range(CHUNKS):
                    pe.wait_ge(*max_put(PAIRS * i + 2 * ch + 2))
                    if ch < 2:
                        pe.wait_ge(*qk_put(CHUNKS * i + CHUNKS))
                    else:
                        pe.wait_ge(*topped(CHUNKS * i + ch - 1))
                    for qt in range(2):
                        ins = nc.tensor.transpose(c.ps[:, 4 + ch % 2, qt * P:(qt + 1) * P],
                                                  mx[:, qt, ch].rearrange("p h s -> p (h s)").bitcast(F32),
                                                  c.ident[:])
                    ins.then_inc(max_turned.sem, 1)

                def score_T(p):
                    ch = p // 2
                    pe.wait_ge(*topped(CHUNKS * i + ch + 1))
                    pe.wait_ge(*k_rest(CHUNKS * i + ch + 1))
                    pe.wait_ge(*q_rest(CHUNKS * i + ch + 1))
                    if p < 2:
                        pe.wait_ge(*max_put(PAIRS * i + PAIRS))
                    else:
                        pe.wait_ge(*exped(PAIRS * i + p - 1))
                    for j in range(2):
                        for kt in range(2):
                            out = c.ps[:, 2 * (p % 2) + j, kt * S:(kt + 1) * S]
                            keys = slice(kt * P, (kt + 1) * P)
                            nc.tensor.matmul(out, kh[:, 2 * p + j, keys], qh[:, ch, :], start=True, stop=False)
                            nc.tensor.matmul(out, kh[:, 2 * p + j, keys], ql[:, ch, :], start=False, stop=False)
                            ins = nc.tensor.matmul(out, kl[:, 2 * p + j, keys], qh[:, ch, :], start=False, stop=True)
                    ins.then_inc(scored_T.sem, 1)

                def weigh(ch):
                    pe.wait_ge(*exped(PAIRS * i + 2 * ch + 2))
                    if ch == 0:
                        pe.wait_ge(*v_put(2 * i + 2))
                    for kt in range(2):
                        for j in range(HPC):
                            ins = nc.tensor.matmul(
                                c.ps[j * SLOT:(j + 1) * SLOT, 6 + ch // 2, (ch % 2) * S:(ch % 2 + 1) * S],
                                va[:, kt, ch * HPC + j], pt[:, ch % 2, j, kt], start=(kt == 0), stop=(kt == 1),
                                tile_position=(0, j * SLOT))
                    ins.then_inc(weighed.sem, 1)

                for ch in range(CHUNKS):
                    score_T(2 * ch)
                    score_T(2 * ch + 1)
                    if ch >= 1:
                        weigh(ch - 1)
                weigh(CHUNKS - 1)
                pe.wait_ge(*o_put(2 * i + 2))
                for ch in range(CHUNKS):
                    ins = nc.tensor.matmul(c.ps[0:HEADS, 4, 0:S], pick[:, ch], ot[:, ch], start=(ch == 0),
                                           stop=(ch == CHUNKS - 1))
                ins.then_inc(summed.sem, 1)
                pe.wait_ge(*inverted(i + 1))
                for ch in range(CHUNKS):
                    ins = nc.tensor.matmul(c.ps[:, 5 - ch // 2, (ch % 2) * S:(ch % 2 + 1) * S], give[:, ch], rec[:],
                                           start=True, stop=True)
                    if ch % 2:
                        ins.then_inc(spread.sem, 1)
                pe.wait_ge(*o_normed(2 * i + 2))
                for qt in range(2):
                    if biased:
                        nc.tensor.matmul(c.ps[:, qt, 0:D], c.ones[0:1, :], rows[:, 1], start=True, stop=False)
                    for ch in range(CHUNKS):
                        ins = nc.tensor.matmul(c.ps[:, qt, 0:D], ot[:, ch, qt * P:(qt + 1) * P], wo[:, ch],
                                               start=(ch == 0 and not biased), stop=(ch == CHUNKS - 1))
                    ins.then_inc(y_done.sem, 1)

        @block.scalar
        def _(act):
            act.wait_ge(*loaded(16 * n_loads))
            act.wait_ge(*mstep(MSTEPS))
            with act.Fori(0, B) as i:
                for ch in range(CHUNKS):
                    act.wait_ge(*qk_proj(CHUNKS * i + ch + 1))
                    before = CHUNKS * i + ch - 1 if ch >= 2 else CHUNKS * i
                    act.wait_ge(*q_rest(before))
                    act.wait_ge(*k_rest(before))
                    bank = c.ps[:, 4 + ch % 2]
                    for q in (qk[:, ch % 2, 0], qh[:, ch]):
                        nc.scalar.activation(q, bank[:, 0:S], ACT.Identity,
                                             bias=qcols[:, ch:ch + 1] if scale_in else cols[:, 0, ch:ch + 1],
                                             scale=qscale[:, 0:1] if scale_in else scale)
                    nc.scalar.activation(qk[:, ch % 2, 1], bank[:, S:2 * S], ACT.Identity, bias=cols[:, 1, ch:ch + 1])
                    for j in range(HPC):
                        r = slice(j * SLOT, (j + 1) * SLOT)
                        ins = nc.scalar.activation(kh[r, ch * HPC + j], bank[r, S:2 * S], ACT.Identity,
                                                   bias=cols[r, 1, ch:ch + 1])
                    ins.then_inc(qk_put.sem, 1)
                for p in range(PAIRS):
                    act.wait_ge(*scored_T(PAIRS * i + p + 1))
                    if p >= 4:
                        act.wait_ge(*weighed(CHUNKS * i + p // 2 - 1))
                    b0 = 2 * (p % 2)
                    nc.scalar.activation(pt[:, p // 2 % 2, b0:b0 + 2].rearrange("p j k s -> p (j k s)"),
                                         c.ps[:, b0:b0 + 2].rearrange("p j n -> p (j n)"),
                                         ACT.Exp).then_inc(exped.sem, 1)
                for n in range(2):
                    act.wait_ge(*weighed(CHUNKS * i + 2 * n + 2))
                    nc.scalar.copy(ot[:, 2 * n:2 * n + 2].rearrange("p c s -> p (c s)"), c.ps[:, 6 + n]
                                   ).then_inc(o_put.sem, 1)

        @block.vector
        def _(dve):
            step = Steps(mstep)
            step.n = 1
            dve.wait_ge(*mstep(1))
            dve.wait_ge(*loaded(16 * n_loads))
            if masked:
                step.link(dve, nc.vector.tensor_copy(mask[:], mask8[:]))
                step.mark(nc.vector.tensor_tensor(ctxk[:, 0], c.ctxT[:, 0], mask[:], ALU.mult))
                step.mark(nc.vector.tensor_tensor(ctxk[0:KC[1], 1], c.ctxT[0:KC[1], 1], mask[0:KC[1]], ALU.mult))
                step.link(dve, nc.vector.tensor_reduce(anyk[:], mask[:].rearrange("p (b s) -> p b s", b=B), AX_X,
                                                       ALU.max))
                step.link(dve, nc.vector.tensor_scalar(mbias[:], mask[0:1], -1.0, HUGE, ALU.add, ALU.mult))
                step.link(dve, nc.vector.tensor_tensor(
                    mbias[:].rearrange("p (b s) -> p b s", b=B), mbias[:].rearrange("p (b s) -> p b s", b=B),
                    anyk[0:1].unsqueeze(2).to_broadcast([1, B, S]), ALU.mult))
            elif scale_in:
                step.link(dve, nc.vector.tensor_scalar(qcols[:], cols[:, 0], qscale[:, 0:1], None, ALU.mult))
            assert step.n == MSTEPS
            with dve.Fori(0, B) as i:
                def rest(ch):
                    dve.wait_ge(*qk_put(CHUNKS * i + ch + 1))
                    for j in range(HPC):
                        r = slice(j * SLOT, (j + 1) * SLOT)
                        ins = nc.vector.tensor_tensor(kl[r, ch * HPC + j], qk[r, ch % 2, 1],
                                                      kh[r, ch * HPC + j].bitcast(F32), ALU.subtract)
                    ins.then_inc(k_rest.sem, 1)

                for ch in range(CHUNKS):
                    rest(ch)
                for kt in range(2):
                    dve.wait_ge(*v_proj(2 * i + kt + 1))
                    nc.vector.tensor_copy(va[:, kt, :, 0:HD],
                                          c.ps[:, 6 + kt, 0:D].rearrange("p (h d) -> p h d", h=HEADS)
                                          ).then_inc(v_put.sem, 1)
                for p in range(PAIRS):
                    dve.wait_ge(*scored(PAIRS * i + p + 1))
                    b0 = 2 * (p % 2)
                    nc.vector.tensor_reduce(mx[:, :, p // 2, b0:b0 + 2, MAX_ROW].rearrange("p t h -> p h t"),
                                            c.ps[:, b0:b0 + 2].rearrange("p j (t n) -> p j t n", t=2), AX_X,
                                            ALU.max).then_inc(max_put.sem, 1)
                for ch in range(CHUNKS):
                    dve.wait_ge(*q_rest(CHUNKS * i + ch + 1))
                    dve.wait_ge(*max_turned(CHUNKS * i + ch + 1))
                    nc.vector.tensor_tensor(qh[:, ch], qh[:, ch].bitcast(F32), c.ps[:, 4 + ch % 2, 0:S], ALU.add
                                            ).then_inc(topped.sem, 1)
                dve.wait_ge(*summed(i + 1))
                nc.vector.reciprocal(rec[0:HEADS], c.ps[0:HEADS, 4, 0:S]).then_inc(inverted.sem, 1)
                for n in range(2):
                    dve.wait_ge(*spread(2 * i + n + 1))
                    o = ot[:, 2 * n:2 * n + 2].rearrange("p c s -> p (c s)")
                    nc.vector.tensor_tensor(o, o, c.ps[:, 5 - n], ALU.mult).then_inc(o_normed.sem, 1)
                for qt in range(2):
                    dve.wait_ge(*y_done(2 * i + qt + 1))
                    xt = c.x[:, ds(2 * i + qt, 1)].squeeze(1)
                    nc.vector.tensor_tensor(xt, xt, c.ps[:, qt, 0:D], ALU.add).then_inc(y_added.sem, 1)
    loaded.spent(16 * n_loads)
    mstep.spent(MSTEPS)
    for sgn, n in ((staged, 1), (qk_proj, CHUNKS), (qk_put, CHUNKS), (v_proj, 2), (v_put, 2),
                   (q_rest, CHUNKS), (k_rest, CHUNKS), (scored, PAIRS), (max_put, PAIRS),
                   (max_turned, CHUNKS), (topped, CHUNKS), (scored_T, PAIRS), (exped, PAIRS), (weighed, CHUNKS),
                   (o_put, 2), (summed, 1), (inverted, 1), (spread, 2), (o_normed, 2), (y_done, 2), (y_added, 2)):
        sgn.spent(B * n)


def rank_rule(nc, dve, step, v, gt, eq, tri, rank):
    shape = [P, v.shape[1], v.shape[2], v.shape[2]]
    other, own = v.unsqueeze(2).to_broadcast(shape), v.unsqueeze(3).to_broadcast(shape)
    step.mark(nc.vector.tensor_tensor(gt, other, own, ALU.is_gt))
    step.link(dve, nc.vector.tensor_tensor(eq, other, own, ALU.is_equal))
    step.link(dve, nc.vector.tensor_tensor(eq, eq, tri.unsqueeze(1).to_broadcast(shape), ALU.mult))
    step.link(dve, nc.vector.tensor_tensor(gt, gt, eq, ALU.add))
    step.link(dve, nc.vector.tensor_reduce(rank, gt, AX_X, ALU.add))


def logits_on_pe(c, pe, wr, lgT, n, made, copied, lg_bank=2):
    nc = c.nc
    for g in range(NG):
        if g >= 2:
            pe.wait_ge(*copied(g - 1))
        for k in range(KD):
            ins = nc.tensor.matmul(c.ps[0:n, g % 2, :], wr[:, k], c.xT[:, k, g * GROUP:(g + 1) * GROUP],
                                   start=(k == 0), stop=(k == KD - 1))
        ins.then_inc(made.sem, 1)
    pe.wait_ge(*copied(NG))
    for t in range(NT):
        ins = nc.tensor.transpose(c.ps[:, lg_bank, t * n:(t + 1) * n], lgT[0:n, t * P:(t + 1) * P],
                                  c.ident[0:n, 0:n])
    ins.then_inc(made.sem, 1)


def softmax_router(c, tag, top, weights, slots, rows_back, firsts, passed=None):
    nc, ctx = c.nc, ExitStack()
    loaded, made, copied, step_s = c.sig("weights_in"), c.sig("logits"), c.sig("logitsT_put"), c.sig("dve_step")
    shifted, exped, chosen, counted = c.sig("shifted"), c.sig("exped"), c.sig("chosen"), c.sig("counted")
    tiles = tile_count(top)
    with ctx:
        def sb(name, shape):
            return c.sb("ro_" + name, shape, F32, ctx)

        wr, lgT, tri = sb("wr", [P, KD, E]), sb("lgT", [P, T]), sb("tri", [P, E, E])
        upto, edges, own_row = sb("upto", [P, P]), sb("edges", [P, NT - 1]), sb("own_row", [P, NT])
        v, pr, hot = sb("v", [P, NT, E]), sb("pr", [P, NT, E]), sb("hot", [P, 2, NT, E])
        gt, eq, rank = sb("gt", [P, NT, E, E]), sb("eq", [P, NT, E, E]), sb("rank", [P, NT, E])
        m, s = sb("m", [P, NT]), sb("s", [P, NT])
        before, run = sb("before", [P, 2, NT, E]), sb("run", [P, NT, E])
        kept, spare, place = sb("kept", [P, NT]), sb("spare", [P, NT]), sb("place", [P, 2, NT])
        total, over = sb("total", [P, E]), sb("over", [P, E, NT - 1])
        n_tiles, first, less = sb("n_tiles", [P, E]), sb("first", [P, E]), sb("less", [P, E, E])
        block = ctx.enter_context(nc.Block(no_gpsimd_drain=True))
        count = [0]

        @block.sync
        def _(sp):
            sp.dma_start(wr[:], c.dram[tag + "wr"]).then_inc(loaded.sem, 16)
            sp.dma_start(upto[:], c.dram["upto"]).then_inc(loaded.sem, 16)
            sp.dma_start(own_row[:], c.dram["own_row"]).then_inc(loaded.sem, 16)
            for dst, name in ((tri, "tri8"), (edges, "tile_edges")):
                sp.dma_start(dst[:], c.dram[name].partition_broadcast(P)).then_inc(loaded.sem, 16)

        @block.tensor
        def _(pe):
            pe.wait_ge(*loaded(80))
            logits_on_pe(c, pe, wr, lgT, E, made, copied)
            pe.wait_ge(*chosen(1))
            flat = hot[:, top - 1].rearrange("p t e -> p (t e)")
            nc.tensor.matmul(c.ps[:, 3, 0:NT * E], upto[:], flat, start=True, stop=True)
            nc.tensor.matmul(c.ps[:, 4, 0:NT * E], c.ones[:], flat, start=True, stop=True
                             ).then_inc(counted.sem, 1)

        @block.scalar
        def _(act):
            for g in range(NG):
                act.wait_ge(*made(g + 1))
                nc.scalar.copy(lgT[0:E, g * GROUP:(g + 1) * GROUP], c.ps[0:E, g % 2, :]).then_inc(copied.sem, 1)
            act.wait_ge(*shifted(1))
            nc.scalar.activation(pr[:].rearrange("p t e -> p (t e)"), v[:].rearrange("p t e -> p (t e)"),
                                 ACT.Exp).then_inc(exped.sem, 1)

        @block.vector
        def _(dve):
            step = Steps(step_s)
            per_token = [P, NT, E]
            dve.wait_ge(*made(NG + 1))
            dve.wait_ge(*loaded(80))
            lg = c.ps[:, 2, 0:NT * E].rearrange("p (t e) -> p t e", e=E)
            step.link(dve, nc.vector.tensor_reduce(m[:], lg, AX_X, ALU.max))
            nc.vector.tensor_tensor(v[:], lg, m[:].unsqueeze(2).to_broadcast(per_token), ALU.subtract
                                    ).then_inc(shifted.sem, 1)
            dve.wait_ge(*exped(1))
            step.link(dve, nc.vector.tensor_reduce(s[:], pr[:], AX_X, ALU.add))
            step.link(dve, nc.vector.reciprocal(s[:], s[:]))
            step.link(dve, nc.vector.tensor_tensor(pr[:], pr[:], s[:].unsqueeze(2).to_broadcast(per_token),
                                                   ALU.mult))
            rank_rule(nc, dve, step, pr[:], gt[:], eq[:], tri[:], rank[:])
            for n in range(top):
                ins = nc.vector.tensor_scalar(hot[:, n], rank[:], n + 1.0, None, ALU.is_lt)
            ins.then_inc(chosen.sem, 1)
            dve.wait_ge(*counted(1))
            within = c.ps[:, 3, 0:NT * E].rearrange("p (t e) -> p t e", e=E)
            whole = c.ps[:, 4, 0:NT * E].rearrange("p (t e) -> p t e", e=E)
            step.mark(nc.vector.memset(before[:, 0, 0:1], 0.0))
            step.link(dve, nc.vector.tensor_copy(before[:, 0, 1:NT], whole[:, 0:NT - 1]))
            side, d = 0, 1
            while d < NT:
                a, b = before[:, side], before[:, 1 - side]
                step.mark(nc.vector.tensor_copy(b[:, 0:d], a[:, 0:d]))
                step.link(dve, nc.vector.tensor_tensor(b[:, d:NT], a[:, d:NT], a[:, 0:NT - d], ALU.add))
                side, d = 1 - side, 2 * d
            step.mark(nc.vector.tensor_tensor(run[:], within, before[:, side], ALU.add))
            step.link(dve, nc.vector.tensor_tensor(total[:], before[:, side, NT - 1], whole[:, NT - 1], ALU.add))
            if top == 1:
                step.mark(nc.vector.tensor_scalar(total[:], total[:], float(CAP), None, ALU.min))
                step.link(dve, nc.vector.tensor_scalar(rank[:], run[:], float(CAP), None, ALU.is_le))
                step.link(dve, nc.vector.tensor_tensor(hot[:, 0], hot[:, 0], rank[:], ALU.mult))
                step.link(dve, nc.vector.tensor_reduce(kept[:], hot[:, 0], AX_X, ALU.add))
                step.link(dve, nc.vector.tensor_scalar(passed[:], kept[:], -1.0, 1.0, ALU.mult, ALU.add))
                step.mark(nc.vector.tensor_tensor(spare[:], passed[:], own_row[:], ALU.mult))
            else:
                step.link(dve, nc.vector.tensor_tensor(hot[:, 1], hot[:, 1], hot[:, 0], ALU.subtract))
            shape = [P, E, NT - 1]
            step.link(dve, nc.vector.tensor_tensor(over[:], total[:].unsqueeze(2).to_broadcast(shape),
                                                   edges[:].unsqueeze(1).to_broadcast(shape), ALU.is_gt))
            step.link(dve, nc.vector.tensor_reduce(n_tiles[:], over[:], AX_X, ALU.add))
            step.link(dve, nc.vector.tensor_scalar(n_tiles[:], n_tiles[:], 1.0, None, ALU.add))
            step.link(dve, nc.vector.tensor_tensor(less[:], tri[:], n_tiles[:].unsqueeze(1).to_broadcast([P, E, E]),
                                                   ALU.mult))
            step.link(dve, nc.vector.tensor_reduce(first[:], less[:], AX_X, ALU.add))
            step.mark(nc.vector.tensor_copy(firsts[:, 0:E], first[0:1]))
            step.mark(nc.vector.memset(firsts[:, E:E + 1], tiles))
            step.link(dve, nc.vector.tensor_scalar(less[:, 0], first[:], float(P), -1.0, ALU.mult, ALU.add))
            step.link(dve, nc.vector.tensor_tensor(run[:], run[:], less[:, 0].unsqueeze(1).to_broadcast(per_token),
                                                   ALU.add))
            for n in range(top):
                step.link(dve, nc.vector.tensor_tensor(gt[:, :, 0], hot[:, n], run[:], ALU.mult))
                step.mark(nc.vector.tensor_tensor(gt[:, :, 1], hot[:, n], pr[:], ALU.mult))
                step.link(dve, nc.vector.tensor_reduce(place[:, n], gt[:, :, 0], AX_X, ALU.add))
                step.link(dve, nc.vector.tensor_reduce(weights[:, n], gt[:, :, 1], AX_X, ALU.add))
                step.link(dve, nc.vector.tensor_copy(rows_back[:, n], place[:, n]))
                if top == 1:
                    step.link(dve, nc.vector.tensor_tensor(place[:, n], place[:, n], spare[:], ALU.add))
                step.link(dve, nc.vector.tensor_copy(slots[:, n], place[:, n]))
            if top == 2:
                step.link(dve, nc.vector.tensor_tensor(s[:], weights[:, 0], weights[:, 1], ALU.add))
                step.link(dve, nc.vector.tensor_scalar(s[:], s[:], 1e-9, None, ALU.add))
                step.link(dve, nc.vector.reciprocal(s[:], s[:]))
                step.link(dve, nc.vector.tensor_tensor(weights[:], weights[:],
                                                       s[:].unsqueeze(1).to_broadcast([P, 2, NT]), ALU.mult))
            count[0] = step.n
    step_s.spent(count[0])
    loaded.spent(80)
    made.spent(NG + 1)
    copied.spent(NG)
    for sgn in (shifted, exped, chosen, counted):
        sgn.spent(1)


def tile_count(top):
    return top * T // P + E - 1


def dispatch_phase(c, tag, top, slots, passed, xgT, w1, w2, b1):
    nc, ctx, shared = c.nc, ExitStack(), top == 2
    PART = 4
    parts = -(-tile_count(top) // PART)
    assert parts % 2 == 0
    sent, zeroed, in_par = c.sig("rows_sent"), c.sig("scratch_zeroed"), [c.sig("even_part_in"), c.sig("odd_part_in")]
    turned, put, w_in = c.sig("turned"), c.sig("xT_put"), c.sig("weights_in")
    h_done, h_put, y_done, y_added, passing = (c.sig(n) for n in ("h_done", "h_put", "y_done", "y_added", "dve_step"))
    with ctx:
        xg = c.sb("di_rows", [P, 2, PART, D], ctx=ctx)
        b2 = c.sb("di_b2", [1, D], ctx=ctx)
        h = c.sb("di_h", [P, FC, GROUP], ctx=ctx) if shared else None
        block = ctx.enter_context(nc.Block(no_gpsimd_drain=True))

        @block.gpsimd
        def _(pool):
            pool.wait_ge(*zeroed(16))
            for t in range(NT):
                for n in range(top):
                    nc.gpsimd.indirect_dma_start(c.dram["rows_in"], bass.IndirectOffsetOnAxis(slots[:, n, t:t + 1], 0),
                                                 c.xn[:, t], None).then_inc(sent.sem, 16)
            pool.wait_ge(*sent(16 * top * NT))

        @block.sync
        def _(sp):
            if shared:
                for dst, name in ((w1[:, 0], "w1s"), (w2[:, 0], "w2s"), (b1[:, 0], "b1s"), (b2[:], "b2s")):
                    sp.dma_start(dst, c.dram[tag + name]).then_inc(w_in.sem, 16)
            sp.wait_ge(*sent(16 * top * NT))
            rows = c.dram["rows_in"][0:parts * PART * P].rearrange("(a p) d -> p a d", p=P)
            with sp.Fori(0, parts // 2) as i:
                for s in range(2):
                    sp.wait_ge(*turned(2 * i + s - 1))
                    sp.dma_start(xg[:, s], rows[:, ds((2 * i + s) * PART, PART)]).then_inc(in_par[s].sem, 16)

        @block.tensor
        def _(pe):
            if shared:
                pe.wait_ge(*w_in(64))
                with pe.Fori(0, NG) as g:
                    for f in range(FC):
                        pe.wait_ge(*h_put(FC * g + max(f - 1, 0)))
                        for k in range(KD):
                            ins = nc.tensor.matmul(c.ps[:, f % 2, :], w1[:, 0, k, f * P:(f + 1) * P],
                                                   c.xT[:, k, ds(g * GROUP, GROUP)], start=(k == 0),
                                                   stop=(k == KD - 1))
                        ins.then_inc(h_done.sem, 1)
                    pe.wait_ge(*h_put(FC * g + FC))
                    pe.wait_ge(*y_added(TPG * g))
                    for tt in range(TPG):
                        out = c.ps[:, 2 + tt, 0:D]
                        nc.tensor.matmul(out, c.ones[0:1, :], b2[:], start=True, stop=False)
                        for f in range(FC):
                            ins = nc.tensor.matmul(out, h[:, f, tt * P:(tt + 1) * P], w2[:, 0, f], start=False,
                                                   stop=(f == FC - 1))
                        ins.then_inc(y_done.sem, 1)
            with pe.Fori(0, parts // 2) as i:
                for s in range(2):
                    pe.wait_ge(*in_par[s](16 * i + 16))
                    pe.wait_ge(*put(2 * i + s))
                    for a in range(PART):
                        for k in range(KD):
                            ins = nc.tensor.transpose(c.ps[:, 6 + a // 2, (a % 2 * KD + k) * P:(a % 2 * KD + k + 1) * P],
                                                      xg[:, s, a, k * P:(k + 1) * P], c.ident[:])
                    ins.then_inc(turned.sem, 1)

        @block.scalar
        def _(act):
            if shared:
                act.wait_ge(*w_in(64))
                with act.Fori(0, NG) as g:
                    for f in range(FC):
                        act.wait_ge(*h_done(FC * g + f + 1))
                        nc.scalar.activation(h[:, f], c.ps[:, f % 2, :], ACT.Silu, bias=b1[:, 0, f:f + 1]
                                             ).then_inc(h_put.sem, 1)
            with act.Fori(0, parts) as i:
                act.wait_ge(*turned(i + 1))
                nc.scalar.copy(xgT[:, ds(i * PART, PART)].rearrange("p a k t -> p (a k t)"),
                               c.ps[:, 6:8].rearrange("p b n -> p (b n)")).then_inc(put.sem, 1)

        @block.vector
        def _(dve):
            if shared:
                with dve.Fori(0, NG) as g:
                    for tt in range(TPG):
                        dve.wait_ge(*y_done(TPG * g + tt + 1))
                        xt = c.x[:, ds(g * TPG + tt, 1)].squeeze(1)
                        nc.vector.scalar_tensor_tensor(xt, c.ps[:, 2 + tt, 0:D], 0.1, xt, ALU.mult, ALU.add
                                                       ).then_inc(y_added.sem, 1)
            else:
                with dve.Fori(0, NT) as t:
                    xt = c.x[:, ds(t, 1)].squeeze(1)
                    nc.vector.scalar_tensor_tensor(xt, c.xn[:, ds(t, 1)].squeeze(1), passed[:, ds(t, 1)], xt, ALU.mult,
                                                   ALU.add).then_inc(passing.sem, 1)
    sent.spent(16 * top * NT)
    turned.spent(parts)
    put.spent(parts)
    for par in range(2):
        in_par[par].spent(16 * (parts // 2))
    if shared:
        w_in.spent(64)
        h_done.spent(FC * NG)
        h_put.spent(FC * NG)
        y_done.spent(TPG * NG)
        y_added.spent(TPG * NG)
    else:
        passing.spent(NT)


def expert_phases(c, tag):
    nc, ctx, first = c.nc, ExitStack(), tag == "L0f_"
    top = 1 if first else 2
    tiles = tile_count(top)
    loads = 2 if first else 4
    QUART = NT // 4
    w_in, h_done, h_put = [c.sig("even_expert_in"), c.sig("odd_expert_in")], c.sig("h_done"), c.sig("h_put")
    y_done, y_put, used, summed = c.sig("y_done"), c.sig("y_put"), c.sig("expert_used"), c.sig("y_added")
    out_stored, back = c.sig("tile_stored"), [c.sig(f"quarter{q}_back") for q in range(4)]
    with ctx:
        weights = c.sb("weights", [P, top, NT], ctx=ctx)
        slots, rows_back = (c.sb(n, [P, top, NT], U32, ctx) for n in ("slots", "rows_back"))
        firsts = c.sb("firsts", [1, E + 1], I32, ctx)
        passed = c.sb("passed", [P, NT], ctx=ctx) if first else None
        softmax_router(c, tag, top, weights, slots, rows_back, firsts, passed)
        w1 = c.sb("ex_w1", [P, 2, KD, FF], ctx=ctx)
        w2 = c.sb("ex_w2", [P, 2, FC, D], ctx=ctx)
        b1 = c.sb("ex_b1", [P, 2, FC], ctx=ctx)
        b2 = c.sb("ex_b2", [P, 2, D], ctx=ctx)
        xgT = c.sb("ex_tiles", [P, tiles + 1, KD, P], ctx=ctx)
        dispatch_phase(c, tag, top, slots, passed, xgT, w1, w2, b1)
        h = c.sb("ex_h", [P, FC, P], ctx=ctx)
        block = ctx.enter_context(nc.Block(no_gpsimd_drain=True))
        out_rows = c.dram["rows_out"].rearrange("(a p) d -> p a d", p=P)

        def tile_of(n):
            return xgT[:, ds(n, 1)].squeeze(1)

        def experts(eng, body, after=None, pairs=(0, E // 2)):
            with eng.Fori(*pairs) as i:
                for par in range(2):
                    e = 2 * i + par
                    lo = eng.value_load(firsts[0:1, ds(e, 1)], min_val=0, max_val=tiles)
                    hi = eng.value_load(firsts[0:1, ds(e + 1, 1)], min_val=0, max_val=tiles)
                    with eng.Fori(lo, hi) as n:
                        body(n, par, i)
                    if after:
                        after(e, par)

        @block.sync
        def _(sp):
            def load(e, par):
                parts = [(w1[:, par], "w1"), (w2[:, par], "w2")]
                parts += [] if first else [(b1[:, par], "b1")]
                for dst, name in parts:
                    sp.dma_start(dst, c.dram[tag + name][ds(e, 1)].squeeze(0)).then_inc(w_in[par].sem, 16)
                if not first:
                    sp.dma_start(b2[:, par], c.dram[tag + "b2"][ds(e, 1)].squeeze(0).partition_broadcast(P)
                                 ).then_inc(w_in[par].sem, 16)

            def store(n, par, pair):
                sp.wait_ge(*y_put(n + 1))
                sp.dma_start(out_rows[:, ds(n, 1)].squeeze(1), tile_of(n).rearrange("p k t -> p (k t)")
                             ).then_inc(out_stored.sem, 16)

            def load_next(e, par):
                sp.wait_ge(*used(e + 1))
                load(e + 2, par)

            load(0, 0)
            load(1, 1)
            experts(sp, store, load_next, (0, E // 2 - 1))
            experts(sp, store, None, (E // 2 - 1, E // 2))

        @block.tensor
        def _(pe):
            def ffn(n, par, pair):
                pe.wait_ge(*w_in[par](pair * 16 * loads + 16 * loads))
                for f in range(FC):
                    if f >= 4:
                        pe.wait_ge(*h_put(FC * n + f - 3))
                    for k in range(KD):
                        ins = nc.tensor.matmul(c.ps[:, f % 4, 0:P], w1[:, par, k, f * P:(f + 1) * P],
                                               tile_of(n)[:, k], start=(k == 0), stop=(k == KD - 1))
                    ins.then_inc(h_done.sem, 1)
                pe.wait_ge(*y_put(n))
                for f in range(FC):
                    pe.wait_ge(*h_put(FC * n + f + 1))
                    ins = nc.tensor.matmul(c.ps[:, 4, 0:D], h[:, f], w2[:, par, f], start=(f == 0),
                                           stop=(f == FC - 1))
                ins.then_inc(y_done.sem, 1)

            def through(e, par):
                hi = pe.value_load(firsts[0:1, ds(e + 1, 1)], min_val=0, max_val=tiles)
                pe.wait_ge(*y_put(hi))
                pe.sem_inc(used.sem, 1)

            experts(pe, ffn, through)

        @block.scalar
        def _(act):
            def activate(n, par, pair):
                for f in range(FC):
                    if not first and f == 0:
                        act.wait_ge(*w_in[par](pair * 16 * loads + 16 * loads))
                    act.wait_ge(*h_done(FC * n + f + 1))
                    nc.scalar.activation(h[:, f], c.ps[:, f % 4, 0:P], ACT.Relu if first else ACT.Silu,
                                         bias=0.0 if first else b1[:, par, f:f + 1]).then_inc(h_put.sem, 1)

            experts(act, activate)

        @block.vector
        def _(dve):
            def put_out(n, par, pair):
                y = tile_of(n).rearrange("p k t -> p (k t)")
                if not first:
                    dve.wait_ge(*w_in[par](pair * 16 * loads + 16 * loads))
                dve.wait_ge(*y_done(n + 1))
                if first:
                    nc.vector.tensor_copy(y, c.ps[:, 4, 0:D]).then_inc(y_put.sem, 1)
                else:
                    nc.vector.tensor_tensor(y, c.ps[:, 4, 0:D], b2[:, par], ALU.add).then_inc(y_put.sem, 1)

            experts(dve, put_out)
            for t in range(NT):
                if t % QUART == 0:
                    dve.wait_ge(*back[t // QUART](16 * top * QUART))
                xt = c.x[:, t]
                for n in range(top):
                    got = xgT[:, t].rearrange("p k t -> p (k t)") if n else c.xn[:, t]
                    if n:
                        dve.wait_ge(*summed(top * t + n))
                    nc.vector.scalar_tensor_tensor(xt, got, weights[:, n, t:t + 1], xt, ALU.mult, ALU.add
                                                   ).then_inc(summed.sem, 1)

        @block.gpsimd
        def _(pool):
            pool.wait_ge(*out_stored(16 * tiles))
            for t in range(NT):
                for n in range(top):
                    got = xgT[:, t].rearrange("p k t -> p (k t)") if n else c.xn[:, t]
                    nc.gpsimd.indirect_dma_start(got, None, c.dram["rows_out"][0:tiles * P],
                                                 bass.IndirectOffsetOnAxis(rows_back[:, n, t:t + 1], 0)
                                                 ).then_inc(back[t // QUART].sem, 16)
            for q in range(4):
                pool.wait_ge(*back[q](16 * top * QUART))
    for par in range(2):
        w_in[par].spent(16 * loads * (E // 2))
        back[par].spent(16 * top * QUART)
        back[par + 2].spent(16 * top * QUART)
    used.spent(E)
    h_done.spent(FC * tiles)
    h_put.spent(FC * tiles)
    y_done.spent(tiles)
    y_put.spent(tiles)
    out_stored.spent(16 * tiles)
    summed.spent(top * NT)


def grouped_router(c, cw):
    nc, ctx = c.nc, ExitStack()
    loaded, made, copied, step_s = c.sig("weights_in"), c.sig("logits"), c.sig("logitsT_put"), c.sig("dve_step")
    scored = c.sig("exped")
    n, per = E3, E3 // NGRP3
    with ctx:
        def sb(name, shape):
            return c.sb("gr_" + name, shape, F32, ctx)

        wr, lgT = sb("wr", [P, KD, n]), sb("lgT", [P, T])
        tri4, tri16, bias = sb("tri4", [P, per, per]), sb("tri16", [P, n, n]), sb("bias", [P, 1, n])
        score, choice, hot = sb("score", [P, NT, n]), sb("choice", [P, NT, n]), sb("hot", [P, NT, n])
        gt, eq, rank = sb("gt", [P, NT, n, n]), sb("eq", [P, NT, n, n]), sb("rank", [P, NT, n])
        gs, grank, s = sb("gs", [P, NT, NGRP3]), sb("grank", [P, NT, NGRP3]), sb("s", [P, NT])
        block = ctx.enter_context(nc.Block(no_gpsimd_drain=True))
        count = [0]

        @block.sync
        def _(sp):
            sp.dma_start(wr[:], c.dram["L3f_wr"]).then_inc(loaded.sem, 16)
            sp.dma_start(tri4[:], c.dram["tri4"].partition_broadcast(P)).then_inc(loaded.sem, 16)
            sp.dma_start(tri16[:], c.dram["tri16"].partition_broadcast(P)).then_inc(loaded.sem, 16)
            sp.dma_start(bias[:], c.dram["L3f_bias"].partition_broadcast(P)).then_inc(loaded.sem, 16)

        @block.tensor
        def _(pe):
            pe.wait_ge(*loaded(64))
            logits_on_pe(c, pe, wr, lgT, n, made, copied)

        @block.scalar
        def _(act):
            for g in range(NG):
                act.wait_ge(*made(g + 1))
                nc.scalar.copy(lgT[0:n, g * GROUP:(g + 1) * GROUP], c.ps[0:n, g % 2, :]).then_inc(copied.sem, 1)
            act.wait_ge(*made(NG + 1))
            nc.scalar.activation(score[:].rearrange("p t e -> p (t e)"), c.ps[:, 2, 0:NT * n], ACT.Sigmoid
                                 ).then_inc(scored.sem, 1)

        @block.vector
        def _(dve):
            step = Steps(step_s)
            dve.wait_ge(*scored(1))
            dve.wait_ge(*loaded(64))
            step.link(dve, nc.vector.tensor_tensor(choice[:], score[:], bias[:].to_broadcast([P, NT, n]), ALU.add))
            by_group = choice[:].rearrange("p t (g e) -> p (t g) e", g=NGRP3)
            small = [P, NT * NGRP3, per, per]
            gt4 = gt[:].rearrange("p t a b -> p (t a b)")[:, 0:NT * n * per].rearrange(
                "p (g a b) -> p g a b", a=per, b=per)
            eq4 = eq[:].rearrange("p t a b -> p (t a b)")[:, 0:NT * n * per].rearrange(
                "p (g a b) -> p g a b", a=per, b=per)
            rank_rule(nc, dve, step, by_group, gt4, eq4, tri4[:], rank[:].rearrange("p t (g e) -> p (t g) e", g=NGRP3))
            step.link(dve, nc.vector.tensor_scalar(hot[:], rank[:], 2.0, None, ALU.is_lt))
            step.link(dve, nc.vector.tensor_tensor(hot[:], hot[:], choice[:], ALU.mult))
            step.link(dve, nc.vector.tensor_reduce(gs[:].rearrange("p t g -> p (t g)"),
                                                   hot[:].rearrange("p t (g e) -> p (t g) e", g=NGRP3), AX_X, ALU.add))
            gtg = gt[:].rearrange("p t a b -> p (t a b)")[:, 0:NT * per * per].rearrange(
                "p (t a b) -> p t a b", a=per, b=per)
            eqg = eq[:].rearrange("p t a b -> p (t a b)")[:, 0:NT * per * per].rearrange(
                "p (t a b) -> p t a b", a=per, b=per)
            rank_rule(nc, dve, step, gs[:], gtg, eqg, tri4[:], grank[:])
            step.link(dve, nc.vector.tensor_scalar(gs[:], grank[:], float(TOPG3), None, ALU.is_lt))
            step.link(dve, nc.vector.tensor_scalar(grank[:], gs[:], -1.0, 1e9, ALU.add, ALU.mult))
            step.link(dve, nc.vector.tensor_tensor(
                by_group, by_group,
                gs[:].rearrange("p t g -> p (t g)").unsqueeze(2).to_broadcast([P, NT * NGRP3, per]), ALU.mult))
            step.link(dve, nc.vector.tensor_tensor(
                by_group, by_group,
                grank[:].rearrange("p t g -> p (t g)").unsqueeze(2).to_broadcast([P, NT * NGRP3, per]), ALU.add))
            rank_rule(nc, dve, step, choice[:], gt[:], eq[:], tri16[:], rank[:])
            step.link(dve, nc.vector.tensor_scalar(hot[:], rank[:], float(TOPK3), None, ALU.is_lt))
            step.link(dve, nc.vector.tensor_tensor(hot[:], hot[:], score[:], ALU.mult))
            step.link(dve, nc.vector.tensor_reduce(s[:], hot[:], AX_X, ALU.add))
            step.link(dve, nc.vector.tensor_scalar(s[:], s[:], 1e-20, None, ALU.add))
            step.link(dve, nc.vector.reciprocal(s[:], s[:]))
            step.link(dve, nc.vector.tensor_scalar(s[:], s[:], SCALED3, None, ALU.mult))
            step.link(dve, nc.vector.tensor_tensor(cw[:], hot[:], s[:].unsqueeze(2).to_broadcast([P, NT, n]),
                                                   ALU.mult))
            count[0] = step.n
    step_s.spent(count[0])
    loaded.spent(64)
    made.spent(NG + 1)
    copied.spent(NG)
    scored.spent(1)


def grouped_experts(c):
    nc, ctx = c.nc, ExitStack()
    w_in = [c.sig("even_expert_in"), c.sig("odd_expert_in")]
    h_done, gated, h_put = c.sig("h_done"), c.sig("gated"), c.sig("h_put")
    y_done, y_added = c.sig("y_done"), c.sig("y_added")
    WE = 2 * KD * I3 + D
    with ctx:
        cw = c.sb("cw", [P, NT, E3], ctx=ctx)
        grouped_router(c, cw)
        w = c.sb("ge_w", [P, 2, WE], ctx=ctx)
        sg = c.sb("ge_gate", [P, 2, GROUP], ctx=ctx)
        h = c.sb("ge_h", [P, 2, GROUP], ctx=ctx)
        block = ctx.enter_context(nc.Block(no_gpsimd_drain=True))

        @block.sync
        def _(sp):
            for e in range(2):
                sp.dma_start(w[:, e], c.dram["L3f_w"][e]).then_inc(w_in[e].sem, 16)
            with sp.Fori(0, E3 // 2 - 1) as i:
                for par in range(2):
                    sp.wait_ge(*y_done((2 * i + par + 1) * NG * TPG))
                    sp.dma_start(w[:, par], c.dram["L3f_w"][ds(2 * i + par + 2, 1)].squeeze(0)
                                 ).then_inc(w_in[par].sem, 16)

        @block.tensor
        def _(pe):
            with pe.Fori(0, E3 // 2) as i:
                for par in range(2):
                    n0 = (2 * i + par) * NG
                    pe.wait_ge(*w_in[par](16 * i + 16))
                    gate = w[:, par, 0:KD * I3].rearrange("p (k m) -> p k m", k=KD)
                    up = w[:, par, KD * I3:2 * KD * I3].rearrange("p (k m) -> p k m", k=KD)

                    def rise(g):
                        pe.wait_ge(*h_put(n0 + max(g - 1, 0)))
                        for n, m in enumerate((gate, up)):
                            for k in range(KD):
                                ins = nc.tensor.matmul(c.ps[:, 2 * (g % 2) + n, :], m[:, k],
                                                       c.xT[:, k, g * GROUP:(g + 1) * GROUP],
                                                       start=(k == 0), stop=(k == KD - 1))
                        ins.then_inc(h_done.sem, 1)

                    def fall(g):
                        pe.wait_ge(*h_put(n0 + g + 1))
                        pe.wait_ge(*y_added((n0 + g) * TPG))
                        for tt in range(TPG):
                            nc.tensor.matmul(c.ps[:, 4 + tt, 0:D], h[:, g % 2, tt * P:(tt + 1) * P],
                                             w[:, par, 2 * KD * I3:WE], start=True, stop=True
                                             ).then_inc(y_done.sem, 1)

                    rise(0)
                    for g in range(NG):
                        if g + 1 < NG:
                            rise(g + 1)
                        fall(g)

        @block.scalar
        def _(act):
            with act.Fori(0, E3 // 2) as i:
                for par in range(2):
                    for g in range(NG):
                        act.wait_ge(*h_done((2 * i + par) * NG + g + 1))
                        nc.scalar.activation(sg[:, g % 2], c.ps[:, 2 * (g % 2), :], ACT.Silu).then_inc(gated.sem, 1)

        @block.vector
        def _(dve):
            with dve.Fori(0, E3 // 2) as i:
                for par in range(2):
                    e = 2 * i + par

                    def multiply(g):
                        n = e * NG + g
                        dve.wait_ge(*gated(n + 1))
                        nc.vector.tensor_tensor(h[:, g % 2], sg[:, g % 2], c.ps[:, 2 * (g % 2) + 1, :], ALU.mult
                                                ).then_inc(h_put.sem, 1)

                    def add(g):
                        n = e * NG + g
                        dve.wait_ge(*y_added(n * TPG))
                        for tt in range(TPG):
                            dve.wait_ge(*y_done(TPG * n + tt + 1))
                            t = g * TPG + tt
                            weight = cw[:, t, ds(e, 1)]
                            nc.vector.scalar_tensor_tensor(c.x[:, t], c.ps[:, 4 + tt, 0:D], weight, c.x[:, t],
                                                           ALU.mult, ALU.add).then_inc(y_added.sem, 1)

                    multiply(0)
                    for g in range(NG):
                        if g + 1 < NG:
                            multiply(g + 1)
                        add(g)
    for sgn in w_in:
        sgn.spent(16 * E3 // 2)
    h_done.spent(NG * E3)
    gated.spent(NG * E3)
    h_put.spent(NG * E3)
    y_done.spent(TPG * NG * E3)
    y_added.spent(TPG * NG * E3)


def similarity_phase(c):
    nc, ctx = c.nc, ExitStack()
    loaded, staged, projected, put = c.sig("weights_in"), c.sig("ctx_staged"), c.sig("qk_proj"), c.sig("qk_put")
    squared, summed, rooted = c.sig("squared"), c.sig("sq_summed"), c.sig("rooted")
    dotted, added, step_s = c.sig("y_done"), c.sig("y_added"), c.sig("dve_step")
    with ctx:
        def sb(name, shape):
            return c.sb("si_" + name, shape, F32, ctx)

        w, b = sb("w", [P, 2, KD, HSIM]), sb("b", [P, 2])
        vt, sq = sb("vt", [P, 2, 2, S]), sb("sq", [P, 2, 2 * S])
        nrm = sb("nrm", [1, 2, 2 * S])
        r = sb("r", [P, 2, 2 * S])
        block = ctx.enter_context(nc.Block(no_gpsimd_drain=True))
        H = B // 2

        @block.sync
        def _(sp):
            sp.dma_start(w[:], c.dram["L1x_w"]).then_inc(loaded.sem, 16)
            sp.dma_start(b[:], c.dram["L1x_b"]).then_inc(loaded.sem, 16)

        @block.tensor
        def _(pe):
            pe.wait_ge(*loaded(32))
            with pe.Fori(0, H) as i:
                for s in range(2):
                    bank = c.ps[:, s, :]
                    pe.wait_ge(*squared(2 * i))
                    cols = ds((2 * i + s) * S, S)
                    for k in range(KD):
                        nc.tensor.matmul(bank[:, 0:S], w[:, 0, k], c.xT[:, k, cols], start=(k == 0),
                                         stop=(k == KD - 1))
                    for k, rows in enumerate(KC):
                        ins = nc.tensor.matmul(bank[:, S:2 * S], w[0:rows, 1, k], c.ctxT[0:rows, k, cols],
                                               start=(k == 0), stop=(k == 1))
                    ins.then_inc(projected.sem, 1)
                for s in range(2):
                    pe.wait_ge(*squared(2 * i + s + 1))
                    pe.wait_ge(*rooted(2 * i))
                    nc.tensor.matmul(c.ps[0:1, 2 + s, :], c.ones[:, 0:1], sq[:, s], start=True, stop=True
                                     ).then_inc(summed.sem, 1)
                for s in range(2):
                    pe.wait_ge(*added(2 * i))
                    for qt in range(2):
                        nc.tensor.matmul(c.ps[:, 6 + s, qt * S:(qt + 1) * S], vt[:, s, 0, qt * P:(qt + 1) * P],
                                         vt[:, s, 1], start=True, stop=True)
                    pe.wait_ge(*rooted(2 * i + s + 1))
                    for qt in range(2):
                        ins = nc.tensor.matmul(c.ps[:, 4 + s, qt * S:(qt + 1) * S], nrm[:, s, qt * P:(qt + 1) * P],
                                               nrm[:, s, S:2 * S], start=True, stop=True)
                    ins.then_inc(dotted.sem, 1)

        @block.scalar
        def _(act):
            act.wait_ge(*loaded(32))
            with act.Fori(0, H) as i:
                for s in range(2):
                    act.wait_ge(*projected(2 * i + s + 1))
                    for side in range(2):
                        part = c.ps[:, s, side * S:(side + 1) * S]
                        nc.scalar.activation(vt[:, s, side], part, ACT.Identity, bias=b[:, side:side + 1])
                        ins = nc.scalar.activation(sq[:, s, side * S:(side + 1) * S], part, ACT.Square,
                                                   bias=b[:, side:side + 1])
                    ins.then_inc(squared.sem, 1)
                for s in range(2):
                    act.wait_ge(*summed(2 * i + s + 1))
                    nc.scalar.activation(nrm[:, s], c.ps[0:1, 2 + s, :], ACT.Sqrt).then_inc(rooted.sem, 1)

        @block.vector
        def _(dve):
            with dve.Fori(0, H) as i:
                for s in range(2):
                    step = Steps(step_s, 2 * i + s, 3)
                    dve.wait_ge(*dotted(2 * i + s + 1))
                    dve.wait_ge(*added(2 * i))
                    step.link(dve, nc.vector.tensor_scalar(r[:, s], c.ps[:, 4 + s, :], 1e-8, None, ALU.max))
                    step.link(dve, nc.vector.reciprocal(r[:, s], r[:, s]))
                    step.link(dve, nc.vector.tensor_tensor(r[:, s], r[:, s], c.ps[:, 6 + s, :], ALU.mult))
                    xt = c.x[:, ds(2 * (2 * i + s), 2)].rearrange("p t d -> p (t d)")
                    nc.vector.tensor_tensor(xt, xt, r[:, s], ALU.add).then_inc(added.sem, 1)
    loaded.spent(32)
    step_s.spent(3 * B)
    for sgn in (projected, squared, summed, rooted, dotted, added):
        sgn.spent(B)



def local_attention(c, d, z):
    nc, ctx, dram = c.nc, ExitStack(), c.dram
    names = ("weights_in", "dve_step", "z_staged", "h_turned", "h_put", "qkv_done", "squared", "v_put", "sq_summed",
             "rooted", "lengthed", "q_rotated", "k_rotated", "qk_turned", "qk_put", "scored", "max_put", "max_negated",
             "exped", "p_turned", "p_put", "weighed", "inverted", "o_normed", "o_turned", "o_put", "y_done",
             "y_added", "pool_step", "dve_pair")
    (loaded, step_s, z_staged, h_turned, h_put, qkv_done, squared, v_put, summed, rooted, lengthed, q_rot, k_rot,
     qk_turned, qk_put, scored, topped, negated, exped, p_turned, p_put, weighed, inverted, o_normed, o_turned,
     o_put, y_done, added, pool_s, pair_s) = (c.sig(n) for n in names)
    HC = INNER // P
    HALF = LD // 2
    with ctx:
        def sb(name, shape):
            return c.sb("la_" + name, shape, F32, ctx)

        wqkv, wo = sb("wqkv", [P, KD, 3 * INNER]), sb("wo", [P, HC, D])
        rope, gain = sb("rope", [P, 2, 2, 2, LD]), sb("gain", [P, 2, LD])
        tab = sb("tab", [P, 2, 2, 2, LD])
        mask = sb("mask", [P, 3 * WIN])
        maskb, identb = (c.sb("la_" + n, [P, m], BF16, ctx) for n, m in (("maskb", 3 * WIN), ("identb", P)))
        zst, hs = sb("zst", [P, 2, D]), sb("hs", [P, KD, S])
        sq, ss = sb("sq", [P, 2, 2 * INNER]), sb("ss", [P, 2, 2 * LH])
        root, rn = sb("root", [P, 2, 2 * LH]), sb("rn", [P, 2, 2 * LH])
        t1, t2 = sb("t1", [P, 2, 2, INNER]), sb("t2", [P, 2, 2, INNER])
        qT, kT, v = sb("qT", [P, HC, S]), sb("kT", [P, HC, S]), sb("v", [P, 2, INNER])
        pr, pT = sb("p", [P, 2, 3 * WIN]), sb("pT", [P, 2, 3 * WIN])
        mx, nm, rs = sb("mx", [P, LH, 2]), sb("nm", [P, LH, 2]), sb("rs", [P, LH, 2])
        rec, on, ot = sb("rec", [P, LH, 2]), sb("on", [P, 2, INNER]), sb("ot", [P, 2, HC, P])
        block = ctx.enter_context(nc.Block(no_gpsimd_drain=True))
        SPLIT = [(0, WIN), (WIN, 3 * WIN)]
        SETUP = 9

        @block.sync
        def _(sp):
            for dst, name in ((wqkv, "wqkv"), (wo, "wo")):
                sp.dma_start(dst[:], dram["L1f_" + name][d]).then_inc(loaded.sem, 16)
            sp.dma_start(gain[:], dram["L1f_gain"][d].partition_broadcast(P)).then_inc(loaded.sem, 16)
            sp.dma_start(rope[:], dram["rope"]).then_inc(loaded.sem, 16)
            sp.dma_start(mask[:], dram["window"]).then_inc(loaded.sem, 16)

        def rotate(engine, eng, step, tt, side):
            a = t1[:, tt, side].rearrange("p (h d) -> p h d", h=LH)
            b = t2[:, tt, side].rearrange("p (h d) -> p h d", h=LH)
            for lo, hi in ((0, HALF), (HALF, LD)):
                src = a[:, :, HALF - lo:HALF - lo + HALF]
                step.mark(engine.tensor_tensor(
                    b[:, :, lo:hi], src, tab[:, side, 1, tt, lo:hi].unsqueeze(1).to_broadcast([P, LH, HALF]), ALU.mult))
            step.settle(eng)
            step.link(eng, engine.tensor_tensor(
                a, a, tab[:, side, 0, tt].unsqueeze(1).to_broadcast([P, LH, LD]), ALU.mult))
            return engine.tensor_tensor(a, a, b, ALU.add)

        @block.gpsimd
        def _(pool):
            nc.gpsimd.memset(hs[:, 1, 0:1], 0.0).then_inc(pool_s.sem, 1)
            with pool.Fori(0, B) as i:
                pool.wait_ge(*h_turned(i))
                nc.gpsimd.tensor_copy(zst[:], z[:, ds(2 * i, 2)]).then_inc(z_staged.sem, 1)
                for tt in range(2):
                    pool.wait_ge(*summed(2 * i + tt + 1))
                    nc.gpsimd.tensor_tensor(root[:, tt], ss[:, tt], c.half[:, 0, 0:2 * LH], ALU.pow
                                            ).then_inc(rooted.sem, 1)
                for tt in range(2):
                    step = Steps(pool_s, i, 6)
                    step.n = 1 + 3 * tt
                    pool.wait_ge(*lengthed(2 * i + tt + 1))
                    rotate(nc.gpsimd, pool, step, tt, 1).then_inc(k_rot.sem, 1)
            pool.wait_ge(*k_rot(2 * B))

        @block.tensor
        def _(pe):
            pe.wait_ge(*loaded(80))
            pe.wait_ge(*pair_s(SETUP - 1))
            with pe.Fori(0, B) as i:
                pe.wait_ge(*p_put(LH * i))
                pe.wait_ge(*z_staged(i + 1))
                for k in range(KD):
                    for tt in range(2):
                        ins = nc.tensor.transpose(c.ps[:, 0, k * S + tt * P:k * S + (tt + 1) * P],
                                                  zst[:, tt, k * P:(k + 1) * P], c.ident[:])
                ins.then_inc(h_turned.sem, 1)
                pe.wait_ge(*h_put(i + 1))
                pe.wait_ge(*added(2 * i))
                pe.wait_ge(*o_put(2 * i))
                pe.wait_ge(*o_normed(2 * i))
                for tt in range(2):
                    for n in range(3):
                        for k in range(KD):
                            ins = nc.tensor.matmul(c.ps[:, 1 + 3 * tt + n, :], hs[:, k, tt * P:(tt + 1) * P],
                                                   wqkv[:, k, n * INNER:(n + 1) * INNER],
                                                   start=(k == 0), stop=(k == KD - 1))
                    ins.then_inc(qkv_done.sem, 1)
                for tt in range(2):
                    pe.wait_ge(*q_rot(2 * i + tt + 1))
                    pe.wait_ge(*k_rot(2 * i + tt + 1))
                    for side in range(2):
                        bank = c.ps[:, ((7, 0), (1, 2))[tt][side], :]
                        for hc in range(HC):
                            ins = nc.tensor.transpose(bank[:, hc * P:(hc + 1) * P],
                                                      t1[:, tt, side, hc * P:(hc + 1) * P], c.ident[:])
                        ins.then_inc(qk_turned.sem, 1)

                def score(h):
                    r, hc = LD * (h % 2), h // 2
                    if h >= 2:
                        pe.wait_ge(*exped(LH * i + h - 1))
                    bank = c.ps[:, 3 + h % 2, :]
                    nc.tensor.matmul(bank[:, 0:3 * WIN], identb[:], maskb[:], start=True, stop=False)
                    nc.tensor.matmul(bank[:, 0:WIN], qT[r:r + LD, hc, 0:WIN], kT[r:r + LD, hc, 0:WIN],
                                     start=False, stop=False)
                    nc.tensor.matmul(bank[:, WIN:3 * WIN], qT[r:r + LD, hc, WIN:S], kT[r:r + LD, hc, :],
                                     start=False, stop=True).then_inc(scored.sem, 1)

                def turn(h):
                    pe.wait_ge(*exped(LH * i + h + 1))
                    if h >= 2:
                        pe.wait_ge(*p_put(LH * i + h - 1))
                    for n in range(3):
                        ins = nc.tensor.transpose(c.ps[:, 7 * (1 - h % 2), n * P:(n + 1) * P],
                                                  pr[:, h % 2, n * P:(n + 1) * P], c.ident[:])
                    ins.then_inc(p_turned.sem, 1)

                def weigh(h):
                    pe.wait_ge(*p_put(LH * i + h + 1))
                    cols = slice(h * LD, (h + 1) * LD)
                    nc.tensor.matmul(c.ps[:, 5, cols], pT[:, h % 2, 0:P], v[:, 0, cols], start=True, stop=True)
                    for kt in range(2):
                        ins = nc.tensor.matmul(c.ps[:, 6, cols], pT[:, h % 2, (1 + kt) * P:(2 + kt) * P],
                                               v[:, kt, cols], start=(kt == 0), stop=(kt == 1))
                    ins.then_inc(weighed.sem, 1)

                pe.wait_ge(*qk_put(4 * i + 4))
                pe.wait_ge(*v_put(2 * i + 2))
                score(0)
                score(1)
                for h in range(LH):
                    turn(h)
                    if h + 2 < LH:
                        score(h + 2)
                    if h >= 1:
                        weigh(h - 1)
                weigh(LH - 1)
                for qt in range(2):
                    pe.wait_ge(*o_normed(2 * i + qt + 1))
                    for hc in range(HC):
                        ins = nc.tensor.transpose(c.ps[:, 3 + qt, hc * P:(hc + 1) * P],
                                                  on[:, qt, hc * P:(hc + 1) * P], c.ident[:])
                    ins.then_inc(o_turned.sem, 1)
                for qt in range(2):
                    pe.wait_ge(*o_put(2 * i + qt + 1))
                    for hc in range(HC):
                        ins = nc.tensor.matmul(c.ps[:, 1 + qt, 0:D], ot[:, qt, hc], wo[:, hc],
                                               start=(hc == 0), stop=(hc == HC - 1))
                    ins.then_inc(y_done.sem, 1)

        @block.scalar
        def _(act):
            with act.Fori(0, B) as i:
                act.wait_ge(*h_turned(i + 1))
                nc.scalar.copy(hs[:, 0, :], c.ps[:, 0, 0:S])
                nc.scalar.copy(hs[:, 1, 1:S], c.ps[:, 0, S:2 * S - 1]).then_inc(h_put.sem, 1)
                for tt in range(2):
                    act.wait_ge(*qkv_done(2 * i + tt + 1))
                    nc.scalar.activation(sq[:, tt], c.ps[:, 1 + 3 * tt:3 + 3 * tt, :].rearrange("p a b -> p (a b)"),
                                         ACT.Square).then_inc(squared.sem, 1)
                    nc.scalar.copy(v[:, tt], c.ps[:, 3 + 3 * tt, :]).then_inc(v_put.sem, 1)
                for tt in range(2):
                    for side, dst in ((0, qT), (1, kT)):
                        act.wait_ge(*qk_turned(4 * i + 2 * tt + side + 1))
                        nc.scalar.copy(dst[:, :, tt * P:(tt + 1) * P],
                                       c.ps[:, ((7, 0), (1, 2))[tt][side], :].rearrange("p (h t) -> p h t", h=HC)
                                       ).then_inc(qk_put.sem, 1)
                for h in range(LH + 1):
                    if h < LH:
                        act.wait_ge(*negated(LH * i + h + 1))
                        if h >= 2:
                            act.wait_ge(*p_turned(LH * i + h - 1))
                        for n, (lo, hi) in enumerate(SPLIT):
                            ins = nc.scalar.activation(pr[:, h % 2, lo:hi], c.ps[:, 3 + h % 2, lo:hi], ACT.Exp,
                                                       bias=nm[:, h, n:n + 1], accum_out=rs[:, h, n:n + 1])
                        ins.then_inc(exped.sem, 1)
                    if h >= 1:
                        g = h - 1
                        act.wait_ge(*p_turned(LH * i + g + 1))
                        if g >= 2:
                            act.wait_ge(*weighed(LH * i + g - 1))
                        nc.scalar.copy(pT[:, g % 2], c.ps[:, 7 * (1 - g % 2), 0:3 * WIN]).then_inc(p_put.sem, 1)
                for qt in range(2):
                    act.wait_ge(*o_turned(2 * i + qt + 1))
                    nc.scalar.copy(ot[:, qt].rearrange("p k t -> p (k t)"), c.ps[:, 3 + qt, :]).then_inc(o_put.sem, 1)

        @block.vector
        def _(dve):
            dve.wait_ge(*loaded(80))
            step = Steps(pair_s)
            for side in range(2):
                g = gain[:, side]
                step.mark(nc.vector.tensor_tensor(tab[:, side, 0], rope[:, side, 0],
                                                  g.unsqueeze(1).to_broadcast([P, 2, LD]), ALU.mult))
                for lo, hi in ((0, HALF), (HALF, LD)):
                    step.mark(nc.vector.tensor_tensor(
                        tab[:, side, 1, :, lo:hi], rope[:, side, 1, :, lo:hi],
                        g[:, HALF - lo:HALF - lo + HALF].unsqueeze(1).to_broadcast([P, 2, HALF]), ALU.mult))
            step.mark(nc.vector.tensor_copy(maskb[:], mask[:]))
            step.mark(nc.vector.tensor_copy(identb[:], c.ident[:]))
            step.settle(dve)
            assert step.n == SETUP - 1
            with dve.Fori(0, B) as i:
                step = Steps(step_s, i, 5)
                for tt in range(2):
                    dve.wait_ge(*squared(2 * i + tt + 1))
                    nc.vector.tensor_reduce(ss[:, tt], sq[:, tt].rearrange("p (h d) -> p h d", d=LD), AX_X, ALU.add
                                            ).then_inc(summed.sem, 1)
                for tt in range(2):
                    dve.wait_ge(*rooted(2 * i + tt + 1))
                    step.link(dve, nc.vector.tensor_scalar(rn[:, tt], root[:, tt], 1e-12, None, ALU.max))
                    step.link(dve, nc.vector.reciprocal(rn[:, tt], rn[:, tt]))
                    nc.vector.tensor_tensor(
                        t1[:, tt].rearrange("p a (h d) -> p (a h) d", d=LD),
                        c.ps[:, 1 + 3 * tt:3 + 3 * tt, :].rearrange("p a (h d) -> p (a h) d", d=LD),
                        rn[:, tt].unsqueeze(2).to_broadcast([P, 2 * LH, LD]), ALU.mult).then_inc(lengthed.sem, 1)
                for tt in range(2):
                    dve.wait_ge(*lengthed(2 * i + tt + 1))
                    rot = Steps(pair_s, i, 6)
                    rot.n = SETUP - 1 + 3 * tt
                    rotate(nc.vector, dve, rot, tt, 0).then_inc(q_rot.sem, 1)
                for h in range(LH):
                    dve.wait_ge(*scored(LH * i + h + 1))
                    for n, (lo, hi) in enumerate(SPLIT):
                        ins = nc.vector.tensor_reduce(mx[:, h, n:n + 1], c.ps[:, 3 + h % 2, lo:hi], AX_X, ALU.max)
                    ins.then_inc(topped.sem, 1)
                    dve.wait_ge(*topped(LH * i + h + 1))
                    nc.vector.tensor_scalar(nm[:, h], mx[:, h], -1.0, None, ALU.mult).then_inc(negated.sem, 1)
                dve.wait_ge(*exped(LH * i + LH))
                step.link(dve, nc.vector.reciprocal(rec[:], rs[:]))
                dve.wait_ge(*weighed(LH * i + LH))
                for qt in range(2):
                    nc.vector.tensor_tensor(on[:, qt].rearrange("p (h d) -> p h d", h=LH),
                                            c.ps[:, 5 + qt, :].rearrange("p (h d) -> p h d", h=LH),
                                            rec[:, :, qt].unsqueeze(2).to_broadcast([P, LH, LD]), ALU.mult
                                            ).then_inc(o_normed.sem, 1)
                for qt in range(2):
                    dve.wait_ge(*y_done(2 * i + qt + 1))
                    zt = z[:, ds(2 * i + qt, 1)].squeeze(1)
                    nc.vector.tensor_tensor(zt, zt, c.ps[:, 1 + qt, 0:D], ALU.add).then_inc(added.sem, 1)
    loaded.spent(80)
    pool_s.spent(1 + 6 * B)
    pair_s.spent(SETUP - 1 + 6 * B)
    step_s.spent(5 * B)
    for sgn, n in ((z_staged, 1), (h_turned, 1), (h_put, 1), (qkv_done, 2), (squared, 2), (v_put, 2), (summed, 2),
                   (rooted, 2), (lengthed, 2), (q_rot, 2), (k_rot, 2), (qk_turned, 4), (qk_put, 4), (scored, LH),
                   (topped, LH), (negated, LH), (exped, LH), (p_turned, LH), (p_put, LH), (weighed, LH),
                   (o_normed, 2), (o_turned, 2), (o_put, 2), (y_done, 2), (added, 2)):
        sgn.spent(B * n)


def local_ff(c, d, z, last):
    nc, ctx, dram = c.nc, ExitStack(), c.dram
    loaded, moved, zeroed = c.sig("weights_in"), c.sig("shifted_in"), c.sig("pool_step")
    h_done, gated, h_put = c.sig("h_done"), c.sig("gated"), c.sig("h_put")
    y_done, added, ended = c.sig("y_done"), c.sig("y_added"), c.sig("dve_step")
    with ctx:
        def sb(name, shape):
            return c.sb("lf_" + name, shape, F32, ctx)

        w1, w2 = sb("w1", [P, KD, 2 * HPAD]), sb("w2", [P, HC_FF, D])
        b1, b2, affine = sb("b1", [P, 2, HC_FF]), sb("b2", [1, D]), sb("affine", [P, 2, KD])
        late = sb("late", [P, NT, D // 2])
        with nc.Block(no_gpsimd_drain=True) as block:
            @block.gpsimd
            def _(pool):
                nc.gpsimd.memset(late[0:1, :, :], 0.0).then_inc(zeroed.sem, 1)
                pool.wait_ge(*zeroed(1))

            @block.sync
            def _(sp):
                sp.dma_start(late[1:P], z[0:P - 1, :, D // 2:D]).then_inc(moved.sem, 16)
                sp.wait_ge(*zeroed(1))
                sp.dma_start(late[0:1].rearrange("p (b t) d -> p b t d", t=2)[:, :, 1],
                             z[P - 1:P].rearrange("p (b t) d -> p b t d", t=2)[:, :, 0, D // 2:D]
                             ).then_inc(moved.sem, 16)
                for dst, name in ((w1, "w1"), (w2, "w2"), (b1, "b1"), (b2, "b2"), (affine, "affine")):
                    sp.dma_start(dst[:], dram["L1f_" + name][d]).then_inc(loaded.sem, 16)
                sp.wait_ge(*moved(32))
                sp.wait_ge(*loaded(80))
        zeroed.spent(1)
        moved.spent(32)
        loaded.spent(80)
        norm_phase(c, [(z[:, :, 0:D // 2], 0), (late, D // 2)], affine=affine)
        gs = sb("gs", [P, 2, GROUP])
        h = sb("h", [P, HC_FF, GROUP])
        block = ctx.enter_context(nc.Block(no_gpsimd_drain=True))
        NH = HC_FF

        @block.tensor
        def _(pe):
            with pe.Fori(0, NG) as g:
                for f in range(NH):
                    pe.wait_ge(*h_put(NH * g + max(f - 1, 0)))
                    for side in range(2):
                        for k in range(KD):
                            ins = nc.tensor.matmul(c.ps[:, 2 * (f % 2) + side, :],
                                                   w1[:, k, side * HPAD + f * P:side * HPAD + (f + 1) * P],
                                                   c.xT[:, k, ds(g * GROUP, GROUP)], start=(k == 0),
                                                   stop=(k == KD - 1))
                    ins.then_inc(h_done.sem, 1)
                pe.wait_ge(*h_put(NH * g + NH))
                pe.wait_ge(*added(TPG * g))
                for tt in range(TPG):
                    nc.tensor.matmul(c.ps[:, 4 + tt, 0:D], c.ones[0:1, :], b2[:], start=True, stop=False)
                    for f in range(NH):
                        ins = nc.tensor.matmul(c.ps[:, 4 + tt, 0:D], h[:, f, tt * P:(tt + 1) * P], w2[:, f],
                                               start=False, stop=(f == NH - 1))
                    ins.then_inc(y_done.sem, 1)

        @block.scalar
        def _(act):
            with act.Fori(0, NG) as g:
                for f in range(NH):
                    act.wait_ge(*h_done(NH * g + f + 1))
                    nc.scalar.activation(gs[:, f % 2], c.ps[:, 2 * (f % 2) + 1, :], ACT.Gelu,
                                         bias=b1[:, 1, f:f + 1]).then_inc(gated.sem, 1)

        @block.vector
        def _(dve):
            with dve.Fori(0, NG) as g:
                for f in range(NH):
                    dve.wait_ge(*gated(NH * g + f + 1))
                    nc.vector.scalar_tensor_tensor(h[:, f], c.ps[:, 2 * (f % 2), :], b1[:, 0, f:f + 1],
                                                   gs[:, f % 2], ALU.add, ALU.mult).then_inc(h_put.sem, 1)
                for tt in range(TPG):
                    dve.wait_ge(*y_done(TPG * g + tt + 1))
                    zt = z[:, ds(g * TPG + tt, 1)].squeeze(1)
                    nc.vector.tensor_tensor(zt, zt, c.ps[:, 4 + tt, 0:D], ALU.add).then_inc(added.sem, 1)
            if last:
                dve.wait_ge(*added(NT))
                nc.vector.tensor_tensor(c.x[:], c.x[:], z[:], ALU.add).then_inc(ended.sem, 1)
    h_done.spent(NH * NG)
    gated.spent(NH * NG)
    h_put.spent(NH * NG)
    y_done.spent(NT)
    added.spent(NT)
    if last:
        ended.spent(1)


def local_transformer(c):
    norm_phase(c, [(c.x, 0)], keep=True, transposed=False)
    for d in range(DEPTH):
        local_attention(c, d, c.xn)
        local_ff(c, d, c.xn, last=(d == DEPTH - 1))


def _more_layouts(a, o):
    f4 = np.float32
    for n, name in ((E, "tri8"), (4, "tri4"), (16, "tri16")):
        o[name] = np.tril(np.ones((n, n), f4), -1)[None]
    o["upto"] = np.triu(np.ones((P, P), f4))
    o["L0f_wr"] = _chunked(a["L0_ffn_Wr"])
    o["L2f_wr"] = _chunked(a["L2_ffn_Wg"])
    for tag, w1, w2 in (("L0f_", a["L0_ffn_W1"], a["L0_ffn_W2"]),
                        ("L2f_", a["L2_ffn_W1"], a["L2_ffn_W2"])):
        o[tag + "w1"] = w1.reshape(-1, KD, P, FF).swapaxes(1, 2)
        o[tag + "w2"] = w2.reshape(-1, FC, P, D).swapaxes(1, 2)
    o["L2f_b1"] = a["L2_ffn_b1"].reshape(-1, FC, P).swapaxes(1, 2)
    o["L2f_b2"] = a["L2_ffn_b2"][:, None]
    o["L2f_w1s"], o["L2f_w2s"] = _chunked(a["L2_ffn_Ws1"]), _chunked(a["L2_ffn_Ws2"])
    o["L2f_b1s"], o["L2f_b2s"] = a["L2_ffn_bs1"].reshape(FC, P).T, a["L2_ffn_bs2"][None]
    o["tile_edges"] = (P * np.arange(1, NT, dtype=f4))[None]
    o["own_row"] = (SLOT_ROWS + np.arange(T, dtype=f4)).reshape(NT, P).T
    o["L3f_wr"] = _chunked(a["L3_ffn_router_weight"].T)
    o["L3f_bias"] = a["L3_ffn_router_bias"].reshape(1, 1, E3)
    gu = [a["L3_ffn_w_" + n].swapaxes(1, 2).reshape(E3, KD, P, I3).swapaxes(1, 2).reshape(E3, P, KD * I3)
          for n in ("gate", "up")]
    o["L3f_w"] = np.concatenate(gu + [a["L3_ffn_w_down"].swapaxes(1, 2)], 2)
    o["L1x_w"] = np.stack([_chunked(a["L1_xattn_Wv"].T), _chunked(a["L1_xattn_Wt"].T)], 1)
    o["L1x_b"] = np.stack([a["L1_xattn_bv"], a["L1_xattn_bt"]], 1)
    w1 = np.zeros((DEPTH, D, 2, HPAD), f4)
    w1[..., 0:HID] = a["L1_ffn_w1"].reshape(DEPTH, D, 2, HID)
    for name, w in (("wqkv", a["L1_ffn_wqkv"]), ("wo", a["L1_ffn_wo"]), ("w1", w1.reshape(DEPTH, D, 2 * HPAD)),
                    ("w2", a["L1_ffn_w2"])):
        o["L1f_" + name] = np.stack([_chunked(m) for m in w])
    o["L1f_gain"] = np.stack([a["L1_ffn_q_scale"], a["L1_ffn_k_scale"]], 1)[:, None]
    b1 = a["L1_ffn_b1"].reshape(DEPTH, 2, HID)
    o["L1f_b1"] = np.stack([np.stack([_chunked(b[s]) for s in range(2)], 1) for b in b1])
    o["L1f_b2"] = a["L1_ffn_b2"][:, None]
    o["L1f_affine"] = np.stack([a["L1_ffn_ln_g"], a["L1_ffn_ln_b"]], 1).reshape(DEPTH, 2, KD, P).transpose(0, 3, 1, 2)
    o["rope"] = _rope()
    q, k = np.arange(P)[:, None], np.arange(P)[None]
    off = lambda seen: np.where(seen, 0.0, -HUGE).astype(f4)
    o["window"] = np.concatenate([off(k <= q), off(k >= q), off(k <= q)], 1)


def _rope():
    f4 = np.float32
    half = np.arange(0, LD, 2, dtype=f4)
    t = np.arange(S, dtype=f4)
    freqs = t[:, None] * (f4(1.0) / f4(10000.0) ** (half / f4(LD)))[None]
    base = (half + f4(0.4 * LD)) / f4(1.4 * LD)
    scale = base[None] ** ((t - S // 2) / f4(WIN // 2))[:, None]
    cos, sin = np.cos(freqs), np.sin(freqs)
    out = np.empty((2, 2, S, LD), f4)
    for side, s in ((0, scale * f4(QK_SCALE)), (1, f4(1.0) / scale)):
        out[side, 0] = np.concatenate([cos * s, cos * s], 1)
        out[side, 1] = np.concatenate([-sin * s, sin * s], 1)
    return out.reshape(2, 2, 2, P, LD).transpose(3, 0, 1, 2, 4)


STAGES = (0, 8)


def _program(nc, dram, stages):
    with ExitStack() as ctx:
        c = Core(nc, ctx, dram)
        load_phase(c)
        layers = [
            lambda: (norm_phase(c, [(c.x, 0)]), xattn_phase(c, "L0x_", masked=True)),
            lambda: (norm_phase(c, [(c.x, 0)], keep=True), expert_phases(c, "L0f_")),
            lambda: (norm_phase(c, [(c.x, 0)]), similarity_phase(c)),
            lambda: local_transformer(c),
            lambda: (norm_phase(c, [(c.x, 0)]), xattn_phase(c, "L2x_", biased=True, scale_in=True)),
            lambda: (norm_phase(c, [(c.x, 0)], keep=True), expert_phases(c, "L2f_")),
            lambda: (norm_phase(c, [(c.x, 0)]), xattn_phase(c, "L3x_", biased=True)),
            lambda: (norm_phase(c, [(c.x, 0)]), grouped_experts(c)),
        ]
        for n in range(*stages):
            layers[n]()
        store_phase(c)


def _chunked(a, rows=P):
    n = -(-a.shape[0] // rows)
    out = np.zeros((n * rows,) + a.shape[1:], a.dtype)
    out[:a.shape[0]] = a
    return out.reshape((n, rows) + a.shape[1:]).swapaxes(0, 1)


def _padded_heads(w):
    out = np.zeros(w.shape[:-1] + (HEADS, SLOT), w.dtype)
    out[..., 0:HD] = w.reshape(w.shape[:-1] + (HEADS, HD))
    return out.reshape(w.shape[:-1] + (HEADS * SLOT,))


def _layouts(inp):
    f4 = np.float32
    a = {k: np.asarray(v) for k, v in inp.items()}
    o = {}
    o["x"] = a["x"].reshape(NT, P, D).swapaxes(0, 1)
    o["ctxT"] = _chunked(a["ctx_768"].reshape(T, DC).T)
    o["mask"] = a["mask_BxS2_bf1"].reshape(1, T).view(np.uint8)
    o["ident"] = np.eye(P, dtype=f4)
    z = np.zeros(D, f4)
    for tag, src, bq, bk, bv, bo in (("L0x_", "L0_xattn_", z, z, z, z),
                                     ("L2x_", "L2_xattn_", a["L2_xattn_bq"], a["L2_xattn_bk"], a["L2_xattn_bv"],
                                      a["L2_xattn_bo"]),
                                     ("L3x_", "L3_xattn_", z, z, z, a["L3_xattn_bo"])):
        o[tag + "wq"] = _chunked(_padded_heads(a[src + "Wq"]))
        o[tag + "wk"] = _chunked(_padded_heads(a[src + "Wk"]))
        o[tag + "wv"] = _chunked(a[src + "Wv"])
        o[tag + "wo"] = _chunked(np.ascontiguousarray(_padded_heads(a[src + "Wo"].T).T))
        qb = _padded_heads(bq).reshape(HEADS, SLOT).copy()
        kb = _padded_heads(bk).reshape(HEADS, SLOT).copy()
        qb[:, MASK_ROW] = 1.0 if tag == "L0x_" else 0.0
        kb[:, MAX_ROW] = -1.0
        o[tag + "cols"] = np.stack([qb.reshape(CHUNKS, P).T, kb.reshape(CHUNKS, P).T], 1)
        if tag != "L0x_":
            o[tag + "rows"] = np.stack([bv, bo])[None]
    sel = np.zeros((1, HPC, SLOT), f4)
    sel[:, :, MASK_ROW] = 1.0
    o["rowsel"] = sel.reshape(1, P)
    pick, give = np.zeros((HPC, SLOT, CHUNKS, HEADS), f4), np.zeros((P, CHUNKS, HPC, SLOT), f4)
    for h in range(HEADS):
        pick[h % HPC, HD, h // HPC, h] = 1.0
        give[h, h // HPC, h % HPC] = 1.0
    o["pick"], o["give"] = pick.reshape(P, CHUNKS, HEADS), give.reshape(P, CHUNKS, P)
    o["L2x_scale"] = a["L2_xattn_scale"].reshape(1, 1)
    _more_layouts(a, o)
    return {k: np.ascontiguousarray(v) for k, v in o.items()}


def kernel(**inputs):
    import concourse.bacc as _bacc
    from concourse import mybir as _mybir
    from concourse.bass_utils import run_bass_kernel_spmd as _run

    nc = _bacc.Bacc("TRN2", target_bir_lowering=False, num_devices=1)
    arrays, dram = {}, {}
    for name, a in _layouts(inputs).items():
        arrays[f"in_{name}_dram"] = a
        dram[name] = nc.dram_tensor(f"in_{name}_dram", a.shape, _mybir.dt.from_np(a.dtype), kind="ExternalInput").ap()
    out = nc.dram_tensor("out_0_dram", (B, S, D), _mybir.dt.float32, kind="ExternalOutput").ap()
    dram["out"] = out.rearrange("b (t p) d -> p (b t) d", p=P)
    for name, rows in (("rows_in", SLOT_ROWS + T), ("rows_out", SLOT_ROWS)):
        dram[name] = nc.dram_tensor(name, (rows, D), _mybir.dt.float32, kind="Internal").ap()
    _program(nc, dram, STAGES)
    r = _run(nc, [arrays], core_ids=[0])
    return r.results[0]["out_0_dram"]
```

```python
from contextlib import ExitStack

import numpy as np

import concourse.bass as bass
from concourse import mybir

F32 = mybir.dt.float32
BF16 = mybir.dt.bfloat16
F32R = mybir.dt.float32r
U8, U32, I32 = mybir.dt.uint8, mybir.dt.uint32, mybir.dt.int32
ALU = mybir.AluOpType
ACT = mybir.ActivationFunctionType
AX_X = mybir.AxisListType.X
ds = bass.ds

P = 128
B, S, D = 8, 256, 256
T = B * S
NT = T // P
KD = D // P
DC = 192
KC = [P, DC - P]
GROUP = 512
NG = T // GROUP
TPG = GROUP // P
EPS = 1e-5
HUGE = 1e30

HEADS, HD, SLOT = 16, 16, 32
CHUNKS = HEADS * SLOT // P
HPC = P // SLOT
MASK_ROW, MAX_ROW = HD, HD + 1

E, FF = 8, 1024
FC = FF // P
CAP = int(1.25 * T / E)
SLOT_ROWS = -(-(2 * T // P + E - 1) // 8) * 8 * P
E3, I3, NGRP3, TOPG3, TOPK3, SCALED3 = 16, 128, 4, 2, 4, 2.5

HSIM = 128
DEPTH, LH, LD, WIN = 2, 8, 64, 128
INNER = LH * LD
HID = int(D * 4 * 2 / 3)
HC_FF = -(-HID // P)
HPAD = HC_FF * P
QK_SCALE = 8.0


SIGNALS = """dve_step dve_pair pool_step variance powered normed turned xT_put kept mask_step ctx_staged qk_proj
qk_put v_proj v_put scored max_put max_turned q_topped scored_T exped weighed summed o_normed o_turned o_put y_done
y_added logits logitsT_put shifted chosen counted h_done h_put gated expert_used squared sq_summed rooted z_staged
h_turned qkv_done lengthed q_rotated k_rotated qk_turned max_negated p_turned p_put inverted set_up
q_rest_put k_rest_put spread y_put q_staged v_staged p_normed x_lead_put
x_rest_put w_lead_put w_rest_put h_lead_put h_rest_put""".split()
DMA_SIGNALS = """loaded weights_in even_expert_in odd_expert_in shifted_in stored shared_in
rows_sent scratch_zeroed even_part_in odd_part_in tile_stored quarter0_back quarter1_back quarter2_back
quarter3_back""".split()


START = 8


class Signal:

    def __init__(self, sem, base):
        self.sem, self.base = sem, base

    def __call__(self, n):
        return self.sem, self.base + n

    def spent(self, n):
        self.base += n


class Steps:

    def __init__(self, count, i=0, per=0):
        self.count, self.at, self.n = count, i * per, 0

    def mark(self, ins):
        self.n += 1
        return ins.then_inc(self.count.sem, 1)

    def settle(self, eng):
        eng.wait_ge(*self.count(self.at + self.n))

    def link(self, eng, ins):
        self.mark(ins)
        self.settle(eng)


class Core:

    def __init__(self, nc, ctx, dram):
        self.nc, self.ctx, self.dram, self.counts, self.tensors = nc, ctx, dram, {}, 0
        for names, base in ((SIGNALS, START), (DMA_SIGNALS, 0)):
            for name in names:
                self.counts[name] = Signal(ctx.enter_context(nc.semaphore(name)), base)
        self.x = self.sb("x_res", [P, NT, D])
        self.xT = self.sb("xn_T", [P, KD, T])
        self.xn = self.sb("xn_tok", [P, NT, D])
        self.ctxT = self.sb("ctx_T", [P, 2, T])
        self.ident = self.sb("ident", [P, P])
        self.ones = self.sb("ones", [P, P])
        self.half = self.sb("pow_half", [P, 2, P])
        self.zero = self.sb("zero", [P, 1, D])
        self.ps = ctx.enter_context(nc.psum_tensor("ps", [P, 8, 512], F32))

    def sb(self, name, shape, dt=F32, ctx=None):
        self.tensors += 1
        return (ctx or self.ctx).enter_context(self.nc.sbuf_tensor(f"{name}_{self.tensors}", shape, dt))

    def sig(self, name):
        return self.counts[name]


def load_phase(c):
    nc, loaded, set_up = c.nc, c.sig("loaded"), c.sig("set_up")
    with nc.Block() as block:
        @block.vector
        def _(dve):
            for name in SIGNALS:
                if name != "set_up":
                    dve.sem_inc(c.sig(name).sem, START)

        @block.sync
        def _(sp):
            for name, dst in (("x", c.x), ("ctxT", c.ctxT), ("ident", c.ident)):
                sp.dma_start(dst[:], c.dram[name]).then_inc(loaded.sem, 16)
            sp.wait_ge(*set_up(4))
            rows = c.dram["rows_in"][0:SLOT_ROWS].rearrange("(a p) d -> p a d", p=P)
            sp.dma_start(rows, c.zero[:].to_broadcast([P, SLOT_ROWS // P, D])).then_inc(c.sig("scratch_zeroed").sem, 16)
            sp.wait_ge(*loaded(48))

        @block.gpsimd
        def _(pool):
            nc.gpsimd.memset(c.ones[:], 1.0).then_inc(set_up.sem, 1)
            nc.gpsimd.memset(c.half[:, 0], 0.5).then_inc(set_up.sem, 1)
            nc.gpsimd.memset(c.half[:, 1], -0.5).then_inc(set_up.sem, 1)
            nc.gpsimd.memset(c.zero[:], 0.0).then_inc(set_up.sem, 1)
            pool.sem_inc(set_up.sem, START)
            pool.wait_ge(*set_up(4))
    loaded.spent(48)
    set_up.spent(4)


def store_phase(c):
    nc, stored = c.nc, c.sig("stored")
    with nc.Block() as block:
        @block.sync
        def _(sp):
            sp.dma_start(c.dram["out"], c.x[:]).then_inc(stored.sem, 16)
            sp.wait_ge(*stored(16))
    stored.spent(16)


def norm_phase(c, pieces, keep=False, transposed=True, affine=None, fetch=None, prepare=None):
    ROWS = 4
    nc, ctx = c.nc, ExitStack()
    stepped, variance, powered = c.sig("dve_step"), c.sig("variance"), c.sig("powered")
    normed, turned, put, kept = c.sig("normed"), c.sig("turned"), c.sig("xT_put"), c.sig("kept")
    npc, count = len(pieces), [0]
    ns = 2 * npc
    with ctx:
        xs = c.sb("ln_row", [P, ROWS, D], ctx=ctx)
        stats = c.sb("ln_stats", [P, NT, ns, 3], ctx=ctx)
        mean, rstd, var = (c.sb("ln_" + n, [P, NT], ctx=ctx) for n in ("mean", "rstd", "var"))
        total, sq_in, sq_dev = (c.sb("ln_" + n, [P, NT], ctx=ctx) for n in ("total", "sq_in", "sq_dev"))
        dev = c.sb("ln_dev", [P, 2, NT, ns], ctx=ctx)
        block = ctx.enter_context(nc.Block(no_gpsimd_drain=True))

        @block.vector
        def _(dve):
            step = Steps(stepped)
            for t in range(NT):
                for n, (src, _) in enumerate(pieces):
                    ins = nc.vector.bn_stats(stats[:, t, 2 * n:2 * n + 2].rearrange("p a b -> p (a b)"), src[:, t])
            step.link(dve, ins)
            step.mark(nc.vector.tensor_reduce(sq_in[:], stats[:, :, :, 2], AX_X, ALU.add))
            step.link(dve, nc.vector.tensor_reduce(total[:], stats[:, :, :, 1], AX_X, ALU.add))
            step.link(dve, nc.vector.tensor_scalar(mean[:], total[:], 1.0 / ns, None, ALU.mult))
            step.link(dve, nc.vector.tensor_tensor(dev[:, 0], stats[:, :, :, 1],
                                                   mean[:].unsqueeze(2).to_broadcast([P, NT, ns]), ALU.subtract))
            step.link(dve, nc.vector.tensor_tensor(dev[:, 1], dev[:, 0], dev[:, 0], ALU.mult))
            step.link(dve, nc.vector.tensor_reduce(sq_dev[:], dev[:, 1], AX_X, ALU.add))
            step.link(dve, nc.vector.scalar_tensor_tensor(total[:], sq_dev[:], float(D // ns), sq_in[:], ALU.mult,
                                                          ALU.add))
            nc.vector.tensor_scalar(var[:], total[:], 1.0 / D, EPS, ALU.mult, ALU.add).then_inc(variance.sem, 1)
            count[0] = step.n
            dve.wait_ge(*powered(1))
            with dve.Fori(0, NT // ROWS) as i:
                for s in range(ROWS):
                    t = ROWS * i + s
                    if transposed:
                        dve.wait_ge(*turned(t - ROWS + 1))
                    if keep:
                        dve.wait_ge(*kept(t - ROWS + 1))
                    for src, at in pieces:
                        ins = nc.vector.tensor_scalar(xs[:, s, at:at + D // npc], src[:, ds(t, 1)].squeeze(1),
                                                      mean[:, ds(t, 1)], rstd[:, ds(t, 1)], ALU.subtract, ALU.mult)
                    ins.then_inc(normed.sem, 1)

        @block.gpsimd
        def _(pool):
            pool.wait_ge(*variance(1))
            nc.gpsimd.tensor_tensor(rstd[:], var[:], c.half[:, 1, 0:NT], ALU.pow).then_inc(powered.sem, 1)
            if prepare:
                prepare(pool)
            if keep:
                with pool.Fori(0, NT // ROWS) as i:
                    for s in range(ROWS):
                        pool.wait_ge(*normed(ROWS * i + s + 1))
                        nc.gpsimd.tensor_copy(c.xn[:, ds(ROWS * i + s, 1)], xs[:, s]).then_inc(kept.sem, 1)
                pool.wait_ge(*kept(NT))

        if fetch:
            @block.sync
            def _(sp):
                fetch(sp)

        if transposed:
            @block.tensor
            def _(pe):
                with pe.Fori(0, NT // ROWS) as i:
                    for s in range(ROWS):
                        pe.wait_ge(*put(ROWS * i + s - ROWS + 1))
                        pe.wait_ge(*normed(ROWS * i + s + 1))
                        for k in range(KD):
                            ins = nc.tensor.transpose(c.ps[:, s, k * P:(k + 1) * P], xs[:, s, k * P:(k + 1) * P],
                                                      c.ident[:])
                        ins.then_inc(turned.sem, 1)

            @block.scalar
            def _(act):
                with act.Fori(0, NT // ROWS) as i:
                    for s in range(ROWS):
                        cols = ds((ROWS * i + s) * P, P)
                        act.wait_ge(*turned(ROWS * i + s + 1))
                        if affine is None:
                            ins = nc.scalar.copy(c.xT[:, :, cols], c.ps[:, s, 0:D].rearrange("p (k t) -> p k t", k=KD))
                        else:
                            for k in range(KD):
                                ins = nc.scalar.activation(c.xT[:, k, cols], c.ps[:, s, k * P:(k + 1) * P],
                                                           ACT.Identity, scale=affine[:, 0, k:k + 1],
                                                           bias=affine[:, 1, k:k + 1])
                        ins.then_inc(put.sem, 1)
    stepped.spent(count[0])
    for sgn, n in ((variance, 1), (powered, 1), (normed, NT)):
        sgn.spent(n)
    if transposed:
        turned.spent(NT)
        put.spent(NT)
    if keep:
        kept.spent(NT)


def xattn_phase(c, tag, masked=False, scale=0.25, biased=False, scale_in=False):
    nc, ctx, dram = c.nc, ExitStack(), c.dram
    names = ("weights_in", "mask_step", "ctx_staged", "qk_proj", "qk_put", "v_proj", "v_put", "q_rest_put",
             "k_rest_put", "scored", "max_put", "max_turned", "q_topped", "scored_T", "exped", "weighed", "o_put",
             "summed", "inverted", "spread", "o_normed", "y_done", "y_added")
    (loaded, mstep, staged, qk_proj, qk_put, v_proj, v_put, q_rest, k_rest, scored, max_put, max_turned,
     topped, scored_T, exped, weighed, o_put, summed, inverted, spread, o_normed, y_done, y_added) = (
        c.sig(n) for n in names)
    PAIRS = HEADS // 2
    MAXIMA = 2 + HPC * (CHUNKS - 1)
    with ctx:
        def sb(name, shape, dt=F32):
            return c.sb("xa_" + name, shape, dt, ctx)

        wq, wk = sb("wq", [P, KD, HEADS * SLOT]), sb("wk", [P, 2, HEADS * SLOT])
        wv, wo = sb("wv", [P, 2, D]), sb("wo", [P, CHUNKS, D])
        cols = sb("cols", [P, 2, CHUNKS])
        pick, give = sb("pick", [P, CHUNKS, HEADS]), sb("give", [P, CHUNKS, P])
        rows = sb("rows", [1, 2, D]) if biased else None
        q = sb("q", [P, 2, S])
        qh, ql = sb("qh", [P, CHUNKS, S], F32R), sb("ql", [P, CHUNKS, S], F32R)
        kh, kl = sb("kh", [P, HEADS, S], F32R), sb("kl", [P, HEADS, S], F32R)
        cst = sb("ctx", [P, 2, S])
        va = sb("v", [P, 2, HEADS, SLOT])
        mx = sb("mx", [P, 2, CHUNKS, HPC, SLOT], F32R)
        pt = sb("pT", [P, 2, HPC, 2, S])
        ot, rec = sb("ot", [P, CHUNKS, S]), sb("rec", [P, S])
        qscale = sb("qscale", [P, 1]) if scale_in else None
        qcols = sb("qcols", [P, CHUNKS]) if scale_in else None
        ctxk = c.ctxT
        if masked:
            mask8, mask = sb("mask8", [P, T], U8), sb("mask", [P, T])
            anyk, mbias, ctxk = sb("anyk", [P, B]), sb("mbias", [1, T]), sb("ctxk", [P, 2, T])
            rowsel = sb("rowsel", [1, P])
        n_loads = 7 + biased + scale_in + 2 * masked
        MSTEPS = 7 if masked else 2 if scale_in else 1

        def fetch(sp):
            loads = [(wq, tag + "wq"), (wk, tag + "wk"), (wv, tag + "wv"), (wo, tag + "wo"), (cols, tag + "cols"),
                     (pick, "pick"), (give, "give")]
            loads += [(rows, tag + "rows")] if biased else []
            loads += [(rowsel, "rowsel")] if masked else []
            for dst, name in loads:
                sp.dma_start(dst[:], dram[name]).then_inc(loaded.sem, 16)
            if scale_in:
                sp.dma_start(qscale[:], dram[tag + "scale"].partition_broadcast(P)).then_inc(loaded.sem, 16)
            if masked:
                sp.dma_start(mask8[:], dram["mask"].partition_broadcast(P)).then_inc(loaded.sem, 16)

        def prepare(pool):
            nc.gpsimd.memset(kh[:].bitcast(F32), 0.0)
            nc.gpsimd.memset(kl[:].bitcast(F32), 0.0)
            nc.gpsimd.memset(rec[:], 0.0)
            nc.gpsimd.memset(mx[:].bitcast(F32), 0.0)
            nc.gpsimd.memset(va[:], 1.0).then_inc(mstep.sem, 1)
            pool.wait_ge(*mstep(1))

        norm_phase(c, [(c.x, 0)], fetch=fetch, prepare=prepare)
        block = ctx.enter_context(nc.Block(no_gpsimd_drain=True))

        @block.gpsimd
        def _(pool):
            with pool.Fori(0, B) as i:
                pool.wait_ge(*v_proj(2 * i))
                nc.gpsimd.tensor_copy(cst[:], c.ctxT[:, :, ds(i * S, S)]).then_inc(staged.sem, 1)
                for ch in range(CHUNKS):
                    pool.wait_ge(*qk_put(CHUNKS * i + ch + 1))
                    nc.gpsimd.tensor_tensor(ql[:, ch], q[:, ch % 2], qh[:, ch].bitcast(F32), ALU.subtract
                                            ).then_inc(q_rest.sem, 1)
            pool.wait_ge(*q_rest(CHUNKS * B))

        @block.tensor
        def _(pe):
            pe.wait_ge(*loaded(16 * n_loads))
            pe.wait_ge(*mstep(MSTEPS))
            def project(i, ch):
                cols_of = ds(i * S, S)
                if ch < 2:
                    pe.wait_ge(*topped(CHUNKS * i))
                    pe.wait_ge(*k_rest(CHUNKS * i))
                else:
                    pe.wait_ge(*qk_put(CHUNKS * i + ch - 1))
                    pe.wait_ge(*k_rest(CHUNKS * i + ch - 1))
                bank = c.ps[:, 4 + ch % 2]
                w = slice(ch * P, (ch + 1) * P)
                for kk in range(KD):
                    nc.tensor.matmul(bank[:, 0:S], wq[:, kk, w], c.xT[:, kk, cols_of],
                                     start=(kk == 0), stop=(kk == KD - 1))
                for kk, rows_k in enumerate(KC):
                    ins = nc.tensor.matmul(bank[:, S:2 * S], wk[0:rows_k, kk, w], ctxk[0:rows_k, kk, cols_of],
                                           start=(kk == 0), stop=(kk == 1 and not masked))
                if masked:
                    ins = nc.tensor.matmul(bank[:, S:2 * S], rowsel[:], mbias[:, cols_of], start=False, stop=True)
                ins.then_inc(qk_proj.sem, 1)

            def project_v(i):
                pe.wait_ge(*staged(i + 1))
                pe.wait_ge(*o_put(CHUNKS * i))
                for kt in range(2):
                    bank = c.ps[:, 6 + kt]
                    if biased:
                        nc.tensor.matmul(bank[:, 0:D], c.ones[0:1, :], rows[:, 0], start=True, stop=False)
                    for kk, rows_k in enumerate(KC):
                        ins = nc.tensor.matmul(bank[:, 0:D], cst[0:rows_k, kk, kt * P:(kt + 1) * P], wv[0:rows_k, kk],
                                               start=(kk == 0 and not biased), stop=(kk == 1))
                    ins.then_inc(v_proj.sem, 1)

            def score_first(i):
                pe.wait_ge(*o_normed(2 * i))
                pe.wait_ge(*exped(PAIRS * i))
                pe.wait_ge(*qk_put(CHUNKS * i + 1))
                for h in range(HPC):
                    for qt in range(2):
                        ins = nc.tensor.matmul(c.ps[:, h, qt * S:(qt + 1) * S], qh[:, 0, qt * P:(qt + 1) * P],
                                               kh[:, h, :], start=True, stop=True)
                    if h % 2:
                        ins.then_inc(scored.sem, 1)

            def score(i, ch, j):
                n = HPC * (ch - 1) + j
                if n == 0:
                    pe.wait_ge(*y_added(2 * i))
                elif n == 1:
                    pe.wait_ge(*v_put(2 * i + 2))
                else:
                    pe.wait_ge(*max_put(MAXIMA * i + 2 + n - 1))
                if j == 0:
                    pe.wait_ge(*qk_put(CHUNKS * i + ch + 1))
                for qt in range(2):
                    ins = nc.tensor.matmul(c.ps[:, 4 + 3 * (n % 2), qt * S:(qt + 1) * S],
                                           qh[:, ch, qt * P:(qt + 1) * P], kh[:, ch * HPC + j, :],
                                           start=True, stop=True)
                ins.then_inc(scored.sem, 1)

            def turn_maxima(i, ch):
                pe.wait_ge(*max_put(MAXIMA * i + 2 + HPC * ch))
                if ch == 0:
                    pe.wait_ge(*k_rest(CHUNKS * i + CHUNKS))
                else:
                    pe.wait_ge(*topped(CHUNKS * i + ch))
                for qt in range(2):
                    ins = nc.tensor.transpose(c.ps[:, 5, qt * P:(qt + 1) * P],
                                              mx[:, qt, ch].rearrange("p h s -> p (h s)").bitcast(F32), c.ident[:])
                ins.then_inc(max_turned.sem, 1)

            def score_T(i, p, j):
                ch = p // 2
                if j == 0:
                    pe.wait_ge(*topped(CHUNKS * i + ch + 1))
                    pe.wait_ge(*k_rest(CHUNKS * i + ch + 1))
                    pe.wait_ge(*q_rest(CHUNKS * i + ch + 1))
                    pe.wait_ge(*exped(PAIRS * i + max(p - 1, 0)))
                for kt in range(2):
                    out = c.ps[:, 2 * (p % 2) + j, kt * S:(kt + 1) * S]
                    keys = slice(kt * P, (kt + 1) * P)
                    nc.tensor.matmul(out, kh[:, 2 * p + j, keys], qh[:, ch, :], start=True, stop=False)
                    nc.tensor.matmul(out, kh[:, 2 * p + j, keys], ql[:, ch, :], start=False, stop=False)
                    ins = nc.tensor.matmul(out, kl[:, 2 * p + j, keys], qh[:, ch, :], start=False, stop=True)
                if j == 1:
                    ins.then_inc(scored_T.sem, 1)

            def weigh(i, ch):
                pe.wait_ge(*exped(PAIRS * i + 2 * ch + 2))
                if ch == 0:
                    pe.wait_ge(*v_put(2 * i + 2))
                elif ch + 1 < CHUNKS:
                    pe.wait_ge(*o_put(CHUNKS * i + ch))
                for kt in range(2):
                    for j in range(HPC):
                        ins = nc.tensor.matmul(
                            c.ps[j * SLOT:(j + 1) * SLOT, 6 + (ch + 1) // CHUNKS, 0:S],
                            va[:, kt, ch * HPC + j], pt[:, ch % 2, j, kt], start=(kt == 0), stop=(kt == 1),
                            tile_position=(0, j * SLOT))
                ins.then_inc(weighed.sem, 1)

            def attend(i):
                turn_maxima(i, 0)
                for ch in range(CHUNKS):
                    for h in range(HPC):
                        if ch + 1 < CHUNKS:
                            score(i, ch + 1, h)
                        score_T(i, 2 * ch + h // 2, h % 2)
                    if ch + 1 < CHUNKS:
                        turn_maxima(i, ch + 1)
                    if ch >= 1:
                        weigh(i, ch - 1)
                weigh(i, CHUNKS - 1)

            def sum_weights(i):
                pe.wait_ge(*o_put(CHUNKS * i + CHUNKS))
                for ch in range(CHUNKS):
                    ins = nc.tensor.matmul(c.ps[0:HEADS, 2, 0:S], pick[:, ch], ot[:, ch], start=(ch == 0),
                                           stop=(ch == CHUNKS - 1))
                ins.then_inc(summed.sem, 1)

            def spread_factors(i):
                pe.wait_ge(*inverted(i + 1))
                for ch in range(CHUNKS):
                    ins = nc.tensor.matmul(c.ps[:, 3 - ch // 2, (ch % 2) * S:(ch % 2 + 1) * S], give[:, ch], rec[:],
                                           start=True, stop=True)
                    if ch % 2:
                        ins.then_inc(spread.sem, 1)

            def output(i, more):
                if more:
                    pe.wait_ge(*k_rest(CHUNKS * i + CHUNKS + 3))
                else:
                    pe.wait_ge(*max_put(MAXIMA * i + MAXIMA))
                pe.wait_ge(*o_normed(2 * i + 2))
                for qt in range(2):
                    out = c.ps[:, 4, qt * D:(qt + 1) * D]
                    if biased:
                        nc.tensor.matmul(out, c.ones[0:1, :], rows[:, 1], start=True, stop=False)
                    for ch in range(CHUNKS):
                        ins = nc.tensor.matmul(out, ot[:, ch, qt * P:(qt + 1) * P], wo[:, ch],
                                               start=(ch == 0 and not biased), stop=(ch == CHUNKS - 1))
                ins.then_inc(y_done.sem, 1)

            for ch in range(CHUNKS):
                project(0, ch)
            score_first(0)
            project_v(0)
            with pe.Fori(0, B - 1) as i:
                attend(i)
                project(i + 1, 0)
                sum_weights(i)
                project(i + 1, 1)
                spread_factors(i)
                project(i + 1, 2)
                project(i + 1, 3)
                score_first(i + 1)
                output(i, True)
                project_v(i + 1)
            attend(B - 1)
            sum_weights(B - 1)
            spread_factors(B - 1)
            output(B - 1, False)

        @block.scalar
        def _(act):
            act.wait_ge(*loaded(16 * n_loads))
            act.wait_ge(*mstep(MSTEPS))

            def put_qk(i, ch):
                act.wait_ge(*qk_proj(CHUNKS * i + ch + 1))
                act.wait_ge(*q_rest(CHUNKS * i + ch - 1))
                act.wait_ge(*k_rest(CHUNKS * i))
                bank = c.ps[:, 4 + ch % 2]
                for dst in (q[:, ch % 2], qh[:, ch]):
                    nc.scalar.activation(dst, bank[:, 0:S], ACT.Identity,
                                         bias=qcols[:, ch:ch + 1] if scale_in else cols[:, 0, ch:ch + 1],
                                         scale=qscale[:, 0:1] if scale_in else scale)
                for j in range(HPC):
                    r = slice(j * SLOT, (j + 1) * SLOT)
                    ins = nc.scalar.activation(kh[r, ch * HPC + j], bank[r, S:2 * S], ACT.Identity,
                                               bias=cols[r, 1, ch:ch + 1])
                ins.then_inc(qk_put.sem, 1)

            def put_o(i, ch):
                act.wait_ge(*weighed(CHUNKS * i + ch + 1))
                nc.scalar.copy(ot[:, ch], c.ps[:, 6 + (ch + 1) // CHUNKS, 0:S]).then_inc(o_put.sem, 1)

            def weights(i):
                for p in range(PAIRS):
                    act.wait_ge(*scored_T(PAIRS * i + p + 1))
                    if p >= 4:
                        act.wait_ge(*weighed(CHUNKS * i + p // 2 - 1))
                    b0 = 2 * (p % 2)
                    nc.scalar.activation(pt[:, p // 2 % 2, b0:b0 + 2].rearrange("p j k s -> p (j k s)"),
                                         c.ps[:, b0:b0 + 2].rearrange("p j n -> p (j n)"),
                                         ACT.Exp).then_inc(exped.sem, 1)
                    if p >= 3 and p % 2:
                        put_o(i, p // 2 - 1)
                put_o(i, CHUNKS - 1)

            for ch in range(CHUNKS):
                put_qk(0, ch)
            with act.Fori(0, B - 1) as i:
                weights(i)
                for ch in range(CHUNKS):
                    put_qk(i + 1, ch)
            weights(B - 1)

        @block.vector
        def _(dve):
            step = Steps(mstep)
            step.n = 1
            dve.wait_ge(*mstep(1))
            dve.wait_ge(*loaded(16 * n_loads))
            if masked:
                step.link(dve, nc.vector.tensor_copy(mask[:], mask8[:]))
                step.mark(nc.vector.tensor_tensor(ctxk[:, 0], c.ctxT[:, 0], mask[:], ALU.mult))
                step.mark(nc.vector.tensor_tensor(ctxk[0:KC[1], 1], c.ctxT[0:KC[1], 1], mask[0:KC[1]], ALU.mult))
                step.link(dve, nc.vector.tensor_reduce(anyk[:], mask[:].rearrange("p (b s) -> p b s", b=B), AX_X,
                                                       ALU.max))
                step.link(dve, nc.vector.tensor_scalar(mbias[:], mask[0:1], -1.0, HUGE, ALU.add, ALU.mult))
                step.link(dve, nc.vector.tensor_tensor(
                    mbias[:].rearrange("p (b s) -> p b s", b=B), mbias[:].rearrange("p (b s) -> p b s", b=B),
                    anyk[0:1].unsqueeze(2).to_broadcast([1, B, S]), ALU.mult))
            elif scale_in:
                step.link(dve, nc.vector.tensor_scalar(qcols[:], cols[:, 0], qscale[:, 0:1], None, ALU.mult))
            assert step.n == MSTEPS

            def rest(i, ch):
                dve.wait_ge(*qk_put(CHUNKS * i + ch + 1))
                for j in range(HPC):
                    r = slice(j * SLOT, (j + 1) * SLOT)
                    ins = nc.vector.scalar_tensor_tensor(kl[r, ch * HPC + j], c.ps[r, 4 + ch % 2, S:2 * S],
                                                         cols[r, 1, ch:ch + 1], kh[r, ch * HPC + j].bitcast(F32),
                                                         ALU.add, ALU.subtract)
                ins.then_inc(k_rest.sem, 1)

            def put_v(i):
                for kt in range(2):
                    dve.wait_ge(*v_proj(2 * i + kt + 1))
                    nc.vector.tensor_copy(va[:, kt, :, 0:HD],
                                          c.ps[:, 6 + kt, 0:D].rearrange("p (h d) -> p h d", h=HEADS)
                                          ).then_inc(v_put.sem, 1)

            def first_maxima(i):
                for n in range(2):
                    dve.wait_ge(*scored(MAXIMA * i + n + 1))
                    nc.vector.tensor_reduce(mx[:, :, 0, 2 * n:2 * n + 2, MAX_ROW].rearrange("p t h -> p h t"),
                                            c.ps[:, 2 * n:2 * n + 2].rearrange("p j (t n) -> p j t n", t=2), AX_X,
                                            ALU.max).then_inc(max_put.sem, 1)

            def maxima(i):
                for ch in range(CHUNKS):
                    for j in range(HPC if ch else 0):
                        n = HPC * (ch - 1) + j
                        dve.wait_ge(*scored(MAXIMA * i + 2 + n + 1))
                        nc.vector.tensor_reduce(mx[:, :, ch, j, MAX_ROW],
                                                c.ps[:, 4 + 3 * (n % 2)].rearrange("p (t n) -> p t n", t=2), AX_X,
                                                ALU.max).then_inc(max_put.sem, 1)
                    dve.wait_ge(*q_rest(CHUNKS * i + ch + 1))
                    dve.wait_ge(*max_turned(CHUNKS * i + ch + 1))
                    nc.vector.tensor_tensor(qh[:, ch], qh[:, ch].bitcast(F32), c.ps[:, 5, 0:S], ALU.add
                                            ).then_inc(topped.sem, 1)

            def invert(i):
                dve.wait_ge(*summed(i + 1))
                nc.vector.reciprocal(rec[0:HEADS], c.ps[0:HEADS, 2, 0:S]).then_inc(inverted.sem, 1)

            def normalise(i):
                for n in range(2):
                    dve.wait_ge(*spread(2 * i + n + 1))
                    o = ot[:, 2 * n:2 * n + 2].rearrange("p c s -> p (c s)")
                    nc.vector.tensor_tensor(o, o, c.ps[:, 3 - n], ALU.mult).then_inc(o_normed.sem, 1)

            def add(i):
                dve.wait_ge(*y_done(i + 1))
                for qt in range(2):
                    xt = c.x[:, ds(2 * i + qt, 1)].squeeze(1)
                    nc.vector.tensor_tensor(xt, xt, c.ps[:, 4, qt * D:(qt + 1) * D], ALU.add).then_inc(y_added.sem, 1)

            for ch in range(CHUNKS):
                rest(0, ch)
            first_maxima(0)
            put_v(0)
            with dve.Fori(0, B - 1) as i:
                maxima(i)
                invert(i)
                rest(i + 1, 0)
                normalise(i)
                for ch in range(1, CHUNKS):
                    rest(i + 1, ch)
                first_maxima(i + 1)
                add(i)
                put_v(i + 1)
            maxima(B - 1)
            invert(B - 1)
            normalise(B - 1)
            add(B - 1)
    loaded.spent(16 * n_loads)
    mstep.spent(MSTEPS)
    for sgn, n in ((staged, 1), (qk_proj, CHUNKS), (qk_put, CHUNKS), (v_proj, 2), (v_put, 2),
                   (q_rest, CHUNKS), (k_rest, CHUNKS), (scored, MAXIMA), (max_put, MAXIMA),
                   (max_turned, CHUNKS), (topped, CHUNKS), (scored_T, PAIRS), (exped, PAIRS), (weighed, CHUNKS),
                   (o_put, CHUNKS), (summed, 1), (inverted, 1), (spread, 2), (o_normed, 2), (y_done, 1), (y_added, 2)):
        sgn.spent(B * n)


def rank_rule(nc, dve, step, v, gt, eq, tri, rank):
    shape = [P, v.shape[1], v.shape[2], v.shape[2]]
    other, own = v.unsqueeze(2).to_broadcast(shape), v.unsqueeze(3).to_broadcast(shape)
    step.mark(nc.vector.tensor_tensor(gt, other, own, ALU.is_gt))
    step.link(dve, nc.vector.tensor_tensor(eq, other, own, ALU.is_equal))
    step.link(dve, nc.vector.tensor_tensor(eq, eq, tri.unsqueeze(1).to_broadcast(shape), ALU.mult))
    step.link(dve, nc.vector.tensor_tensor(gt, gt, eq, ALU.add))
    step.link(dve, nc.vector.tensor_reduce(rank, gt, AX_X, ALU.add))


def logits_on_pe(c, pe, wr, lgT, n, made, copied, lg_bank=2):
    nc = c.nc
    for g in range(NG):
        if g >= 2:
            pe.wait_ge(*copied(g - 1))
        for k in range(KD):
            ins = nc.tensor.matmul(c.ps[0:n, g % 2, :], wr[:, k], c.xT[:, k, g * GROUP:(g + 1) * GROUP],
                                   start=(k == 0), stop=(k == KD - 1))
        ins.then_inc(made.sem, 1)
    pe.wait_ge(*copied(NG))
    for t in range(NT):
        ins = nc.tensor.transpose(c.ps[:, lg_bank, t * n:(t + 1) * n], lgT[0:n, t * P:(t + 1) * P],
                                  c.ident[0:n, 0:n])
    ins.then_inc(made.sem, 1)


def softmax_router(c, tag, top, weights, slots, rows_back, firsts, passed=None, shared=None):
    nc, ctx = c.nc, ExitStack()
    loaded, made, copied, step_s = c.sig("weights_in"), c.sig("logits"), c.sig("logitsT_put"), c.sig("dve_step")
    shifted, exped, chosen, counted = c.sig("shifted"), c.sig("exped"), c.sig("chosen"), c.sig("counted")
    with ctx:
        def sb(name, shape):
            return c.sb("ro_" + name, shape, F32, ctx)

        wr, lgT, tri = sb("wr", [P, KD, E]), sb("lgT", [P, T]), sb("tri", [P, E, E])
        upto, edges, own_row = sb("upto", [P, P]), sb("edges", [P, NT - 1]), sb("own_row", [P, NT])
        v, pr, hot = sb("v", [P, NT, E]), sb("pr", [P, NT, E]), sb("hot", [P, 2, NT, E])
        gt, eq, rank = sb("gt", [P, NT, E, E]), sb("eq", [P, NT, E, E]), sb("rank", [P, NT, E])
        m, s = sb("m", [P, NT]), sb("s", [P, NT])
        before, run = sb("before", [P, 2, NT, E]), sb("run", [P, NT, E])
        kept, spare, place = sb("kept", [P, NT]), sb("spare", [P, NT]), sb("place", [P, 2, NT])
        total, over = sb("total", [P, E]), sb("over", [P, E, NT - 1])
        n_tiles, first, less = sb("n_tiles", [P, E]), sb("first", [P, E]), sb("less", [P, E, E])
        count = [0]

        def fetch(sp):
            sp.dma_start(wr[:], c.dram[tag + "wr"]).then_inc(loaded.sem, 16)
            sp.dma_start(upto[:], c.dram["upto"]).then_inc(loaded.sem, 16)
            sp.dma_start(own_row[:], c.dram["own_row"]).then_inc(loaded.sem, 16)
            for dst, name in ((tri, "tri8"), (edges, "tile_edges")):
                sp.dma_start(dst[:], c.dram[name].partition_broadcast(P)).then_inc(loaded.sem, 16)
            if shared:
                shared.fetch(sp)

        norm_phase(c, [(c.x, 0)], keep=True, fetch=fetch)
        block = ctx.enter_context(nc.Block(no_gpsimd_drain=True))

        @block.tensor
        def _(pe):
            pe.wait_ge(*loaded(80))
            logits_on_pe(c, pe, wr, lgT, E, made, copied, lg_bank=6)
            if shared:
                shared.rise(pe, 0)
            pe.wait_ge(*chosen(1))
            flat = hot[:, top - 1].rearrange("p t e -> p (t e)")
            nc.tensor.matmul(c.ps[:, 7, 0:NT * E], upto[:], flat, start=True, stop=True)
            nc.tensor.matmul(c.ps[:, 7, NT * E:2 * NT * E], c.ones[:], flat, start=True, stop=True
                             ).then_inc(counted.sem, 1)
            if shared:
                shared.fall(pe, 0)

        @block.scalar
        def _(act):
            for g in range(NG):
                act.wait_ge(*made(g + 1))
                nc.scalar.copy(lgT[0:E, g * GROUP:(g + 1) * GROUP], c.ps[0:E, g % 2, :]).then_inc(copied.sem, 1)
            act.wait_ge(*shifted(1))
            nc.scalar.activation(pr[:].rearrange("p t e -> p (t e)"), v[:].rearrange("p t e -> p (t e)"),
                                 ACT.Exp).then_inc(exped.sem, 1)
            if shared:
                shared.activate(act, 0)

        @block.vector
        def _(dve):
            step = Steps(step_s)
            per_token = [P, NT, E]
            dve.wait_ge(*made(NG + 1))
            dve.wait_ge(*loaded(80))
            lg = c.ps[:, 6, 0:NT * E].rearrange("p (t e) -> p t e", e=E)
            step.link(dve, nc.vector.tensor_reduce(m[:], lg, AX_X, ALU.max))
            nc.vector.tensor_tensor(v[:], lg, m[:].unsqueeze(2).to_broadcast(per_token), ALU.subtract
                                    ).then_inc(shifted.sem, 1)
            dve.wait_ge(*exped(1))
            step.link(dve, nc.vector.tensor_reduce(s[:], pr[:], AX_X, ALU.add))
            step.link(dve, nc.vector.reciprocal(s[:], s[:]))
            step.link(dve, nc.vector.tensor_tensor(pr[:], pr[:], s[:].unsqueeze(2).to_broadcast(per_token),
                                                   ALU.mult))
            rank_rule(nc, dve, step, pr[:], gt[:], eq[:], tri[:], rank[:])
            for n in range(top):
                ins = nc.vector.tensor_scalar(hot[:, n], rank[:], n + 1.0, None, ALU.is_lt)
            ins.then_inc(chosen.sem, 1)
            dve.wait_ge(*counted(1))
            within = c.ps[:, 7, 0:NT * E].rearrange("p (t e) -> p t e", e=E)
            whole = c.ps[:, 7, NT * E:2 * NT * E].rearrange("p (t e) -> p t e", e=E)
            step.mark(nc.vector.memset(before[:, 0, 0:1], 0.0))
            step.link(dve, nc.vector.tensor_copy(before[:, 0, 1:NT], whole[:, 0:NT - 1]))
            side, d = 0, 1
            while d < NT:
                a, b = before[:, side], before[:, 1 - side]
                step.mark(nc.vector.tensor_copy(b[:, 0:d], a[:, 0:d]))
                step.link(dve, nc.vector.tensor_tensor(b[:, d:NT], a[:, d:NT], a[:, 0:NT - d], ALU.add))
                side, d = 1 - side, 2 * d
            step.mark(nc.vector.tensor_tensor(run[:], within, before[:, side], ALU.add))
            step.link(dve, nc.vector.tensor_tensor(total[:], before[:, side, NT - 1], whole[:, NT - 1], ALU.add))
            if top == 1:
                step.mark(nc.vector.tensor_scalar(total[:], total[:], float(CAP), None, ALU.min))
                step.link(dve, nc.vector.tensor_scalar(rank[:], run[:], float(CAP), None, ALU.is_le))
                step.link(dve, nc.vector.tensor_tensor(hot[:, 0], hot[:, 0], rank[:], ALU.mult))
                step.link(dve, nc.vector.tensor_reduce(kept[:], hot[:, 0], AX_X, ALU.add))
                step.link(dve, nc.vector.tensor_scalar(passed[:], kept[:], -1.0, 1.0, ALU.mult, ALU.add))
                step.mark(nc.vector.tensor_tensor(spare[:], passed[:], own_row[:], ALU.mult))
            else:
                step.link(dve, nc.vector.tensor_tensor(hot[:, 1], hot[:, 1], hot[:, 0], ALU.subtract))
            shape = [P, E, NT - 1]
            step.link(dve, nc.vector.tensor_tensor(over[:], total[:].unsqueeze(2).to_broadcast(shape),
                                                   edges[:].unsqueeze(1).to_broadcast(shape), ALU.is_gt))
            step.link(dve, nc.vector.tensor_reduce(n_tiles[:], over[:], AX_X, ALU.add))
            step.link(dve, nc.vector.tensor_scalar(n_tiles[:], n_tiles[:], 1.0, None, ALU.add))
            step.link(dve, nc.vector.tensor_tensor(less[:], tri[:], n_tiles[:].unsqueeze(1).to_broadcast([P, E, E]),
                                                   ALU.mult))
            step.link(dve, nc.vector.tensor_reduce(first[:], less[:], AX_X, ALU.add))
            step.mark(nc.vector.tensor_copy(firsts[:, 0:E], first[0:1]))
            step.mark(nc.vector.tensor_tensor(firsts[:, E:E + 1], first[0:1, E - 1:E], n_tiles[0:1, E - 1:E], ALU.add))
            step.link(dve, nc.vector.tensor_scalar(less[:, 0], first[:], float(P), -1.0, ALU.mult, ALU.add))
            step.link(dve, nc.vector.tensor_tensor(run[:], run[:], less[:, 0].unsqueeze(1).to_broadcast(per_token),
                                                   ALU.add))
            for n in range(top):
                step.link(dve, nc.vector.tensor_tensor(gt[:, :, 0], hot[:, n], run[:], ALU.mult))
                step.mark(nc.vector.tensor_tensor(gt[:, :, 1], hot[:, n], pr[:], ALU.mult))
                step.link(dve, nc.vector.tensor_reduce(place[:, n], gt[:, :, 0], AX_X, ALU.add))
                step.link(dve, nc.vector.tensor_reduce(weights[:, n], gt[:, :, 1], AX_X, ALU.add))
                step.link(dve, nc.vector.tensor_copy(rows_back[:, n], place[:, n]))
                if top == 1:
                    step.link(dve, nc.vector.tensor_tensor(place[:, n], place[:, n], spare[:], ALU.add))
                step.link(dve, nc.vector.tensor_copy(slots[:, n], place[:, n]))
            if top == 2:
                step.link(dve, nc.vector.tensor_tensor(s[:], weights[:, 0], weights[:, 1], ALU.add))
                step.link(dve, nc.vector.tensor_scalar(s[:], s[:], 1e-9, None, ALU.add))
                step.link(dve, nc.vector.reciprocal(s[:], s[:]))
                step.link(dve, nc.vector.tensor_tensor(weights[:], weights[:],
                                                       s[:].unsqueeze(1).to_broadcast([P, 2, NT]), ALU.mult))
            if shared:
                shared.add(dve, 0)
            count[0] = step.n
    step_s.spent(count[0])
    loaded.spent(80)
    made.spent(NG + 1)
    copied.spent(NG)
    for sgn in (shifted, exped, chosen, counted):
        sgn.spent(1)


def tile_count(top):
    return top * T // P + E - 1


def dispatch_phase(c, tag, top, slots, passed, xgT, load, shared=None):
    nc, ctx = c.nc, ExitStack()
    PART = 4
    parts = -(-tile_count(top) // PART)
    assert parts % 2 == 0
    sent, zeroed, in_par = c.sig("rows_sent"), c.sig("scratch_zeroed"), [c.sig("even_part_in"), c.sig("odd_part_in")]
    turned, put, passing = c.sig("turned"), c.sig("xT_put"), c.sig("dve_step")
    with ctx:
        xg = c.sb("di_rows", [P, 2, PART, D], ctx=ctx)
        block = ctx.enter_context(nc.Block(no_gpsimd_drain=True))

        @block.gpsimd
        def _(pool):
            pool.wait_ge(*zeroed(16))
            for t in range(NT):
                for n in range(top):
                    nc.gpsimd.indirect_dma_start(c.dram["rows_in"], bass.IndirectOffsetOnAxis(slots[:, n, t:t + 1], 0),
                                                 c.xn[:, t], None).then_inc(sent.sem, 16)
            pool.wait_ge(*sent(16 * top * NT))

        @block.sync
        def _(sp):
            load(sp, 1, 1)
            if not shared:
                load(sp, 0, 0)
            sp.wait_ge(*sent(16 * top * NT))
            rows = c.dram["rows_in"][0:parts * PART * P].rearrange("(a p) d -> p a d", p=P)
            with sp.Fori(0, parts // 2) as i:
                for s in range(2):
                    sp.wait_ge(*turned(2 * i + s - 1))
                    sp.dma_start(xg[:, s], rows[:, ds((2 * i + s) * PART, PART)]).then_inc(in_par[s].sem, 16)
            if shared:
                shared.finish(sp)
                load(sp, 0, 0)

        @block.tensor
        def _(pe):
            if shared:
                with pe.Fori(1, NG) as g:
                    shared.rise(pe, g)
                    shared.fall(pe, g)
            with pe.Fori(0, parts // 2) as i:
                for s in range(2):
                    pe.wait_ge(*in_par[s](16 * i + 16))
                    pe.wait_ge(*put(2 * i + s - 1))
                    for a in range(PART):
                        for k in range(KD):
                            ins = nc.tensor.transpose(c.ps[:, 6 * s + a // 2, (a % 2 * KD + k) * P:(a % 2 * KD + k + 1) * P],
                                                      xg[:, s, a, k * P:(k + 1) * P], c.ident[:])
                    ins.then_inc(turned.sem, 1)

        @block.scalar
        def _(act):
            if shared:
                with act.Fori(1, NG) as g:
                    shared.activate(act, g)
            with act.Fori(0, parts // 2) as i:
                for s in range(2):
                    act.wait_ge(*turned(2 * i + s + 1))
                    nc.scalar.copy(xgT[:, ds((2 * i + s) * PART, PART)].rearrange("p a k t -> p (a k t)"),
                                   c.ps[:, 6 * s:6 * s + 2].rearrange("p b n -> p (b n)")).then_inc(put.sem, 1)

        @block.vector
        def _(dve):
            if shared:
                with dve.Fori(1, NG) as g:
                    shared.add(dve, g)
            else:
                with dve.Fori(0, NT) as t:
                    xt = c.x[:, ds(t, 1)].squeeze(1)
                    nc.vector.scalar_tensor_tensor(xt, c.xn[:, ds(t, 1)].squeeze(1), passed[:, ds(t, 1)], xt, ALU.mult,
                                                   ALU.add).then_inc(passing.sem, 1)
    sent.spent(16 * top * NT)
    turned.spent(parts)
    put.spent(parts)
    for par in range(2):
        in_par[par].spent(16 * (parts // 2))
    if shared:
        shared.spent()
    else:
        passing.spent(NT)


class SharedExpert:

    def __init__(self, c, ctx, w1, w2, b1):
        self.c, self.w1, self.w2, self.b1 = c, w1, w2, b1
        self.b2 = c.sb("sh_b2", [1, D], ctx=ctx)
        self.h = c.sb("sh_h", [P, FC, GROUP], ctx=ctx)
        self.w_in = c.sig("shared_in")
        self.h_done, self.h_put, self.y_done, self.y_added = (c.sig(n) for n in ("h_done", "h_put", "y_done",
                                                                                "y_added"))

    def fetch(self, sp):
        for dst, name in ((self.w1, "w1s"), (self.w2, "w2s"), (self.b1, "b1s"), (self.b2[:], "b2s")):
            sp.dma_start(dst, self.c.dram["L2f_" + name]).then_inc(self.w_in.sem, 16)

    def rise(self, pe, g):
        nc, c = self.c.nc, self.c
        pe.wait_ge(*self.w_in(64))
        for f in range(FC):
            pe.wait_ge(*self.h_put(FC * g + max(f - 1, 0)))
            for k in range(KD):
                ins = nc.tensor.matmul(c.ps[:, f % 2, :], self.w1[:, k, f * P:(f + 1) * P],
                                       c.xT[:, k, ds(g * GROUP, GROUP)], start=(k == 0), stop=(k == KD - 1))
            ins.then_inc(self.h_done.sem, 1)

    def fall(self, pe, g):
        nc, c = self.c.nc, self.c
        pe.wait_ge(*self.h_put(FC * g + FC))
        pe.wait_ge(*self.y_added(TPG * g))
        for tt in range(TPG):
            out = c.ps[:, 2 + tt, 0:D]
            nc.tensor.matmul(out, c.ones[0:1, :], self.b2[:], start=True, stop=False)
            for f in range(FC):
                ins = nc.tensor.matmul(out, self.h[:, f, tt * P:(tt + 1) * P], self.w2[:, f], start=False,
                                       stop=(f == FC - 1))
            ins.then_inc(self.y_done.sem, 1)

    def activate(self, act, g):
        act.wait_ge(*self.w_in(64))
        for f in range(FC):
            act.wait_ge(*self.h_done(FC * g + f + 1))
            self.c.nc.scalar.activation(self.h[:, f], self.c.ps[:, f % 2, :], ACT.Silu, bias=self.b1[:, f:f + 1]
                                        ).then_inc(self.h_put.sem, 1)

    def add(self, dve, g):
        c = self.c
        for tt in range(TPG):
            dve.wait_ge(*self.y_done(TPG * g + tt + 1))
            xt = c.x[:, ds(g * TPG + tt, 1)].squeeze(1)
            c.nc.vector.scalar_tensor_tensor(xt, c.ps[:, 2 + tt, 0:D], 0.1, xt, ALU.mult, ALU.add
                                             ).then_inc(self.y_added.sem, 1)

    def finish(self, sp):
        sp.wait_ge(*self.y_done(TPG * NG))

    def spent(self):
        self.w_in.spent(64)
        self.h_done.spent(FC * NG)
        self.h_put.spent(FC * NG)
        self.y_done.spent(TPG * NG)
        self.y_added.spent(TPG * NG)


def expert_phases(c, tag):
    nc, ctx, first = c.nc, ExitStack(), tag == "L0f_"
    top = 1 if first else 2
    tiles = tile_count(top)
    loads = 2 if first else 4
    QUART = NT // 4
    w_in, h_done, h_put = [c.sig("even_expert_in"), c.sig("odd_expert_in")], c.sig("h_done"), c.sig("h_put")
    y_done, y_put, summed = c.sig("y_done"), c.sig("y_put"), c.sig("y_added")
    out_stored, back = c.sig("tile_stored"), [c.sig(f"quarter{q}_back") for q in range(4)]
    with ctx:
        weights = c.sb("weights", [P, top, NT], ctx=ctx)
        slots, rows_back = (c.sb(n, [P, top, NT], U32, ctx) for n in ("slots", "rows_back"))
        firsts = c.sb("firsts", [1, E + 1], I32, ctx)
        passed = c.sb("passed", [P, NT], ctx=ctx) if first else None
        w1 = c.sb("ex_w1", [P, 2, KD, FF], ctx=ctx)
        w2 = c.sb("ex_w2", [P, 2, FC, D], ctx=ctx)
        b1 = c.sb("ex_b1", [P, 2, FC], ctx=ctx)
        b2 = c.sb("ex_b2", [P, 2, D], ctx=ctx)
        shared = None if first else SharedExpert(c, ctx, w1[:, 0], w2[:, 0], b1[:, 0])
        softmax_router(c, tag, top, weights, slots, rows_back, firsts, passed, shared)
        xgT = c.sb("ex_tiles", [P, tiles + 1, KD, P], ctx=ctx)

        def load(sp, e, par):
            parts = [(w1[:, par], "w1"), (w2[:, par], "w2")]
            parts += [] if first else [(b1[:, par], "b1")]
            for dst, name in parts:
                sp.dma_start(dst, c.dram[tag + name][ds(e, 1)].squeeze(0)).then_inc(w_in[par].sem, 16)
            if not first:
                sp.dma_start(b2[:, par], c.dram[tag + "b2"][ds(e, 1)].squeeze(0).partition_broadcast(P)
                             ).then_inc(w_in[par].sem, 16)

        dispatch_phase(c, tag, top, slots, passed, xgT, load, shared)
        h = c.sb("ex_h", [P, FC, P], ctx=ctx)
        block = ctx.enter_context(nc.Block(no_gpsimd_drain=True))
        out_rows = c.dram["rows_out"].rearrange("(a p) d -> p a d", p=P)

        def tile_of(n):
            return xgT[:, ds(n, 1)].squeeze(1)

        def experts(eng, body, after=None, pairs=(0, E // 2)):
            with eng.Fori(*pairs) as i:
                for par in range(2):
                    e = 2 * i + par
                    lo = eng.value_load(firsts[0:1, ds(e, 1)], min_val=0, max_val=tiles)
                    hi = eng.value_load(firsts[0:1, ds(e + 1, 1)], min_val=0, max_val=tiles)
                    with eng.Fori(lo, hi) as n:
                        body(n, par, i)
                    if after:
                        after(e, par)

        def for_spare_tiles(eng, signals):
            used = eng.value_load(firsts[0:1, E:E + 1], min_val=0, max_val=tiles)
            with eng.Fori(used, tiles):
                for sgn, n in signals:
                    eng.wait_ge(*sgn(used * n))
                    eng.sem_inc(sgn.sem, n)

        @block.sync
        def _(sp):
            def store(n, par, pair, spare=False):
                if not spare:
                    sp.wait_ge(*y_put(n + 1))
                sp.dma_start(out_rows[:, ds(n, 1)].squeeze(1), tile_of(n).rearrange("p k t -> p (k t)")
                             ).then_inc(out_stored.sem, 16)

            def load_next(e, par):
                load(sp, e + 2, par)

            experts(sp, store, load_next, (0, E // 2 - 1))
            experts(sp, store, None, (E // 2 - 1, E // 2))
            with sp.Fori(sp.value_load(firsts[0:1, E:E + 1], min_val=0, max_val=tiles), tiles) as n:
                store(n, 0, 0, spare=True)

        @block.tensor
        def _(pe):
            def ffn(n, par, pair):
                pe.wait_ge(*w_in[par](pair * 16 * loads + 16 * loads))
                for f in range(FC):
                    if f >= 4:
                        pe.wait_ge(*h_put(FC * n + f - 3))
                    for k in range(KD):
                        ins = nc.tensor.matmul(c.ps[:, f % 4, 0:P], w1[:, par, k, f * P:(f + 1) * P],
                                               tile_of(n)[:, k], start=(k == 0), stop=(k == KD - 1))
                    ins.then_inc(h_done.sem, 1)
                pe.wait_ge(*y_put(n))
                for f in range(FC):
                    pe.wait_ge(*h_put(FC * n + f + 1))
                    ins = nc.tensor.matmul(c.ps[:, 4, 0:D], h[:, f], w2[:, par, f], start=(f == 0),
                                           stop=(f == FC - 1))
                ins.then_inc(y_done.sem, 1)

            experts(pe, ffn)
            for_spare_tiles(pe, [(h_done, FC), (y_done, 1)])

        @block.scalar
        def _(act):
            def activate(n, par, pair):
                for f in range(FC):
                    if not first and f == 0:
                        act.wait_ge(*w_in[par](pair * 16 * loads + 16 * loads))
                    act.wait_ge(*h_done(FC * n + f + 1))
                    nc.scalar.activation(h[:, f], c.ps[:, f % 4, 0:P], ACT.Relu if first else ACT.Silu,
                                         bias=0.0 if first else b1[:, par, f:f + 1]).then_inc(h_put.sem, 1)

            experts(act, activate)
            for_spare_tiles(act, [(h_put, FC)])

        @block.vector
        def _(dve):
            def put_out(n, par, pair):
                y = tile_of(n).rearrange("p k t -> p (k t)")
                if not first:
                    dve.wait_ge(*w_in[par](pair * 16 * loads + 16 * loads))
                dve.wait_ge(*y_done(n + 1))
                if first:
                    nc.vector.tensor_copy(y, c.ps[:, 4, 0:D]).then_inc(y_put.sem, 1)
                else:
                    nc.vector.tensor_tensor(y, c.ps[:, 4, 0:D], b2[:, par], ALU.add).then_inc(y_put.sem, 1)

            experts(dve, put_out)
            for_spare_tiles(dve, [(y_put, 1)])
            for t in range(NT):
                if t % QUART == 0:
                    dve.wait_ge(*back[t // QUART](16 * top * QUART))
                xt = c.x[:, t]
                for n in range(top):
                    got = xgT[:, t].rearrange("p k t -> p (k t)") if n else c.xn[:, t]
                    if n:
                        dve.wait_ge(*summed(top * t + n))
                    nc.vector.scalar_tensor_tensor(xt, got, weights[:, n, t:t + 1], xt, ALU.mult, ALU.add
                                                   ).then_inc(summed.sem, 1)

        @block.gpsimd
        def _(pool):
            pool.wait_ge(*out_stored(16 * tiles))
            for t in range(NT):
                for n in range(top):
                    got = xgT[:, t].rearrange("p k t -> p (k t)") if n else c.xn[:, t]
                    nc.gpsimd.indirect_dma_start(got, None, c.dram["rows_out"][0:tiles * P],
                                                 bass.IndirectOffsetOnAxis(rows_back[:, n, t:t + 1], 0)
                                                 ).then_inc(back[t // QUART].sem, 16)
            for q in range(4):
                pool.wait_ge(*back[q](16 * top * QUART))
    for par in range(2):
        w_in[par].spent(16 * loads * (E // 2))
        back[par].spent(16 * top * QUART)
        back[par + 2].spent(16 * top * QUART)
    h_done.spent(FC * tiles)
    h_put.spent(FC * tiles)
    y_done.spent(tiles)
    y_put.spent(tiles)
    out_stored.spent(16 * tiles)
    summed.spent(top * NT)


def grouped_router(c, cw, x_lead, x_less, first):
    nc, ctx = c.nc, ExitStack()
    loaded, made, copied, step_s = c.sig("weights_in"), c.sig("logits"), c.sig("logitsT_put"), c.sig("dve_step")
    scored, lead_put, rest_put = c.sig("exped"), c.sig("x_lead_put"), c.sig("x_rest_put")
    n, per = E3, E3 // NGRP3
    with ctx:
        def sb(name, shape):
            return c.sb("gr_" + name, shape, F32, ctx)

        wr, lgT = sb("wr", [P, KD, n]), sb("lgT", [P, T])
        tri4, tri16, bias = sb("tri4", [P, per, per]), sb("tri16", [P, n, n]), sb("bias", [P, 1, n])
        score, choice, hot = sb("score", [P, NT, n]), sb("choice", [P, NT, n]), sb("hot", [P, NT, n])
        gt, eq, rank = sb("gt", [P, NT, n, n]), sb("eq", [P, NT, n, n]), sb("rank", [P, NT, n])
        gs, grank, s = sb("gs", [P, NT, NGRP3]), sb("grank", [P, NT, NGRP3]), sb("s", [P, NT])
        block = ctx.enter_context(nc.Block(no_gpsimd_drain=True))
        count = [0]

        @block.sync
        def _(sp):
            sp.dma_start(wr[:], c.dram["L3f_wr"]).then_inc(loaded.sem, 16)
            sp.dma_start(tri4[:], c.dram["tri4"].partition_broadcast(P)).then_inc(loaded.sem, 16)
            sp.dma_start(tri16[:], c.dram["tri16"].partition_broadcast(P)).then_inc(loaded.sem, 16)
            sp.dma_start(bias[:], c.dram["L3f_bias"].partition_broadcast(P)).then_inc(loaded.sem, 16)
            first["sync"](sp)

        @block.tensor
        def _(pe):
            pe.wait_ge(*loaded(64))
            logits_on_pe(c, pe, wr, lgT, n, made, copied)
            pe.wait_ge(*rest_put(NG))
            first["tensor"](pe)

        @block.scalar
        def _(act):
            for g in range(NG):
                act.wait_ge(*made(g + 1))
                nc.scalar.copy(lgT[0:n, g * GROUP:(g + 1) * GROUP], c.ps[0:n, g % 2, :]).then_inc(copied.sem, 1)
            act.wait_ge(*made(NG + 1))
            nc.scalar.activation(score[:].rearrange("p t e -> p (t e)"), c.ps[:, 2, 0:NT * n], ACT.Sigmoid
                                 ).then_inc(scored.sem, 1)
            for g in range(NG):
                nc.scalar.copy(x_lead[:, :, g * GROUP:(g + 1) * GROUP], c.xT[:, :, g * GROUP:(g + 1) * GROUP]
                               ).then_inc(lead_put.sem, 1)
            first["scalar"](act)

        @block.gpsimd
        def _(pool):
            for g in range(NG):
                cols = slice(g * GROUP, (g + 1) * GROUP)
                pool.wait_ge(*lead_put(g + 1))
                nc.gpsimd.tensor_tensor(x_less[:, :, cols], c.xT[:, :, cols],
                                        x_lead[:, :, cols].bitcast(F32), ALU.subtract).then_inc(rest_put.sem, 1)
            pool.wait_ge(*rest_put(NG))
            first["gpsimd"](pool)

        @block.vector
        def _(dve):
            step = Steps(step_s)
            dve.wait_ge(*scored(1))
            dve.wait_ge(*loaded(64))
            step.link(dve, nc.vector.tensor_tensor(choice[:], score[:], bias[:].to_broadcast([P, NT, n]), ALU.add))
            by_group = choice[:].rearrange("p t (g e) -> p (t g) e", g=NGRP3)
            small = [P, NT * NGRP3, per, per]
            gt4 = gt[:].rearrange("p t a b -> p (t a b)")[:, 0:NT * n * per].rearrange(
                "p (g a b) -> p g a b", a=per, b=per)
            eq4 = eq[:].rearrange("p t a b -> p (t a b)")[:, 0:NT * n * per].rearrange(
                "p (g a b) -> p g a b", a=per, b=per)
            rank_rule(nc, dve, step, by_group, gt4, eq4, tri4[:], rank[:].rearrange("p t (g e) -> p (t g) e", g=NGRP3))
            step.link(dve, nc.vector.tensor_scalar(hot[:], rank[:], 2.0, None, ALU.is_lt))
            step.link(dve, nc.vector.tensor_tensor(hot[:], hot[:], choice[:], ALU.mult))
            step.link(dve, nc.vector.tensor_reduce(gs[:].rearrange("p t g -> p (t g)"),
                                                   hot[:].rearrange("p t (g e) -> p (t g) e", g=NGRP3), AX_X, ALU.add))
            gtg = gt[:].rearrange("p t a b -> p (t a b)")[:, 0:NT * per * per].rearrange(
                "p (t a b) -> p t a b", a=per, b=per)
            eqg = eq[:].rearrange("p t a b -> p (t a b)")[:, 0:NT * per * per].rearrange(
                "p (t a b) -> p t a b", a=per, b=per)
            rank_rule(nc, dve, step, gs[:], gtg, eqg, tri4[:], grank[:])
            step.link(dve, nc.vector.tensor_scalar(gs[:], grank[:], float(TOPG3), None, ALU.is_lt))
            step.link(dve, nc.vector.tensor_scalar(grank[:], gs[:], -1.0, 1e9, ALU.add, ALU.mult))
            step.link(dve, nc.vector.tensor_tensor(
                by_group, by_group,
                gs[:].rearrange("p t g -> p (t g)").unsqueeze(2).to_broadcast([P, NT * NGRP3, per]), ALU.mult))
            step.link(dve, nc.vector.tensor_tensor(
                by_group, by_group,
                grank[:].rearrange("p t g -> p (t g)").unsqueeze(2).to_broadcast([P, NT * NGRP3, per]), ALU.add))
            rank_rule(nc, dve, step, choice[:], gt[:], eq[:], tri16[:], rank[:])
            step.link(dve, nc.vector.tensor_scalar(hot[:], rank[:], float(TOPK3), None, ALU.is_lt))
            step.link(dve, nc.vector.tensor_tensor(hot[:], hot[:], score[:], ALU.mult))
            step.link(dve, nc.vector.tensor_reduce(s[:], hot[:], AX_X, ALU.add))
            step.link(dve, nc.vector.tensor_scalar(s[:], s[:], 1e-20, None, ALU.add))
            step.link(dve, nc.vector.reciprocal(s[:], s[:]))
            step.link(dve, nc.vector.tensor_scalar(s[:], s[:], SCALED3, None, ALU.mult))
            step.link(dve, nc.vector.tensor_tensor(cw[:], hot[:], s[:].unsqueeze(2).to_broadcast([P, NT, n]),
                                                   ALU.mult))
            count[0] = step.n
    step_s.spent(count[0])
    loaded.spent(64)
    made.spent(NG + 1)
    copied.spent(NG)
    scored.spent(1)
    lead_put.spent(NG)
    rest_put.spent(NG)


def grouped_experts(c):
    nc, ctx = c.nc, ExitStack()
    w_in = [c.sig("even_expert_in"), c.sig("odd_expert_in")]
    w_lead, w_rest, h_done, gated = c.sig("w_lead_put"), c.sig("w_rest_put"), c.sig("h_done"), c.sig("gated")
    h_put, h_lead, h_rest = c.sig("h_put"), c.sig("h_lead_put"), c.sig("h_rest_put")
    y_done, y_added = c.sig("y_done"), c.sig("y_added")
    UP = KD * I3
    WE = 2 * UP + D
    with ctx:
        cw = c.sb("cw", [P, NT, E3], ctx=ctx)
        xh, xl = (c.sb("ge_" + n, [P, KD, T], F32R, ctx) for n in ("xh", "xl"))
        w = c.sb("ge_w", [P, 2, WE], ctx=ctx)
        wh, wl = (c.sb("ge_" + n, [P, 2, WE], F32R, ctx) for n in ("wh", "wl"))

        def load_two(sp):
            for e in range(2):
                sp.dma_start(w[:, e], c.dram["L3f_w"][e]).then_inc(w_in[e].sem, 16)

        def rise(pe, e, par, g):
            n = e * NG + g
            pe.wait_ge(*h_put(n - 1))
            pe.wait_ge(*w_rest(e + 1))
            cols = slice(g * GROUP, (g + 1) * GROUP)
            for m in range(2):
                for a, (wp, xp) in enumerate(((wh, xh), (wh, xl), (wl, xh))):
                    for k in range(KD):
                        at = m * UP + k * I3
                        ins = nc.tensor.matmul(c.ps[:, 2 * (g % 2) + m, :], wp[:, par, at:at + I3], xp[:, k, cols],
                                               start=(a == 0 and k == 0), stop=(a == 2 and k == KD - 1))
            ins.then_inc(h_done.sem, 1)

        def lead(act, e, par, pair):
            act.wait_ge(*w_in[par](16 * pair + 16))
            if not (isinstance(e, int) and e == 0):
                act.wait_ge(*y_done((e - 1) * NG * TPG))
            nc.scalar.copy(wh[:, par], w[:, par]).then_inc(w_lead.sem, 1)

        def rest(pool, e, par):
            pool.wait_ge(*w_lead(e + 1))
            nc.gpsimd.tensor_tensor(wl[:, par], w[:, par], wh[:, par].bitcast(F32), ALU.subtract
                                    ).then_inc(w_rest.sem, 1)
            if isinstance(e, int) and e == 0:
                pool.wait_ge(*w_rest(1))

        grouped_router(c, cw, xh, xl, {
            "sync": load_two, "tensor": lambda pe: rise(pe, 0, 0, 0), "scalar": lambda act: lead(act, 0, 0, 0),
            "gpsimd": lambda pool: rest(pool, 0, 0)})
        sg, h = (c.sb("ge_" + n, [P, 2, GROUP], ctx=ctx) for n in ("gate", "h"))
        hh, hl = (c.sb("ge_" + n, [P, 2, GROUP], F32R, ctx) for n in ("hh", "hl"))
        block = ctx.enter_context(nc.Block(no_gpsimd_drain=True))

        def experts(eng, expert):
            with eng.Fori(0, E3 // 2 - 1) as i:
                for par in range(2):
                    expert(2 * i + par, par, True)
            for e in range(E3 - 2, E3):
                expert(e, e % 2, e + 1 < E3)

        def following(step, e, par, g, more):
            if g + 1 < NG:
                step(e, par, g + 1)
            elif more:
                step(e + 1, 1 - par, 0)

        @block.sync
        def _(sp):
            with sp.Fori(0, E3 // 2 - 1) as i:
                for par in range(2):
                    e = 2 * i + par
                    sp.wait_ge(*w_rest(e + 1))
                    sp.dma_start(w[:, par], c.dram["L3f_w"][ds(e + 2, 1)].squeeze(0)).then_inc(w_in[par].sem, 16)

        @block.tensor
        def _(pe):
            def expert(e, par, more):
                for g in range(NG):
                    following(lambda *at: rise(pe, *at), e, par, g, more)
                    n = e * NG + g
                    pe.wait_ge(*h_rest(n + 1))
                    pe.wait_ge(*y_added(n * TPG))
                    for tt in range(TPG):
                        rows = slice(tt * P, (tt + 1) * P)
                        for a, (hp, wp) in enumerate(((hh, wh), (hl, wh), (hh, wl))):
                            ins = nc.tensor.matmul(c.ps[:, 4 + tt, 0:D], hp[:, g % 2, rows], wp[:, par, 2 * UP:WE],
                                                   start=(a == 0), stop=(a == 2))
                        ins.then_inc(y_done.sem, 1)

            experts(pe, expert)

        @block.scalar
        def _(act):
            def gate(e, par, g):
                n = e * NG + g
                act.wait_ge(*h_done(n + 1))
                act.wait_ge(*h_put(n - 1))
                nc.scalar.activation(sg[:, g % 2], c.ps[:, 2 * (g % 2), :], ACT.Silu).then_inc(gated.sem, 1)

            def expert(e, par, more):
                for g in range(NG):
                    gate(e, par, g)
                    n = e * NG + g
                    act.wait_ge(*h_put(n + 1))
                    act.wait_ge(*y_done(TPG * (n - 1)))
                    nc.scalar.copy(hh[:, g % 2], h[:, g % 2]).then_inc(h_lead.sem, 1)
                    if g == 1 and more:
                        lead(act, e + 1, 1 - par, (e + 1 - (1 - par)) // 2)

            experts(act, expert)

        @block.gpsimd
        def _(pool):
            def expert(e, par, more):
                for g in range(NG):
                    pool.wait_ge(*h_lead(e * NG + g + 1))
                    nc.gpsimd.tensor_tensor(hl[:, g % 2], h[:, g % 2], hh[:, g % 2].bitcast(F32), ALU.subtract
                                            ).then_inc(h_rest.sem, 1)
                    if g == 1 and more:
                        rest(pool, e + 1, 1 - par)

            experts(pool, expert)
            pool.wait_ge(*h_rest(NG * E3))

        @block.vector
        def _(dve):
            def multiply(e, par, g):
                n = e * NG + g
                dve.wait_ge(*gated(n + 1))
                dve.wait_ge(*h_rest(n - 1))
                nc.vector.tensor_tensor(h[:, g % 2], sg[:, g % 2], c.ps[:, 2 * (g % 2) + 1, :], ALU.mult
                                        ).then_inc(h_put.sem, 1)

            def expert(e, par, more):
                for g in range(NG):
                    following(multiply, e, par, g, more)
                    n = e * NG + g
                    dve.wait_ge(*y_added(n * TPG))
                    for tt in range(TPG):
                        dve.wait_ge(*y_done(TPG * n + tt + 1))
                        t = g * TPG + tt
                        nc.vector.scalar_tensor_tensor(c.x[:, t], c.ps[:, 4 + tt, 0:D], cw[:, t, ds(e, 1)],
                                                       c.x[:, t], ALU.mult, ALU.add).then_inc(y_added.sem, 1)

            multiply(0, 0, 0)
            experts(dve, expert)
    for sgn in w_in:
        sgn.spent(16 * E3 // 2)
    for sgn in (w_lead, w_rest):
        sgn.spent(E3)
    for sgn in (h_done, gated, h_put, h_lead, h_rest):
        sgn.spent(NG * E3)
    y_done.spent(TPG * NG * E3)
    y_added.spent(TPG * NG * E3)


def similarity_phase(c):
    nc, ctx = c.nc, ExitStack()
    loaded, staged, projected, put = c.sig("weights_in"), c.sig("ctx_staged"), c.sig("qk_proj"), c.sig("qk_put")
    squared, summed, rooted = c.sig("squared"), c.sig("sq_summed"), c.sig("rooted")
    dotted, added, step_s = c.sig("y_done"), c.sig("y_added"), c.sig("dve_step")
    with ctx:
        def sb(name, shape):
            return c.sb("si_" + name, shape, F32, ctx)

        w, b = sb("w", [P, 2, KD, HSIM]), sb("b", [P, 2])
        vt, sq = sb("vt", [P, 2, 2, S]), sb("sq", [P, 2, 2 * S])
        nrm = sb("nrm", [1, 2, 2 * S])
        r = sb("r", [P, 2, 2 * S])
        block = ctx.enter_context(nc.Block(no_gpsimd_drain=True))
        H = B // 2

        @block.sync
        def _(sp):
            sp.dma_start(w[:], c.dram["L1x_w"]).then_inc(loaded.sem, 16)
            sp.dma_start(b[:], c.dram["L1x_b"]).then_inc(loaded.sem, 16)

        @block.tensor
        def _(pe):
            pe.wait_ge(*loaded(32))
            with pe.Fori(0, H) as i:
                for s in range(2):
                    bank = c.ps[:, s, :]
                    pe.wait_ge(*squared(2 * i))
                    cols = ds((2 * i + s) * S, S)
                    for k in range(KD):
                        nc.tensor.matmul(bank[:, 0:S], w[:, 0, k], c.xT[:, k, cols], start=(k == 0),
                                         stop=(k == KD - 1))
                    for k, rows in enumerate(KC):
                        ins = nc.tensor.matmul(bank[:, S:2 * S], w[0:rows, 1, k], c.ctxT[0:rows, k, cols],
                                               start=(k == 0), stop=(k == 1))
                    ins.then_inc(projected.sem, 1)
                for s in range(2):
                    pe.wait_ge(*squared(2 * i + s + 1))
                    pe.wait_ge(*rooted(2 * i))
                    nc.tensor.matmul(c.ps[0:1, 2 + s, :], c.ones[:, 0:1], sq[:, s], start=True, stop=True
                                     ).then_inc(summed.sem, 1)
                for s in range(2):
                    pe.wait_ge(*added(2 * i))
                    for qt in range(2):
                        nc.tensor.matmul(c.ps[:, 6 + s, qt * S:(qt + 1) * S], vt[:, s, 0, qt * P:(qt + 1) * P],
                                         vt[:, s, 1], start=True, stop=True)
                    pe.wait_ge(*rooted(2 * i + s + 1))
                    for qt in range(2):
                        ins = nc.tensor.matmul(c.ps[:, 4 + s, qt * S:(qt + 1) * S], nrm[:, s, qt * P:(qt + 1) * P],
                                               nrm[:, s, S:2 * S], start=True, stop=True)
                    ins.then_inc(dotted.sem, 1)

        @block.scalar
        def _(act):
            act.wait_ge(*loaded(32))
            with act.Fori(0, H) as i:
                for s in range(2):
                    act.wait_ge(*projected(2 * i + s + 1))
                    for side in range(2):
                        part = c.ps[:, s, side * S:(side + 1) * S]
                        nc.scalar.activation(vt[:, s, side], part, ACT.Identity, bias=b[:, side:side + 1])
                        ins = nc.scalar.activation(sq[:, s, side * S:(side + 1) * S], part, ACT.Square,
                                                   bias=b[:, side:side + 1])
                    ins.then_inc(squared.sem, 1)
                for s in range(2):
                    act.wait_ge(*summed(2 * i + s + 1))
                    nc.scalar.activation(nrm[:, s], c.ps[0:1, 2 + s, :], ACT.Sqrt).then_inc(rooted.sem, 1)

        @block.vector
        def _(dve):
            with dve.Fori(0, H) as i:
                for s in range(2):
                    step = Steps(step_s, 2 * i + s, 3)
                    dve.wait_ge(*dotted(2 * i + s + 1))
                    dve.wait_ge(*added(2 * i))
                    step.link(dve, nc.vector.tensor_scalar(r[:, s], c.ps[:, 4 + s, :], 1e-8, None, ALU.max))
                    step.link(dve, nc.vector.reciprocal(r[:, s], r[:, s]))
                    step.link(dve, nc.vector.tensor_tensor(r[:, s], r[:, s], c.ps[:, 6 + s, :], ALU.mult))
                    xt = c.x[:, ds(2 * (2 * i + s), 2)].rearrange("p t d -> p (t d)")
                    nc.vector.tensor_tensor(xt, xt, r[:, s], ALU.add).then_inc(added.sem, 1)
    loaded.spent(32)
    step_s.spent(3 * B)
    for sgn in (projected, squared, summed, rooted, dotted, added):
        sgn.spent(B)



def local_projections(c, d, z, qT, kT, v, t1, t2):
    nc, ctx, dram = c.nc, ExitStack(), c.dram
    names = ("weights_in", "dve_step", "z_staged", "h_turned", "h_put", "qkv_done", "squared", "v_put", "sq_summed",
             "rooted", "lengthed", "q_rotated", "k_rotated", "qk_turned", "qk_put", "pool_step", "dve_pair")
    (loaded, step_s, z_staged, h_turned, h_put, qkv_done, squared, v_put, summed, rooted, lengthed, q_rot, k_rot,
     qk_turned, qk_put, pool_s, pair_s) = (c.sig(n) for n in names)
    HC = INNER // P
    HALF = LD // 2
    with ctx:
        def sb(name, shape):
            return c.sb("lp_" + name, shape, F32, ctx)

        wqkv = sb("wqkv", [P, KD, 3 * INNER])
        rope, gain = sb("rope", [P, 2, 2, 2, LD]), sb("gain", [P, 2, LD])
        tab = sb("tab", [P, 2, 2, 2, LD])
        zst, hs = sb("zst", [P, 2, D]), sb("hs", [P, KD, S])
        sq, ss = sb("sq", [P, 2 * INNER]), sb("ss", [P, 2, 2 * LH])
        root, rn = sb("root", [P, 2, 2 * LH]), sb("rn", [P, 2, 2 * LH])
        block = ctx.enter_context(nc.Block(no_gpsimd_drain=True))
        SETUP = 6

        @block.sync
        def _(sp):
            sp.dma_start(wqkv[:], dram["L1f_wqkv"][d]).then_inc(loaded.sem, 16)
            sp.dma_start(gain[:], dram["L1f_gain"][d].partition_broadcast(P)).then_inc(loaded.sem, 16)
            sp.dma_start(rope[:], dram["rope"]).then_inc(loaded.sem, 16)

        def rotate(engine, eng, step, tt, side):
            a = t1[:, tt, side].rearrange("p (h d) -> p h d", h=LH)
            b = t2[:, tt, side].rearrange("p (h d) -> p h d", h=LH)
            for lo, hi in ((0, HALF), (HALF, LD)):
                src = a[:, :, HALF - lo:HALF - lo + HALF]
                step.mark(engine.tensor_tensor(
                    b[:, :, lo:hi], src, tab[:, side, 1, tt, lo:hi].unsqueeze(1).to_broadcast([P, LH, HALF]), ALU.mult))
            step.settle(eng)
            step.link(eng, engine.tensor_tensor(
                a, a, tab[:, side, 0, tt].unsqueeze(1).to_broadcast([P, LH, LD]), ALU.mult))
            return engine.tensor_tensor(a, a, b, ALU.add)

        @block.gpsimd
        def _(pool):
            nc.gpsimd.memset(hs[:, 1, 0:1], 0.0).then_inc(pool_s.sem, 1)

            def stage(i):
                pool.wait_ge(*h_turned(i))
                nc.gpsimd.tensor_copy(zst[:], z[:, ds(2 * i, 2)]).then_inc(z_staged.sem, 1)

            def rotate_k(i, tt):
                step = Steps(pool_s, i, 6)
                step.n = 1 + 3 * tt
                pool.wait_ge(*lengthed(2 * i + tt + 1))
                rotate(nc.gpsimd, pool, step, tt, 1).then_inc(k_rot.sem, 1)

            stage(0)
            with pool.Fori(0, B - 1) as i:
                stage(i + 1)
                rotate_k(i, 0)
                rotate_k(i, 1)
            rotate_k(B - 1, 0)
            rotate_k(B - 1, 1)
            pool.wait_ge(*k_rot(2 * B))

        @block.tensor
        def _(pe):
            def turn_rows(i, bank_read):
                pe.wait_ge(*z_staged(i + 1))
                pe.wait_ge(*bank_read)
                for k in range(KD):
                    for tt in range(2):
                        ins = nc.tensor.transpose(c.ps[:, 6, k * S + tt * P:k * S + (tt + 1) * P],
                                                  zst[:, tt, k * P:(k + 1) * P], c.ident[:])
                ins.then_inc(h_turned.sem, 1)

            def project(i, tt):
                pe.wait_ge(*h_put(i + 1))
                pe.wait_ge(*lengthed(2 * i + max(tt - 1, 0)) if tt else lengthed(2 * i - 1))
                pe.wait_ge(*v_put(2 * i) if tt else v_put(2 * i - 1))
                for n in range(3):
                    for k in range(KD):
                        ins = nc.tensor.matmul(c.ps[:, 3 * tt + n, :], hs[:, k, tt * P:(tt + 1) * P],
                                               wqkv[:, k, n * INNER:(n + 1) * INNER],
                                               start=(k == 0), stop=(k == KD - 1))
                ins.then_inc(qkv_done.sem, 1)

            def turn_qk(i, tt, rows_put):
                pe.wait_ge(*q_rot(2 * i + tt + 1))
                pe.wait_ge(*k_rot(2 * i + tt + 1))
                for side in range(2):
                    n = 4 * i + 2 * tt + side
                    pe.wait_ge(*qk_put(n - 1))
                    if side:
                        pe.wait_ge(*h_put(rows_put))
                    for hc in range(HC):
                        ins = nc.tensor.transpose(c.ps[:, 7 - side, hc * P:(hc + 1) * P],
                                                  t1[:, tt, side, hc * P:(hc + 1) * P], c.ident[:])
                    ins.then_inc(qk_turned.sem, 1)

            pe.wait_ge(*loaded(48))
            turn_rows(0, h_put(0))
            project(0, 0)
            project(0, 1)
            turn_rows(1, h_put(1))
            with pe.Fori(1, B - 1) as i:
                project(i, 0)
                turn_qk(i - 1, 0, i + 1)
                project(i, 1)
                turn_rows(i + 1, qk_put(4 * i - 2))
                turn_qk(i - 1, 1, i + 2)
            project(B - 1, 0)
            turn_qk(B - 2, 0, B)
            project(B - 1, 1)
            turn_qk(B - 2, 1, B)
            turn_qk(B - 1, 0, B)
            turn_qk(B - 1, 1, B)

        @block.scalar
        def _(act):
            def put_rows(i):
                act.wait_ge(*h_turned(i + 1))
                act.wait_ge(*qkv_done(2 * i))
                nc.scalar.copy(hs[:, 0, :], c.ps[:, 6, 0:S])
                nc.scalar.copy(hs[:, 1, 1:S], c.ps[:, 6, S:2 * S - 1]).then_inc(h_put.sem, 1)

            def take(i, tt, between=None):
                act.wait_ge(*qkv_done(2 * i + tt + 1))
                act.wait_ge(*summed(2 * i + tt))
                nc.scalar.activation(sq[:], c.ps[:, 3 * tt:3 * tt + 2, :].rearrange("p a b -> p (a b)"),
                                     ACT.Square).then_inc(squared.sem, 1)
                if between is not None:
                    put_rows(between)
                nc.scalar.copy(v[:, ds(2 * i + tt, 1)].squeeze(1), c.ps[:, 3 * tt + 2, :]).then_inc(v_put.sem, 1)
                act.wait_ge(*summed(2 * i + tt + 1))
                nc.scalar.activation(root[:, tt], ss[:, tt], ACT.Sqrt).then_inc(rooted.sem, 1)

            def put_qk(i, tt):
                for side, dst in ((0, qT), (1, kT)):
                    act.wait_ge(*qk_turned(4 * i + 2 * tt + side + 1))
                    nc.scalar.copy(dst[:, :, ds((2 * i + tt) * P, P)],
                                   c.ps[:, 7 - side, :].rearrange("p (h t) -> p h t", h=HC)).then_inc(qk_put.sem, 1)

            put_rows(0)
            take(0, 0)
            take(0, 1, between=1)
            with act.Fori(1, B - 1) as i:
                take(i, 0)
                put_qk(i - 1, 0)
                take(i, 1, between=i + 1)
                put_qk(i - 1, 1)
            take(B - 1, 0)
            put_qk(B - 2, 0)
            take(B - 1, 1)
            put_qk(B - 2, 1)
            put_qk(B - 1, 0)
            put_qk(B - 1, 1)

        @block.vector
        def _(dve):
            dve.wait_ge(*loaded(48))
            step = Steps(pair_s)
            for side in range(2):
                g = gain[:, side]
                step.mark(nc.vector.tensor_tensor(tab[:, side, 0], rope[:, side, 0],
                                                  g.unsqueeze(1).to_broadcast([P, 2, LD]), ALU.mult))
                for lo, hi in ((0, HALF), (HALF, LD)):
                    step.mark(nc.vector.tensor_tensor(
                        tab[:, side, 1, :, lo:hi], rope[:, side, 1, :, lo:hi],
                        g[:, HALF - lo:HALF - lo + HALF].unsqueeze(1).to_broadcast([P, 2, HALF]), ALU.mult))
            step.settle(dve)
            assert step.n == SETUP
            with dve.Fori(0, B) as i:
                step = Steps(step_s, i, 4)
                for tt in range(2):
                    dve.wait_ge(*squared(2 * i + tt + 1))
                    nc.vector.tensor_reduce(ss[:, tt], sq[:].rearrange("p (h d) -> p h d", d=LD), AX_X, ALU.add
                                            ).then_inc(summed.sem, 1)
                    dve.wait_ge(*rooted(2 * i + tt + 1))
                    step.link(dve, nc.vector.tensor_scalar(rn[:, tt], root[:, tt], 1e-12, None, ALU.max))
                    step.link(dve, nc.vector.reciprocal(rn[:, tt], rn[:, tt]))
                    dve.wait_ge(*qk_turned(4 * i - 2 + 2 * tt))
                    nc.vector.tensor_tensor(
                        t1[:, tt].rearrange("p a (h d) -> p (a h) d", d=LD),
                        c.ps[:, 3 * tt:3 * tt + 2, :].rearrange("p a (h d) -> p (a h) d", d=LD),
                        rn[:, tt].unsqueeze(2).to_broadcast([P, 2 * LH, LD]), ALU.mult).then_inc(lengthed.sem, 1)
                    dve.wait_ge(*lengthed(2 * i + tt + 1))
                    rot = Steps(pair_s, i, 6)
                    rot.n = SETUP + 3 * tt
                    rotate(nc.vector, dve, rot, tt, 0).then_inc(q_rot.sem, 1)
    loaded.spent(48)
    pool_s.spent(1 + 6 * B)
    pair_s.spent(SETUP + 6 * B)
    step_s.spent(4 * B)
    for sgn, n in ((z_staged, 1), (h_turned, 1), (h_put, 1), (qkv_done, 2), (squared, 2), (v_put, 2), (summed, 2),
                   (rooted, 2), (lengthed, 2), (q_rot, 2), (k_rot, 2), (qk_turned, 4), (qk_put, 4)):
        sgn.spent(B * n)


def local_weighing(c, d, z, qT, kT, v):
    nc, ctx, dram = c.nc, ExitStack(), c.dram
    names = ("weights_in", "dve_pair", "q_staged", "v_staged", "scored", "max_put", "max_negated", "exped", "inverted",
             "p_normed", "p_turned", "p_put", "weighed", "o_put", "y_done", "y_added")
    (loaded, pair_s, q_staged, v_staged, scored, topped, negated, exped, inverted, p_normed, p_turned, p_put,
     weighed, o_put, y_done, added) = (c.sig(n) for n in names)
    HC = INNER // P
    AHEAD = 4
    with ctx:
        def sb(name, shape, dt=F32):
            return c.sb("lw_" + name, shape, dt, ctx)

        wo, mask = sb("wo", [P, HC, D]), sb("mask", [P, 3 * WIN])
        maskb, identb = sb("maskb", [P, 3 * WIN], BF16), sb("identb", [P, P], BF16)
        qst, kst = sb("q", [P, HC, S]), sb("k", [P, HC, S])
        pr, pT = sb("p", [P, AHEAD, 3 * WIN]), sb("pT", [P, 2, 3 * WIN])
        mx, nm, rs = sb("mx", [P, LH, 2]), sb("nm", [P, LH, 2]), sb("rs", [P, LH, 2])
        rec, ot, vst = sb("rec", [P, LH, 2]), sb("ot", [P, HC, S]), sb("v", [P, 2, INNER])
        block = ctx.enter_context(nc.Block(no_gpsimd_drain=True))
        SPLIT = [(0, WIN), (WIN, 3 * WIN)]

        def ahead(step, by, i, h, more):
            if h + by < LH:
                step(i, h + by)
            elif more:
                step(i + 1, h + by - LH)

        @block.sync
        def _(sp):
            sp.dma_start(wo[:], dram["L1f_wo"][d]).then_inc(loaded.sem, 16)
            sp.dma_start(mask[:], dram["window"]).then_inc(loaded.sem, 16)

        @block.gpsimd
        def _(pool):
            with pool.Fori(0, B) as i:
                for hc in range(HC):
                    pool.wait_ge(*scored(LH * (i - 1) + 2 * hc + 2))
                    nc.gpsimd.tensor_copy(qst[:, hc], qT[:, hc, ds(i * S, S)])
                    nc.gpsimd.tensor_copy(kst[:, hc], kT[:, hc, ds(i * S, S)]).then_inc(q_staged.sem, 1)
                pool.wait_ge(*weighed(LH // 2 * i))
                nc.gpsimd.tensor_copy(vst[:], v[:, ds(2 * i, 2)]).then_inc(v_staged.sem, 1)
            pool.wait_ge(*q_staged(HC * B))
            pool.wait_ge(*v_staged(B))

        @block.tensor
        def _(pe):
            pe.wait_ge(*loaded(32))
            pe.wait_ge(*pair_s(2))

            def score(i, h):
                r, hc = LD * (h % 2), h // 2
                pe.wait_ge(*q_staged(HC * i + hc + 1))
                pe.wait_ge(*exped(LH * i + h + 1 - AHEAD))
                bank = c.ps[:, 1 + h % AHEAD, :]
                nc.tensor.matmul(bank[:, 0:3 * WIN], identb[:], maskb[:], start=True, stop=False)
                nc.tensor.matmul(bank[:, 0:WIN], qst[r:r + LD, hc, 0:WIN], kst[r:r + LD, hc, 0:WIN],
                                 start=False, stop=False)
                nc.tensor.matmul(bank[:, WIN:3 * WIN], qst[r:r + LD, hc, WIN:S], kst[r:r + LD, hc, :],
                                 start=False, stop=True).then_inc(scored.sem, 1)

            def turn(i, h):
                pe.wait_ge(*p_normed(LH * i + h + 1))
                pe.wait_ge(*p_put(LH * i + h - 1))
                for n in range(3):
                    ins = nc.tensor.transpose(c.ps[:, 7 * (1 - h % 2), n * P:(n + 1) * P],
                                              pr[:, h % AHEAD, n * P:(n + 1) * P], c.ident[:])
                ins.then_inc(p_turned.sem, 1)

            def weigh(i, hc):
                pe.wait_ge(*p_put(LH * i + 2 * hc + 2))
                if hc == 0:
                    pe.wait_ge(*v_staged(i + 1))
                    pe.wait_ge(*o_put(2 * i))
                    pe.wait_ge(*added(2 * i))
                for kt, lo in ((0, 0), (1, WIN)):
                    for j in range(2):
                        h = 2 * hc + j
                        out = c.ps[j * LD:(j + 1) * LD, 5 + hc // 2, hc % 2 * S + lo:(hc % 2 + 1) * S]
                        ins = nc.tensor.matmul(out, vst[:, kt, h * LD:(h + 1) * LD],
                                               pT[:, j, 2 * kt * WIN:(2 + kt) * WIN], start=(kt == 0), stop=(kt == 1),
                                               tile_position=(0, j * LD))
                ins.then_inc(weighed.sem, 1)

            def output(i):
                pe.wait_ge(*o_put(2 * i + 2))
                for qt in range(2):
                    for hc in range(HC):
                        ins = nc.tensor.matmul(c.ps[:, 5, qt * D:(qt + 1) * D], ot[:, hc, qt * P:(qt + 1) * P],
                                               wo[:, hc], start=(hc == 0), stop=(hc == HC - 1))
                ins.then_inc(y_done.sem, 1)

            def head(i, h, more=True, pair=None):
                ahead(score, AHEAD, i, h, more)
                if pair:
                    weigh(*pair)
                turn(i, h)

            def sequence(i, more):
                for h in range(2, LH):
                    head(i, h, more, None if h % 2 else (i, h // 2 - 1))
                if more:
                    head(i + 1, 0, True, (i, LH // 2 - 1))
                    head(i + 1, 1)
                else:
                    weigh(i, LH // 2 - 1)
                output(i)

            for h in range(AHEAD):
                score(0, h)
            head(0, 0)
            head(0, 1)
            with pe.Fori(0, B - 1) as i:
                sequence(i, True)
            sequence(B - 1, False)

        @block.scalar
        def _(act):
            def weights(i, h):
                act.wait_ge(*negated(LH * i + h + 1))
                act.wait_ge(*p_turned(LH * i + h + 1 - AHEAD))
                for n, (lo, hi) in enumerate(SPLIT):
                    ins = nc.scalar.activation(pr[:, h % AHEAD, lo:hi], c.ps[:, 1 + h % AHEAD, lo:hi], ACT.Exp,
                                               bias=nm[:, h, n:n + 1], accum_out=rs[:, h, n:n + 1])
                ins.then_inc(exped.sem, 1)

            def put(i, h):
                act.wait_ge(*p_turned(LH * i + h + 1))
                act.wait_ge(*weighed(LH // 2 * i + h // 2))
                nc.scalar.copy(pT[:, h % 2], c.ps[:, 7 * (1 - h % 2), 0:3 * WIN]).then_inc(p_put.sem, 1)

            def put_o(i, n):
                act.wait_ge(*weighed(LH // 2 * i + 2 * n + 2))
                act.wait_ge(*y_done(i))
                nc.scalar.copy(ot[:, 2 * n:2 * n + 2].rearrange("p c s -> p (c s)"), c.ps[:, 5 + n, :]
                               ).then_inc(o_put.sem, 1)

            def head(i, h, more=True):
                put(i, h)
                ahead(weights, AHEAD - 2, i, h, more)

            def sequence(i, more):
                for h in range(2, LH):
                    head(i, h, more)
                    if h == LH // 2 + 1:
                        put_o(i, 0)
                put_o(i, 1)
                if more:
                    head(i + 1, 0)
                    head(i + 1, 1)

            for h in range(AHEAD - 2):
                weights(0, h)
            head(0, 0)
            head(0, 1)
            with act.Fori(0, B - 1) as i:
                sequence(i, True)
            sequence(B - 1, False)

        @block.vector
        def _(dve):
            dve.wait_ge(*loaded(32))
            step = Steps(pair_s)
            step.mark(nc.vector.tensor_copy(maskb[:], mask[:]))
            step.mark(nc.vector.tensor_copy(identb[:], c.ident[:]))
            step.settle(dve)

            def maximum(i, h):
                dve.wait_ge(*scored(LH * i + h + 1))
                for n, (lo, hi) in enumerate(SPLIT):
                    ins = nc.vector.tensor_reduce(mx[:, h, n:n + 1], c.ps[:, 1 + h % AHEAD, lo:hi], AX_X, ALU.max)
                ins.then_inc(topped.sem, 1)
                dve.wait_ge(*topped(LH * i + h + 1))
                nc.vector.tensor_scalar(nm[:, h], mx[:, h], -1.0, None, ALU.mult).then_inc(negated.sem, 1)

            def norm(i, h):
                n = LH * i + h + 1
                dve.wait_ge(*exped(n))
                nc.vector.reciprocal(rec[:, h], rs[:, h]).then_inc(inverted.sem, 1)
                dve.wait_ge(*inverted(n))
                for m, (lo, hi) in enumerate(SPLIT):
                    p = pr[:, h % AHEAD, lo:hi]
                    ins = nc.vector.tensor_scalar(p, p, rec[:, h, m:m + 1], None, ALU.mult)
                ins.then_inc(p_normed.sem, 1)

            def head(i, h, more=True):
                norm(i, h)
                ahead(maximum, AHEAD - 1, i, h, more)

            def sequence(i, more):
                for h in range(2, LH):
                    head(i, h, more)
                if more:
                    head(i + 1, 0)
                    head(i + 1, 1)
                dve.wait_ge(*y_done(i + 1))
                for qt in range(2):
                    zt = z[:, ds(2 * i + qt, 1)].squeeze(1)
                    nc.vector.tensor_tensor(zt, zt, c.ps[:, 5, qt * D:(qt + 1) * D], ALU.add).then_inc(added.sem, 1)

            for h in range(AHEAD - 1):
                maximum(0, h)
            head(0, 0)
            head(0, 1)
            with dve.Fori(0, B - 1) as i:
                sequence(i, True)
            sequence(B - 1, False)
    loaded.spent(32)
    pair_s.spent(2)
    for sgn, n in ((q_staged, HC), (v_staged, 1), (scored, LH), (topped, LH), (negated, LH), (exped, LH),
                   (inverted, LH), (p_normed, LH), (p_turned, LH), (p_put, LH), (weighed, LH // 2), (o_put, 2),
                   (y_done, 1), (added, 2)):
        sgn.spent(B * n)


def local_attention(c, d, z):
    with ExitStack() as ctx:
        qT, kT = (c.sb("la_" + n, [P, INNER // P, T], ctx=ctx) for n in ("qT", "kT"))
        v = c.sb("la_v", [P, NT, INNER], ctx=ctx)
        t1, t2 = (c.xT[:, k].rearrange("p (t a n) -> p t a n", t=2, a=2) for k in range(KD))
        local_projections(c, d, z, qT, kT, v, t1, t2)
        local_weighing(c, d, z, qT, kT, v)


def local_ff(c, d, z, last):
    nc, ctx, dram = c.nc, ExitStack(), c.dram
    loaded, moved, zeroed = c.sig("weights_in"), c.sig("shifted_in"), c.sig("pool_step")
    h_done, gated, h_put = c.sig("h_done"), c.sig("gated"), c.sig("h_put")
    y_done, added, ended = c.sig("y_done"), c.sig("y_added"), c.sig("dve_step")
    with ctx:
        def sb(name, shape):
            return c.sb("lf_" + name, shape, F32, ctx)

        w1, w2 = sb("w1", [P, KD, 2 * HPAD]), sb("w2", [P, HC_FF, D])
        b1, b2, affine = sb("b1", [P, 2, HC_FF]), sb("b2", [1, D]), sb("affine", [P, 2, KD])
        early = ctx.enter_context(ExitStack())
        late = c.sb("lf_late", [P, NT, D // 2], ctx=early)
        with nc.Block(no_gpsimd_drain=True) as block:
            @block.gpsimd
            def _(pool):
                nc.gpsimd.memset(late[0:1, :, :], 0.0).then_inc(zeroed.sem, 1)
                pool.wait_ge(*zeroed(1))

            @block.sync
            def _(sp):
                sp.dma_start(late[1:P], z[0:P - 1, :, D // 2:D]).then_inc(moved.sem, 16)
                sp.wait_ge(*zeroed(1))
                sp.dma_start(late[0:1].rearrange("p (b t) d -> p b t d", t=2)[:, :, 1],
                             z[P - 1:P].rearrange("p (b t) d -> p b t d", t=2)[:, :, 0, D // 2:D]
                             ).then_inc(moved.sem, 16)
                sp.dma_start(affine[:], dram["L1f_affine"][d]).then_inc(loaded.sem, 16)
                sp.wait_ge(*moved(32))
                sp.wait_ge(*loaded(16))
        zeroed.spent(1)
        moved.spent(32)
        loaded.spent(16)

        def fetch(sp):
            for dst, name in ((w1, "w1"), (w2, "w2"), (b1, "b1"), (b2, "b2")):
                sp.dma_start(dst[:], dram["L1f_" + name][d]).then_inc(loaded.sem, 16)
            sp.wait_ge(*loaded(64))

        norm_phase(c, [(z[:, :, 0:D // 2], 0), (late, D // 2)], affine=affine, fetch=fetch)
        loaded.spent(64)
        early.close()
        NH = HC_FF
        gs, h = sb("gs", [P, 2, GROUP]), sb("h", [P, 2, GROUP])
        (xh, xl), (w1h, w1l), (w2h, w2l), (hh, hl) = (
            [c.sb(f"lf_{n}_{part}", shape, F32R, ctx) for part in ("lead", "less")] for n, shape in (
                ("x", [P, KD, T]), ("w1", [P, KD, 2 * HPAD]), ("w2", [P, NH, D]), ("h", [P, NH + 1, GROUP])))
        x_lead, x_rest, w_lead, w_rest, h_lead, h_rest = (c.sig(n) for n in (
            "x_lead_put", "x_rest_put", "w_lead_put", "w_rest_put", "h_lead_put", "h_rest_put"))
        block = ctx.enter_context(nc.Block(no_gpsimd_drain=True))

        def chunk_of(w, f):
            return w.rearrange("p k (a n) -> p k a n", a=2)[:, :, :, f * P:(f + 1) * P]

        def slot(s, f):
            return f if f or not s else NH

        def groups(eng, group):
            with eng.Fori(0, NG // 2 - 1) as i:
                for s in range(2):
                    group(2 * i + s, s, True)
            for g in range(NG - 2, NG):
                group(g, g % 2, g + 1 < NG)

        @block.tensor
        def _(pe):
            def rise(g, s, f):
                pe.wait_ge(*h_put(NH * g + f - 1))
                pe.wait_ge(*w_rest(f + 1))
                if f == 0:
                    pe.wait_ge(*x_rest(g + 1))
                for side in range(2):
                    for a, (wp, xp) in enumerate(((w1h, xh), (w1h, xl), (w1l, xh))):
                        for k in range(KD):
                            at = side * HPAD + f * P
                            ins = nc.tensor.matmul(c.ps[:, 2 * (f % 2) + side, :], wp[:, k, at:at + P],
                                                   xp[:, k, ds(g * GROUP, GROUP)], start=(a == 0 and k == 0),
                                                   stop=(a == 2 and k == KD - 1))
                ins.then_inc(h_done.sem, 1)

            def group(g, s, more):
                for f in range(1, NH):
                    rise(g, s, f)
                if more:
                    rise(g + 1, 1 - s, 0)
                pe.wait_ge(*w_rest(NH + 1))
                pe.wait_ge(*h_rest(NH * g + NH))
                pe.wait_ge(*added(TPG * g))
                for tt in range(TPG):
                    rows = slice(tt * P, (tt + 1) * P)
                    nc.tensor.matmul(c.ps[:, 4 + tt, 0:D], c.ones[0:1, :], b2[:], start=True, stop=False)
                    for f in range(NH):
                        for a, (hp, wp) in enumerate(((hh, w2h), (hl, w2h), (hh, w2l))):
                            ins = nc.tensor.matmul(c.ps[:, 4 + tt, 0:D], hp[:, slot(s, f), rows], wp[:, f], start=False,
                                                   stop=(f == NH - 1 and a == 2))
                    ins.then_inc(y_done.sem, 1)

            rise(0, 0, 0)
            groups(pe, group)

        @block.scalar
        def _(act):
            def lead_x(g):
                cols = slice(g * GROUP, (g + 1) * GROUP)
                nc.scalar.copy(xh[:, :, cols], c.xT[:, :, cols]).then_inc(x_lead.sem, 1)

            def group(g, s, more):
                for f in range(NH):
                    n = NH * g + f
                    act.wait_ge(*h_done(n + 1))
                    act.wait_ge(*h_put(n - 1))
                    nc.scalar.activation(gs[:, f % 2], c.ps[:, 2 * (f % 2) + 1, :], ACT.Gelu,
                                         bias=b1[:, 1, f:f + 1]).then_inc(gated.sem, 1)
                    act.wait_ge(*h_put(n + 1))
                    act.wait_ge(*y_done(TPG * (g if f else g - 1)))
                    nc.scalar.copy(hh[:, slot(s, f)], h[:, f % 2]).then_inc(h_lead.sem, 1)

            lead_x(0)
            for f in range(NH):
                nc.scalar.copy(chunk_of(w1h[:], f), chunk_of(w1[:], f)).then_inc(w_lead.sem, 1)
            nc.scalar.copy(w2h[:], w2[:]).then_inc(w_lead.sem, 1)
            for g in range(1, NG):
                lead_x(g)
            groups(act, group)

        @block.gpsimd
        def _(pool):
            def group(g, s, more):
                for f in range(NH):
                    pool.wait_ge(*h_lead(NH * g + f + 1))
                    nc.gpsimd.tensor_tensor(hl[:, slot(s, f)], h[:, f % 2], hh[:, slot(s, f)].bitcast(F32), ALU.subtract
                                            ).then_inc(h_rest.sem, 1)

            for g in range(NG):
                cols = slice(g * GROUP, (g + 1) * GROUP)
                pool.wait_ge(*x_lead(g + 1))
                nc.gpsimd.tensor_tensor(xl[:, :, cols], c.xT[:, :, cols], xh[:, :, cols].bitcast(F32), ALU.subtract
                                        ).then_inc(x_rest.sem, 1)
            groups(pool, group)
            pool.wait_ge(*h_rest(NH * NG))

        @block.vector
        def _(dve):
            def multiply(g, s, f):
                dve.wait_ge(*gated(NH * g + f + 1))
                dve.wait_ge(*h_rest(NH * g + f - 1))
                nc.vector.scalar_tensor_tensor(h[:, f % 2], c.ps[:, 2 * (f % 2), :], b1[:, 0, f:f + 1], gs[:, f % 2],
                                               ALU.add, ALU.mult).then_inc(h_put.sem, 1)

            def group(g, s, more):
                for f in range(1, NH):
                    multiply(g, s, f)
                if more:
                    multiply(g + 1, 1 - s, 0)
                for tt in range(TPG):
                    dve.wait_ge(*y_done(TPG * g + tt + 1))
                    zt = z[:, ds(g * TPG + tt, 1)].squeeze(1)
                    nc.vector.tensor_tensor(zt, zt, c.ps[:, 4 + tt, 0:D], ALU.add).then_inc(added.sem, 1)

            for f in range(NH):
                dve.wait_ge(*w_lead(f + 1))
                nc.vector.tensor_tensor(chunk_of(w1l[:], f), chunk_of(w1[:], f), chunk_of(w1h[:], f).bitcast(F32),
                                        ALU.subtract).then_inc(w_rest.sem, 1)
            dve.wait_ge(*w_lead(NH + 1))
            nc.vector.tensor_tensor(w2l[:], w2[:], w2h[:].bitcast(F32), ALU.subtract).then_inc(w_rest.sem, 1)
            multiply(0, 0, 0)
            groups(dve, group)
            if last:
                dve.wait_ge(*added(NT))
                nc.vector.tensor_tensor(c.x[:], c.x[:], z[:], ALU.add).then_inc(ended.sem, 1)
    for sgn in (x_lead, x_rest):
        sgn.spent(NG)
    for sgn in (w_lead, w_rest):
        sgn.spent(NH + 1)
    for sgn in (h_done, gated, h_put, h_lead, h_rest):
        sgn.spent(NH * NG)
    y_done.spent(NT)
    added.spent(NT)
    if last:
        ended.spent(1)


def local_transformer(c):
    norm_phase(c, [(c.x, 0)], keep=True, transposed=False)
    for d in range(DEPTH):
        local_attention(c, d, c.xn)
        local_ff(c, d, c.xn, last=(d == DEPTH - 1))


def _more_layouts(a, o):
    f4 = np.float32
    for n, name in ((E, "tri8"), (4, "tri4"), (16, "tri16")):
        o[name] = np.tril(np.ones((n, n), f4), -1)[None]
    o["upto"] = np.triu(np.ones((P, P), f4))
    o["L0f_wr"] = _chunked(a["L0_ffn_Wr"])
    o["L2f_wr"] = _chunked(a["L2_ffn_Wg"])
    for tag, w1, w2 in (("L0f_", a["L0_ffn_W1"], a["L0_ffn_W2"]),
                        ("L2f_", a["L2_ffn_W1"], a["L2_ffn_W2"])):
        o[tag + "w1"] = w1.reshape(-1, KD, P, FF).swapaxes(1, 2)
        o[tag + "w2"] = w2.reshape(-1, FC, P, D).swapaxes(1, 2)
    o["L2f_b1"] = a["L2_ffn_b1"].reshape(-1, FC, P).swapaxes(1, 2)
    o["L2f_b2"] = a["L2_ffn_b2"][:, None]
    o["L2f_w1s"], o["L2f_w2s"] = _chunked(a["L2_ffn_Ws1"]), _chunked(a["L2_ffn_Ws2"])
    o["L2f_b1s"], o["L2f_b2s"] = a["L2_ffn_bs1"].reshape(FC, P).T, a["L2_ffn_bs2"][None]
    o["tile_edges"] = (P * np.arange(1, NT, dtype=f4))[None]
    o["own_row"] = (SLOT_ROWS + np.arange(T, dtype=f4)).reshape(NT, P).T
    o["L3f_wr"] = _chunked(a["L3_ffn_router_weight"].T)
    o["L3f_bias"] = a["L3_ffn_router_bias"].reshape(1, 1, E3)
    gu = [a["L3_ffn_w_" + n].swapaxes(1, 2).reshape(E3, KD, P, I3).swapaxes(1, 2).reshape(E3, P, KD * I3)
          for n in ("gate", "up")]
    o["L3f_w"] = np.concatenate(gu + [a["L3_ffn_w_down"].swapaxes(1, 2)], 2)
    o["L1x_w"] = np.stack([_chunked(a["L1_xattn_Wv"].T), _chunked(a["L1_xattn_Wt"].T)], 1)
    o["L1x_b"] = np.stack([a["L1_xattn_bv"], a["L1_xattn_bt"]], 1)
    w1 = np.zeros((DEPTH, D, 2, HPAD), f4)
    w1[..., 0:HID] = a["L1_ffn_w1"].reshape(DEPTH, D, 2, HID)
    for name, w in (("wqkv", a["L1_ffn_wqkv"]), ("wo", a["L1_ffn_wo"]), ("w1", w1.reshape(DEPTH, D, 2 * HPAD)),
                    ("w2", a["L1_ffn_w2"])):
        o["L1f_" + name] = np.stack([_chunked(m) for m in w])
    o["L1f_gain"] = np.stack([a["L1_ffn_q_scale"], a["L1_ffn_k_scale"]], 1)[:, None]
    b1 = a["L1_ffn_b1"].reshape(DEPTH, 2, HID)
    o["L1f_b1"] = np.stack([np.stack([_chunked(b[s]) for s in range(2)], 1) for b in b1])
    o["L1f_b2"] = a["L1_ffn_b2"][:, None]
    o["L1f_affine"] = np.stack([a["L1_ffn_ln_g"], a["L1_ffn_ln_b"]], 1).reshape(DEPTH, 2, KD, P).transpose(0, 3, 1, 2)
    o["rope"] = _rope()
    q, k = np.arange(P)[:, None], np.arange(P)[None]
    off = lambda seen: np.where(seen, 0.0, -HUGE).astype(f4)
    o["window"] = np.concatenate([off(k <= q), off(k >= q), off(k <= q)], 1)


def _rope():
    f4 = np.float32
    half = np.arange(0, LD, 2, dtype=f4)
    t = np.arange(S, dtype=f4)
    freqs = t[:, None] * (f4(1.0) / f4(10000.0) ** (half / f4(LD)))[None]
    base = (half + f4(0.4 * LD)) / f4(1.4 * LD)
    scale = base[None] ** ((t - S // 2) / f4(WIN // 2))[:, None]
    cos, sin = np.cos(freqs), np.sin(freqs)
    out = np.empty((2, 2, S, LD), f4)
    for side, s in ((0, scale * f4(QK_SCALE)), (1, f4(1.0) / scale)):
        out[side, 0] = np.concatenate([cos * s, cos * s], 1)
        out[side, 1] = np.concatenate([-sin * s, sin * s], 1)
    return out.reshape(2, 2, 2, P, LD).transpose(3, 0, 1, 2, 4)


STAGES = (0, 8)


def _program(nc, dram, stages):
    with ExitStack() as ctx:
        c = Core(nc, ctx, dram)
        load_phase(c)
        layers = [
            lambda: xattn_phase(c, "L0x_", masked=True),
            lambda: expert_phases(c, "L0f_"),
            lambda: (norm_phase(c, [(c.x, 0)]), similarity_phase(c)),
            lambda: local_transformer(c),
            lambda: xattn_phase(c, "L2x_", biased=True, scale_in=True),
            lambda: expert_phases(c, "L2f_"),
            lambda: xattn_phase(c, "L3x_", biased=True),
            lambda: (norm_phase(c, [(c.x, 0)]), grouped_experts(c)),
        ]
        for n in range(*stages):
            layers[n]()
        store_phase(c)


def _chunked(a, rows=P):
    n = -(-a.shape[0] // rows)
    out = np.zeros((n * rows,) + a.shape[1:], a.dtype)
    out[:a.shape[0]] = a
    return out.reshape((n, rows) + a.shape[1:]).swapaxes(0, 1)


def _padded_heads(w):
    out = np.zeros(w.shape[:-1] + (HEADS, SLOT), w.dtype)
    out[..., 0:HD] = w.reshape(w.shape[:-1] + (HEADS, HD))
    return out.reshape(w.shape[:-1] + (HEADS * SLOT,))


def _layouts(inp):
    f4 = np.float32
    a = {k: np.asarray(v) for k, v in inp.items()}
    o = {}
    o["x"] = a["x"].reshape(NT, P, D).swapaxes(0, 1)
    o["ctxT"] = _chunked(a["ctx_768"].reshape(T, DC).T)
    o["mask"] = a["mask_BxS2_bf1"].reshape(1, T).view(np.uint8)
    o["ident"] = np.eye(P, dtype=f4)
    z = np.zeros(D, f4)
    for tag, src, bq, bk, bv, bo in (("L0x_", "L0_xattn_", z, z, z, z),
                                     ("L2x_", "L2_xattn_", a["L2_xattn_bq"], a["L2_xattn_bk"], a["L2_xattn_bv"],
                                      a["L2_xattn_bo"]),
                                     ("L3x_", "L3_xattn_", z, z, z, a["L3_xattn_bo"])):
        o[tag + "wq"] = _chunked(_padded_heads(a[src + "Wq"]))
        o[tag + "wk"] = _chunked(_padded_heads(a[src + "Wk"]))
        o[tag + "wv"] = _chunked(a[src + "Wv"])
        o[tag + "wo"] = _chunked(np.ascontiguousarray(_padded_heads(a[src + "Wo"].T).T))
        qb = _padded_heads(bq).reshape(HEADS, SLOT).copy()
        kb = _padded_heads(bk).reshape(HEADS, SLOT).copy()
        qb[:, MASK_ROW] = 1.0 if tag == "L0x_" else 0.0
        kb[:, MAX_ROW] = -1.0
        o[tag + "cols"] = np.stack([qb.reshape(CHUNKS, P).T, kb.reshape(CHUNKS, P).T], 1)
        if tag != "L0x_":
            o[tag + "rows"] = np.stack([bv, bo])[None]
    sel = np.zeros((1, HPC, SLOT), f4)
    sel[:, :, MASK_ROW] = 1.0
    o["rowsel"] = sel.reshape(1, P)
    pick, give = np.zeros((HPC, SLOT, CHUNKS, HEADS), f4), np.zeros((P, CHUNKS, HPC, SLOT), f4)
    for h in range(HEADS):
        pick[h % HPC, HD, h // HPC, h] = 1.0
        give[h, h // HPC, h % HPC] = 1.0
    o["pick"], o["give"] = pick.reshape(P, CHUNKS, HEADS), give.reshape(P, CHUNKS, P)
    o["L2x_scale"] = a["L2_xattn_scale"].reshape(1, 1)
    _more_layouts(a, o)
    return {k: np.ascontiguousarray(v) for k, v in o.items()}


def kernel(**inputs):
    import concourse.bacc as _bacc
    from concourse import mybir as _mybir
    from concourse.bass_utils import run_bass_kernel_spmd as _run

    nc = _bacc.Bacc("TRN2", target_bir_lowering=False, num_devices=1)
    arrays, dram = {}, {}
    for name, a in _layouts(inputs).items():
        arrays[f"in_{name}_dram"] = a
        dram[name] = nc.dram_tensor(f"in_{name}_dram", a.shape, _mybir.dt.from_np(a.dtype), kind="ExternalInput").ap()
    out = nc.dram_tensor("out_0_dram", (B, S, D), _mybir.dt.float32, kind="ExternalOutput").ap()
    dram["out"] = out.rearrange("b (t p) d -> p (b t) d", p=P)
    for name, rows in (("rows_in", SLOT_ROWS + T), ("rows_out", SLOT_ROWS)):
        dram[name] = nc.dram_tensor(name, (rows, D), _mybir.dt.float32, kind="Internal").ap()
    _program(nc, dram, STAGES)
    r = _run(nc, [arrays], core_ids=[0])
    return r.results[0]["out_0_dram"]
```
